# Optimizing a Trainium2 kernel written in Bass

```python
import numpy as np
import jax
import jax.numpy as jnp

def _softmax(x, axis=-1):
    return jax.nn.softmax(x, axis=axis)

def _gelu(x):
    return jax.nn.gelu(x, approximate=True)

def _silu(x):
    return jax.nn.silu(x)

def _sigmoid(x):
    return jax.nn.sigmoid(x)

def _layernorm(x, axis=-1, eps=1e-05):
    m = jnp.mean(x, axis=axis, keepdims=True)
    v = jnp.var(x, axis=axis, keepdims=True)
    return (x - m) / jnp.sqrt(v + eps)

def _scatter_add(tgt, idx, src, axis=0):
    return tgt.at[idx].add(src)

def _segment_sum(src, seg, n):
    return jax.ops.segment_sum(src, seg, n)
kernel_name = 'mk_decoder_preln_d1_seqx_r2_1f3135'

def setup_inputs(seed: int=0):
    np.random.seed(seed)
    _w = jnp.asarray

    def _rec_inputs():
        import jax
        import jax.numpy as jnp
        _rk = jax.random.key(seed)
        x = 7.22e-05 + 1 * jax.random.normal(jax.random.fold_in(_rk, 1), (16, 224, 512), jnp.float32)
        _lenS = 224 - jax.random.randint(jax.random.fold_in(_rk, 7), (16,), 0, max(1, 224 // 4) + 1, jnp.int32)
        _lenS2 = 750 - jax.random.randint(jax.random.fold_in(_rk, 8), (16,), 0, max(1, 750 // 4) + 1, jnp.int32)
        _ctx_768P = jax.random.normal(jax.random.fold_in(_rk, 11), (16, 16, 384), jnp.float32)
        _ctx_768c = jax.random.dirichlet(jax.random.fold_in(_rk, 511), 0.3 * jnp.ones((16,), jnp.float32), (16, 750))
        _ctx_768t = jnp.einsum('bsk,bkd->bsd', _ctx_768c, _ctx_768P)
        _ctx_768t = _ctx_768t * jax.lax.rsqrt(jnp.mean(jnp.square(_ctx_768t)) + 1e-12) * 0.953939
        ctx_768 = -0.000191848 + 0.999787 * (_ctx_768t + 0.3 * jax.random.normal(jax.random.fold_in(_rk, 611), (16, 750, 384), jnp.float32))
        _validS = jnp.arange(224)[None, :] < _lenS[:, None]
        _validS2 = jnp.arange(750)[None, :] < _lenS2[:, None]
        _causal = jnp.tril(jnp.ones((224, 224), dtype=bool))
        mask_BxS2_bk0 = jnp.logical_not(jnp.broadcast_to(_validS2[:, :], (16, 750)))
        return (x, ctx_768, mask_BxS2_bk0)
    x, ctx_768, mask_BxS2_bk0 = _rec_inputs()

    def _L0_attn_setup():
        import jax, jax.numpy as jnp
        import numpy as np
        EPS = 1e-06
        NEG = -10000.0

        def compute_alibi_slopes(n_head):
            start = 2.0 ** (-8.0 / n_head)
            return jnp.asarray([start ** (i + 1) for i in range(n_head)], dtype=jnp.float32)

        def rational_softmax(scores, eps=EPS):
            num = 0.5 * (1.0 + scores * jax.lax.rsqrt(1.0 + scores * scores))
            return num / (jnp.sum(num, axis=-1, keepdims=True) + eps)
        key = jax.random.key(seed)
        k1, k2, k3 = jax.random.split(key, 3)
        B, T, C, H = (2, 1024, 512, 16)
        x = jax.random.normal(k1, (B, T, C), dtype=jnp.float32)
        w_qkv = jax.random.normal(k2, (3 * C, C), dtype=jnp.float32) * C ** (-0.5)
        w_out = jax.random.normal(k3, (C, C), dtype=jnp.float32) * C ** (-0.5)
        alibi_slopes = compute_alibi_slopes(H)
        return {'x': x, 'w_qkv': w_qkv, 'w_out': w_out, 'alibi_slopes': alibi_slopes}
    _L0_attn_all = _L0_attn_setup()
    _L0_attn_in = {k: v for k, v in _L0_attn_all.items() if k in ('w_qkv', 'w_out', 'alibi_slopes')}
    del _L0_attn_all

    def _L0_xattn_setup():
        import jax, jax.numpy as jnp
        import numpy as np
        HEADS = 8
        DIM_HEAD = 64
        QUERY_DIM = 512
        CONTEXT_DIM = 384
        INNER = HEADS * DIM_HEAD
        key = jax.random.key(seed)
        ks = jax.random.split(key, 8)
        b, n, j = (4, 1024, 1024)
        x = jax.random.normal(ks[0], (b, n, QUERY_DIM), dtype=jnp.float32)
        context = jax.random.normal(ks[1], (b, j, CONTEXT_DIM), dtype=jnp.float32)
        mask = jax.random.randint(ks[2], (b, j), 0, 2).astype(jnp.bool_)
        W_q = jax.random.normal(ks[3], (QUERY_DIM, INNER), dtype=jnp.float32) / np.sqrt(QUERY_DIM)
        W_k = jax.random.normal(ks[4], (CONTEXT_DIM, INNER), dtype=jnp.float32) / np.sqrt(CONTEXT_DIM)
        W_v = jax.random.normal(ks[5], (CONTEXT_DIM, INNER), dtype=jnp.float32) / np.sqrt(CONTEXT_DIM)
        W_o = jax.random.normal(ks[6], (INNER, QUERY_DIM), dtype=jnp.float32) / np.sqrt(INNER)
        b_o = jax.random.normal(ks[7], (QUERY_DIM,), dtype=jnp.float32) * 0.01
        return {'x': x, 'context': context, 'mask': mask, 'W_q': W_q, 'W_k': W_k, 'W_v': W_v, 'W_o': W_o, 'b_o': b_o}
    _L0_xattn_all = _L0_xattn_setup()
    _L0_xattn_in = {k: v for k, v in _L0_xattn_all.items() if k in ('W_q', 'W_k', 'W_v', 'W_o', 'b_o')}
    del _L0_xattn_all

    def _L0_ffn_setup():
        import jax, jax.numpy as jnp
        import numpy as np
        TOP_K = 2
        CAPACITY_FACTOR = 1.0
        key = jax.random.key(seed)
        ks = jax.random.split(key, 4)
        sl, bs, hs, ffn, E = (1024, 8, 512, 2048, 8)
        x = jax.random.normal(ks[0], (sl, bs, hs), dtype=jnp.float32)
        w_router = jax.random.normal(ks[1], (hs, E), dtype=jnp.float32) * 0.02
        w1 = jax.random.normal(ks[2], (E, hs, ffn), dtype=jnp.float32) * 0.02
        w2 = jax.random.normal(ks[3], (E, ffn, hs), dtype=jnp.float32) * 0.02
        bias = jnp.zeros((1, 1, hs), dtype=jnp.float32)
        return {'x': x, 'w_router': w_router, 'w1': w1, 'w2': w2, 'bias': bias}
    _L0_ffn_all = _L0_ffn_setup()
    _L0_ffn_in = {k: v for k, v in _L0_ffn_all.items() if k in ('w_router', 'w1', 'w2', 'bias')}
    del _L0_ffn_all
    return {'x': x, 'ctx_768': ctx_768, 'mask_BxS2_bk0': mask_BxS2_bk0, 'L0_attn_w_qkv': _L0_attn_in['w_qkv'], 'L0_attn_w_out': _L0_attn_in['w_out'], 'L0_attn_alibi_slopes': _L0_attn_in['alibi_slopes'], 'L0_xattn_W_q': _L0_xattn_in['W_q'], 'L0_xattn_W_k': _L0_xattn_in['W_k'], 'L0_xattn_W_v': _L0_xattn_in['W_v'], 'L0_xattn_W_o': _L0_xattn_in['W_o'], 'L0_xattn_b_o': _L0_xattn_in['b_o'], 'L0_ffn_w_router': _L0_ffn_in['w_router'], 'L0_ffn_w1': _L0_ffn_in['w1'], 'L0_ffn_w2': _L0_ffn_in['w2'], 'L0_ffn_bias': _L0_ffn_in['bias']}

def reference(x, ctx_768, mask_BxS2_bk0, L0_attn_w_qkv, L0_attn_w_out, L0_attn_alibi_slopes, L0_xattn_W_q, L0_xattn_W_k, L0_xattn_W_v, L0_xattn_W_o, L0_xattn_b_o, L0_ffn_w_router, L0_ffn_w1, L0_ffn_w2, L0_ffn_bias):
    import jax
    import jax.numpy as jnp

    def _L0_attn_ref(x, w_qkv, w_out, alibi_slopes):
        import jax, jax.numpy as jnp
        import numpy as np
        EPS = 1e-06
        NEG = -10000.0

        def compute_alibi_slopes(n_head):
            start = 2.0 ** (-8.0 / n_head)
            return jnp.asarray([start ** (i + 1) for i in range(n_head)], dtype=jnp.float32)

        def rational_softmax(scores, eps=EPS):
            num = 0.5 * (1.0 + scores * jax.lax.rsqrt(1.0 + scores * scores))
            return num / (jnp.sum(num, axis=-1, keepdims=True) + eps)
        B, T, C = x.shape
        H = alibi_slopes.shape[0]
        D = C // H
        scale = 1.0 / jnp.sqrt(jnp.float32(D))
        qkv = (x @ w_qkv.T).reshape(B, T, 3, H, D)
        qkv = jnp.transpose(qkv, (2, 0, 3, 1, 4))
        q, k, v = (qkv[0], qkv[1], qkv[2])
        scores = jnp.einsum('bhtd,bhsd->bhts', q, k) * scale
        pos = jnp.arange(T)
        rel = pos[:, None] - pos[None, :]
        alibi = -jnp.abs(rel).astype(jnp.float32) * alibi_slopes[None, :, None, None]
        scores = scores + alibi
        causal = rel < 0
        scores = jnp.where(causal[None, None], NEG, scores)
        probs = rational_softmax(scores, EPS)
        out = jnp.einsum('bhts,bhsd->bhtd', probs, v)
        out = jnp.transpose(out, (0, 2, 1, 3)).reshape(B, T, C)
        return out @ w_out.T

    def _L0_xattn_ref(x, context, mask, W_q, W_k, W_v, W_o, b_o):
        import jax, jax.numpy as jnp
        import numpy as np
        HEADS = 8
        DIM_HEAD = 64
        QUERY_DIM = 512
        CONTEXT_DIM = 384
        INNER = HEADS * DIM_HEAD
        b, n, _ = x.shape
        j = context.shape[1]
        scale = DIM_HEAD ** (-0.5)
        q = (x @ W_q).reshape(b, n, HEADS, DIM_HEAD)
        k = (context @ W_k).reshape(b, j, HEADS, DIM_HEAD)
        v = (context @ W_v).reshape(b, j, HEADS, DIM_HEAD)
        sim = jnp.einsum('bihd,bjhd->bhij', q, k) * scale
        max_neg = -jnp.finfo(sim.dtype).max
        sim = jnp.where(mask[:, None, None, :], sim, max_neg)
        attn = jax.nn.softmax(sim, axis=-1)
        out = jnp.einsum('bhij,bjhd->bihd', attn, v).reshape(b, n, INNER)
        return out @ W_o + b_o

    def _L0_ffn_ref(x, w_router, w1, w2, bias):
        import jax, jax.numpy as jnp
        import numpy as np
        TOP_K = 2
        CAPACITY_FACTOR = 1.0
        sl, bs, hs = x.shape
        E = w_router.shape[1]
        xf = x.reshape(-1, hs)
        T = xf.shape[0]
        capacity = int(CAPACITY_FACTOR * TOP_K * T / E)
        scores = jax.nn.softmax(xf @ w_router, axis=-1)
        expert_weights, top_experts = jax.lax.top_k(scores, TOP_K)
        flat_e = top_experts.reshape(-1)
        flat_w = expert_weights.reshape(-1)
        N = flat_e.shape[0]
        order = jnp.argsort(flat_e, stable=True)
        bin_ids = flat_e[order]
        tpe = jnp.zeros((E,), jnp.int32).at[flat_e].add(1)
        starts = jnp.cumsum(tpe) - tpe
        offsets = jnp.arange(N) - starts[bin_ids]
        valid = offsets < capacity
        slot = jnp.where(valid, bin_ids * capacity + offsets, E * capacity)
        src = order // TOP_K
        xb = jnp.zeros((E * capacity + 1, hs), x.dtype).at[slot].set(xf[src])
        xb = xb[:-1].reshape(E, capacity, hs)
        h = jax.nn.gelu(jnp.einsum('ech,ehf->ecf', xb, w1))
        y = jnp.einsum('ecf,efh->ech', h, w2).reshape(E * capacity, hs)
        yv = jnp.where(valid[:, None], y[jnp.minimum(slot, E * capacity - 1)], 0.0)
        out = jnp.zeros((T, hs), x.dtype).at[src].add(flat_w[order][:, None] * yv)
        return out.reshape(sl, bs, hs) + bias
    x = x + _L0_attn_ref(_layernorm(x, axis=-1), L0_attn_w_qkv, L0_attn_w_out, L0_attn_alibi_slopes)
    x = x + _L0_xattn_ref(_layernorm(x, axis=-1), ctx_768, mask_BxS2_bk0, L0_xattn_W_q, L0_xattn_W_k, L0_xattn_W_v, L0_xattn_W_o, L0_xattn_b_o)
    x = x + _L0_ffn_ref(_layernorm(x, axis=-1), L0_ffn_w_router, L0_ffn_w1, L0_ffn_w2, L0_ffn_bias)
    return x

_drawn_inputs = setup_inputs


def setup_inputs(seed=0):
    import zlib

    import numpy as np

    out = dict(_drawn_inputs(seed))
    spreads = {'L0_ffn_bias': (0.0, 0.1)}
    factors = {'L0_xattn_b_o': 6.133}
    for name, (base, spread) in spreads.items():
        noise = np.random.default_rng([zlib.crc32(name.encode()), seed]).standard_normal(out[name].shape)
        drawn = base * np.exp(spread * noise) if base else spread * noise
        out[name] = jnp.asarray(drawn.astype(out[name].dtype))
    for name, factor in factors.items():
        out[name] = (out[name] * factor).astype(out[name].dtype)
    return out
```

```python
from contextlib import ExitStack

import concourse.bass as bass
from concourse import mybir

F32, F32R, BF16 = mybir.dt.float32, mybir.dt.float32r, mybir.dt.bfloat16
I32, U32, U8 = mybir.dt.int32, mybir.dt.uint32, mybir.dt.uint8
ALU, ACT, AX = mybir.AluOpType, mybir.ActivationFunctionType, mybir.AxisListType

B, T, C = 16, 224, 512
KC = C // 128
R = T // 2
TPI = 4
TOK = TPI * R
H1, D1 = 16, 32
H2, D2 = 8, 64
LN_EPS, RS_EPS = 1e-5, 1e-6
FLT_MAX = 3.4028234663852886e38
J, CC, JB = 750, 3, 125
E, CAP, F = 8, 896, 2048




def self_attention(nc, x, w_qkvT, w_outT, w_qT, slopes, x1_dram, q2_dram):
    NIT = B * T // TOK
    x_v = x.rearrange("(i j r) c -> i r j c", j=TPI, r=R)
    x1_v = x1_dram.rearrange("(i j r) c -> i r j c", j=TPI, r=R)
    q2_v = q2_dram.rearrange("(i b) p k t -> i b p k t", b=2)
    NG = 8
    NPAIR = T + R
    with ExitStack() as ctx:
        sb = lambda n, s, d=F32: ctx.enter_context(nc.sbuf_tensor("a_" + n, s, d))
        sem = lambda n: ctx.enter_context(nc.semaphore("a_" + n))
        wqkv = [sb(f"wqkv{k}", [128, KC, 3 * C], F32R) for k in "hl"]
        wout = [sb(f"wout{k}", [128, KC, C], F32R) for k in "hl"]
        wq2 = [sb(f"wq2{k}", [128, KC, C], F32R) for k in "hl"]
        ident = sb("ident", [R, R])
        dist = sb("dist", [R, NPAIR])
        keep = sb("keep", [R, NPAIR])
        slope = sb("slope", [R, H1])
        ones = sb("ones", [R, 32])
        eps = sb("eps", [128, 3])
        x_in = sb("x_in", [R, TPI, C])
        xr = sb("xr", [R, TPI, C])
        work = sb("work", [128, TPI * C])
        xn = work[0:R, :].rearrange("p (j c) -> p j c", j=TPI)
        oT = work[:, 0:KC * TOK].rearrange("p (k t) -> p k t", k=KC)
        xT = [sb(f"xT{k}", [128, KC, TOK], F32R) for k in "hl"]
        stats = sb("stats", [R, TPI, 6])
        mv = sb("mv", [R, TPI, 2])
        rstd = sb("rstd", [R, TPI])
        nt = sb("nt", [R, 2, TPI])
        qz = sb("qz", [128, KC, 4, TOK])
        kT = sb("kT", [128, KC, TOK])
        v = sb("v", [R, TPI, C])
        s_sb = sb("s_sb", [R, 2, 4, NPAIR])
        r_sb = sb("r_sb", [R, 2, 4, NPAIR])
        u_sb = sb("u_sb", [R, 2, 4, NPAIR])
        num = u_sb
        q_sb = sb("q_sb", [R, 4, NPAIR])
        rden = sb("rden", [128, 2, T])
        dt = sb("dt", [128, 2, T])
        q2 = kT
        bank = [ctx.enter_context(nc.psum_tensor(f"a_bank{k}", [128, 512], F32)) for k in range(8)]
        gen, sc, pvb = bank[0:2], bank[2:6], bank[6:8]

        w_hi, w_lo = sem("w_hi"), sem("w_lo")
        w_loaded = [sem(f"w_loaded{k}") for k in range(4)]
        const_set, const_ready, zeroed, slope_loaded = sem("const_set"), sem("const_ready"), sem("zeroed"), sem("slope_loaded")
        x_loaded, xr_loaded, x1_stored, q2_stored = sem("x_loaded"), sem("xr_loaded"), sem("x1_stored"), sem("q2_stored")
        stats_made = [sem("stats_made0"), sem("stats_made1")]
        mv_made, root_made, rstd_made, xn_made = sem("mv_made"), sem("root_made"), sem("rstd_made"), sem("xn_made")
        newton = [sem(f"newton{k}") for k in range(3)]
        gen_full = sem("gen_full")
        gen_free = [sem("gen_free0"), sem("gen_free1")]
        xT_hi, xT_lo = sem("xT_hi"), sem("xT_lo")
        q_made, k_made, v_made = sem("q_made"), sem("k_made"), sem("v_made")
        qkv_done = sem("qkv_done")
        sc_full, s_made, u_made, r_made, p_made, num_made = (sem(n) for n in ("sc_full", "s_made", "u_made", "r_made", "p_made", "num_made"))
        rr_made, m_made, p2_made, y_made = sem("rr_made"), sem("m_made"), sem("p2_made"), sem("y_made")
        pv_full, rs_made, rden_made, o_made = sem("pv_full"), sem("rs_made"), sem("rden_made"), sem("o_made")
        x1_made, q2_made = sem("x1_made"), sem("q2_made")

        T1, QK, V, OUT, T2, Q2 = 0, 4, 12, 16, 20, 24
        USES = 28
        pieces = [(w_qkvT[:, k, :], wqkv, slice(k, k + 1), 3 * C) for k in range(KC)]
        pieces += [(w_outT[:, k, :], wout, slice(k, k + 1), C) for k in range(KC)]
        pieces += [(w_qT[:, k, :], wq2, slice(k, k + 1), C) for k in range(KC)]
        stage = qz[:, :, :, :].rearrange("p a b c -> p (a b c)")
        NST = 4

        block = ctx.enter_context(nc.Block())

        @block.sync
        def _(sp):
            sp.dma_start(slope[:], slopes.partition_broadcast(R)).then_inc(slope_loaded, 16)
            for n, (src, dst, ks, w) in enumerate(pieces):
                if n >= NST:
                    sp.wait_ge(w_lo, n - NST + 1)
                sp.dma_start(stage[:, (n % NST) * 3 * C:(n % NST) * 3 * C + w], src).then_inc(w_loaded[n % NST], 16)
                if n == 0:
                    sp.dma_start(x_in[:], x_v[0]).then_inc(x_loaded, 16)
                    sp.dma_start(xr[:], x_v[0]).then_inc(xr_loaded, 16)
            with sp.Fori(1, NIT) as i:
                sp.wait_ge(xn_made, i * (2 * TPI) - TPI)
                sp.dma_start(x_in[:], x_v[bass.ds(i, 1)].rearrange("a r j c -> (a r) j c")).then_inc(x_loaded, 16)
                sp.wait_ge(x_loaded, 16)
                sp.wait_ge(x1_made, i * TPI)
                sp.dma_start(x1_v[bass.ds(i - 1, 1)].rearrange("a r j c -> (a r) j c"), xr[:]).then_inc(x1_stored, 16)
                sp.wait_ge(q2_made, i * KC)
                for b in range(2):
                    sp.dma_start(q2_v[bass.ds(i - 1, 1), b].rearrange("a p k t -> (a p) k t"), q2[:, :, b * T:b * T + T]).then_inc(q2_stored, 16)
                sp.wait_ge(slope_loaded, 16)
                sp.wait_ge(x1_stored, i * 16)
                sp.wait_ge(slope_loaded, 16)
                sp.wait_ge(xn_made, i * (2 * TPI))
                sp.dma_start(xr[:], x_v[bass.ds(i, 1)].rearrange("a r j c -> (a r) j c")).then_inc(xr_loaded, 16)
            sp.wait_ge(x1_made, NIT * TPI)
            sp.dma_start(x1_v[NIT - 1], xr[:]).then_inc(x1_stored, 16)
            sp.wait_ge(q2_made, NIT * KC)
            for b in range(2):
                sp.dma_start(q2_v[NIT - 1, b], q2[:, :, b * T:b * T + T]).then_inc(q2_stored, 16)
            sp.wait_ge(x1_stored, NIT * 16)
            sp.wait_ge(q2_stored, NIT * 32)

        @block.gpsimd
        def _(pool):
            pool.iota(dist[:, 0:T], [[-1, T]], base=0, channel_multiplier=1, allow_small_or_imprecise_dtypes=True).then_inc(const_set, 1)
            pool.iota(dist[:, T:], [[-1, R]], base=0, channel_multiplier=1, allow_small_or_imprecise_dtypes=True).then_inc(const_set, 1)
            pool.memset(keep[:], -1.0).then_inc(const_set, 1)
            pool.memset(ident[:], 1.0).then_inc(const_set, 1)
            pool.memset(ones[:], 1.0).then_inc(const_set, 1)
            pool.memset(eps[:, 0:1], LN_EPS).then_inc(const_set, 1)
            pool.memset(eps[:, 1:2], 1.0).then_inc(const_set, 1)
            pool.memset(eps[:, 2:3], 4 * RS_EPS).then_inc(const_set, 1)
            pool.wait_ge(const_set, 8)
            for a, w in ((0, T), (T, R)):
                pool.affine_select(out=keep[:, a:a + w], in_=keep[:, a:a + w], pattern=[[1, w]], compare_op=ALU.is_ge,
                                   fill=0.0, base=0, channel_multiplier=-1).then_inc(const_ready, 1)
            pool.affine_select(out=ident[:], in_=ident[:], pattern=[[1, R]], compare_op=ALU.is_equal, fill=0.0,
                               base=0, channel_multiplier=-1).then_inc(const_ready, 1)
            with pool.Fori(0, NIT) as i:
                for n in range(NG):
                    pool.wait_ge(r_made, i * NG + n + 1)
                    pool.tensor_tensor(s_sb[:, n % 2], s_sb[:, n % 2], r_sb[:, n % 2], ALU.mult).then_inc(p_made, 1)

        CONSTS = 3

        def split_lo(eng, lo, src, hi, inc):
            eng.tensor_tensor(lo, src, hi.bitcast(F32), ALU.subtract).then_inc(inc, 1)

        @block.vector
        def _(dve):
            for n, (src, dst, ks, w) in enumerate(pieces):
                st = stage[:, (n % NST) * 3 * C:(n % NST) * 3 * C + w]
                dve.wait_ge(w_loaded[n % NST], 16 * (n // NST + 1))
                dve.tensor_copy(dst[0][:, ks.start, :], st).then_inc(w_hi, 1)
                dve.wait_ge(w_hi, n + 1)
                dve.tensor_tensor(dst[1][:, ks.start, :], st, dst[0][:, ks.start, :].bitcast(F32), ALU.subtract).then_inc(w_lo, 1)
            dve.wait_ge(w_lo, len(pieces))
            dve.memset(stage, 0.0).then_inc(zeroed, 1)

            def layernorm(i, turn, src, half):
                for j in range(TPI):
                    ins = dve.bn_stats(stats[:, j, :], src[:, j, :])
                ins.then_inc(stats_made[half], 1)
                dve.wait_ge(const_ready, CONSTS)
                dve.wait_ge(stats_made[half], turn)
                for j in range(TPI):
                    dve.bn_aggr(mv[:, j, :], stats[:, j, :]).then_inc(mv_made, 1)
                dve.wait_ge(root_made, i * 2 + half + 1)
                dve.tensor_tensor(nt[:, 0, :], rstd[:], rstd[:], ALU.mult).then_inc(newton[0], 1)
                dve.wait_ge(newton[0], i * 2 + half + 1)
                dve.scalar_tensor_tensor(nt[:, 1, :], mv[:, :, 1], LN_EPS, nt[:, 0, :], ALU.add, ALU.mult).then_inc(newton[1], 1)
                dve.wait_ge(newton[1], i * 2 + half + 1)
                dve.tensor_scalar(nt[:, 0, :], nt[:, 1, :], -0.5, 1.5, ALU.mult, ALU.add).then_inc(newton[2], 1)
                dve.wait_ge(newton[2], i * 2 + half + 1)
                dve.tensor_tensor(rstd[:], rstd[:], nt[:, 0, :], ALU.mult).then_inc(rstd_made, 1)
                for j in range(TPI):
                    if j == 0:
                        dve.wait_ge(gen_full, i * USES + (T1 if half == 0 else T2))
                        dve.wait_ge(rstd_made, i * 2 + half + 1)
                    dve.tensor_scalar(xn[:, j, :], src[:, j, :], mv[:, j, 0:1], rstd[:, j:j + 1], ALU.subtract, ALU.mult).then_inc(xn_made, 1)

            def transposed_lo(i, base, half):
                for c in range(KC):
                    dve.wait_ge(xT_hi, i * (3 * KC) + half * KC + c + 1)
                    dve.tensor_tensor(xT[1][:, c, :], gen[c % 2][:, 0:TOK], xT[0][:, c, :].bitcast(F32),
                                      ALU.subtract).then_inc(gen_free[c % 2], 1)

            dve.wait_ge(slope_loaded, 16)
            with dve.Fori(1, NIT + 1) as turn:
                i = turn - 1
                dve.wait_ge(x_loaded, i * 16 + 16)
                layernorm(i, turn, x_in, 0)
                transposed_lo(i, T1, 0)
                for m in range(KC):
                    u = QK + KC + m
                    dve.wait_ge(gen_full, i * USES + u + 1)
                    if m == 0:
                        dve.wait_ge(q2_stored, i * 32)
                    dve.tensor_copy(kT[:, m, :], gen[u % 2][:, 0:TOK]).then_inc(gen_free[u % 2], 1)

                def score(n):
                    b, g = divmod(n, 4)
                    if n == 0:
                        dve.wait_ge(num_made, i * NG)
                    elif n >= 2:
                        dve.wait_ge(num_made, i * NG + n - 1)
                    for r in range(4):
                        dve.wait_ge(sc_full, i * 32 + 4 * n + r + 1)
                        dve.scalar_tensor_tensor(s_sb[:, n % 2, r, :], dist[:], slope[:, 4 * g + r:4 * g + r + 1],
                                                 sc[r][0:R, 0:NPAIR], ALU.mult, ALU.add).then_inc(s_made, 1)

                def numerator(n):
                    dve.wait_ge(rr_made, i * NG + n + 1)
                    dve.scalar_tensor_tensor(u_sb[:, n % 2], u_sb[:, n % 2], 1.0, q_sb[:], ALU.add, ALU.mult).then_inc(m_made, 1)
                    dve.wait_ge(p_made, i * NG + n + 1)
                    dve.wait_ge(m_made, i * NG + n + 1)
                    dve.scalar_tensor_tensor(s_sb[:, n % 2], u_sb[:, n % 2], 3.0, s_sb[:, n % 2], ALU.subtract, ALU.mult).then_inc(p2_made, 1)
                    dve.wait_ge(p2_made, i * NG + n + 1)
                    dve.scalar_tensor_tensor(num[:, n % 2], s_sb[:, n % 2], 2.0,
                                             keep[:, None, :].broadcast_to([R, 4, NPAIR]), ALU.subtract, ALU.mult).then_inc(num_made, 1)

                def output(n):
                    b, g = divmod(n, 4)
                    dve.wait_ge(rden_made, i * NG + n + 1)
                    dve.wait_ge(o_made, i * NG + n)
                    dve.scalar_tensor_tensor(dt[:, 0, :], pvb[n % 2][:, T:2 * T], 4 * RS_EPS, rden[:, n % 2], ALU.add, ALU.mult).then_inc(y_made, 1)
                    dve.tensor_tensor(dt[:, 1, :], pvb[n % 2][:, 0:T], rden[:, n % 2], ALU.mult).then_inc(y_made, 1)
                    dve.wait_ge(y_made, i * (2 * NG) + 2 * n + 2)
                    dve.scalar_tensor_tensor(oT[:, g, b * T:(b + 1) * T], dt[:, 0, :], 2.0, dt[:, 1, :], ALU.subtract, ALU.mult).then_inc(o_made, 1)

                for n in range(NG + 2):
                    if n < NG:
                        score(n)
                    if 1 <= n <= NG:
                        numerator(n - 1)
                    if n >= 2:
                        output(n - 2)
                for c in range(KC):
                    dve.wait_ge(xT_hi, i * (3 * KC) + KC + c + 1)
                    dve.tensor_tensor(xT[1][:, c, :], oT[:, c, :], xT[0][:, c, :].bitcast(F32), ALU.subtract).then_inc(xT_lo, 1)
                for j in range(TPI):
                    u = OUT + j
                    if j == 0:
                        dve.wait_ge(xr_loaded, i * 16 + 16)
                    dve.wait_ge(gen_full, i * USES + u + 1)
                    dve.tensor_tensor(xr[:, j, :], xr[:, j, :], gen[u % 2][0:R, :], ALU.subtract).then_inc(x1_made, 1)
                dve.wait_ge(x1_made, i * TPI + TPI)
                layernorm(i, turn, xr, 1)
                transposed_lo(i, T2, 2)

        @block.scalar
        def _(act):
            act.wait_ge(const_ready, CONSTS)

            def rstd_of(i, half):
                act.wait_ge(mv_made, i * (2 * TPI) + half * TPI + TPI)
                act.activation(rstd[:], mv[:, :, 1], ACT.Abs_reciprocal_sqrt, bias=eps[0:R, 0:1]).then_inc(root_made, 1)

            def transposed_hi(i, base):
                for c in range(KC):
                    act.wait_ge(gen_full, i * USES + base + c + 1)
                    act.copy(xT[0][:, c, :], gen[c % 2][:, 0:TOK]).then_inc(xT_hi, 1)

            with act.Fori(0, NIT) as i:
                rstd_of(i, 0)
                transposed_hi(i, T1)
                act.wait_ge(zeroed, 1)
                for m in range(KC):
                    u = QK + m
                    act.wait_ge(gen_full, i * USES + u + 1)
                    for r in range(4):
                        ins = act.mul(qz[32 * r:32 * r + 32, m, r, :], gen[u % 2][32 * r:32 * r + 32, 0:TOK], D1 ** -0.5)
                        ins.then_inc(gen_free[u % 2] if r == 3 else q_made, 1)
                for j in range(TPI):
                    u = V + j
                    act.wait_ge(gen_full, i * USES + u + 1)
                    act.copy(v[:, j, :], gen[u % 2][0:R, :]).then_inc(gen_free[u % 2], 1)

                def root(n):
                    if n >= 2:
                        act.wait_ge(pv_full, i * NG + n - 1)
                    act.wait_ge(s_made, i * 32 + 4 * n + 4)
                    act.activation(u_sb[:, n % 2], s_sb[:, n % 2], ACT.Square).then_inc(u_made, 1)
                    act.wait_ge(u_made, i * NG + n + 1)
                    act.activation(r_sb[:, n % 2], u_sb[:, n % 2], ACT.Abs_reciprocal_sqrt, bias=eps[0:R, 1:2]).then_inc(r_made, 1)
                    act.wait_ge(r_made, i * NG + n + 1)
                    if n >= 1:
                        act.wait_ge(m_made, i * NG + n)
                    act.activation(q_sb[:], r_sb[:, n % 2], ACT.Square).then_inc(rr_made, 1)

                def reciprocal(n):
                    act.wait_ge(pv_full, i * NG + n + 1)
                    if n >= 2:
                        act.wait_ge(o_made, i * NG + n - 1)
                    act.activation(rden[:, n % 2], pvb[n % 2][:, T:2 * T], ACT.Abs_reciprocal_sqrt, bias=eps[:, 2:3]).then_inc(rs_made, 1)
                    act.wait_ge(rs_made, i * NG + n + 1)
                    act.activation(rden[:, n % 2], rden[:, n % 2], ACT.Square).then_inc(rden_made, 1)

                for n in range(NG + 2):
                    if n < NG:
                        root(n)
                    if n >= 2:
                        reciprocal(n - 2)
                for c in range(KC):
                    act.wait_ge(o_made, i * NG + 4 + c + 1)
                    act.copy(xT[0][:, c, :], oT[:, c, :]).then_inc(xT_hi, 1)
                rstd_of(i, 1)
                transposed_hi(i, T2)
                for m in range(KC):
                    u = Q2 + m
                    act.wait_ge(gen_full, i * USES + u + 1)
                    act.mul(q2[:, m, :], gen[u % 2][:, 0:TOK], D2 ** -0.5).then_inc(q2_made, 1)

        @block.tensor
        def _(pe):
            def bank_free(i, u):
                b, k = u % 2, u // 2
                if u < OUT:
                    if u // 2 == 0:
                        pe.wait_ge(q2_made, i * KC)
                    else:
                        pe.wait_ge(gen_free[b], i * GF + k)
                elif u < OUT + 2:
                    pe.wait_ge(gen_free[b], i * GF + 8)
                elif u < T2:
                    pe.wait_ge(x1_made, i * TPI + u - OUT - 1)
                elif u < T2 + 2:
                    pe.wait_ge(x1_made, i * TPI + u - OUT - 1)
                elif u < Q2 + 2:
                    pe.wait_ge(gen_free[b], i * GF + 8 + (u - T2) // 2)
                else:
                    pe.wait_ge(q2_made, i * KC + u - Q2 - 1)

            GF = 10

            def transposes(i, base, half):
                pe.wait_ge(xn_made, i * (2 * TPI) + half * TPI + TPI)
                for c in range(KC):
                    bank_free(i, base + c)
                    for j in range(TPI):
                        mm = pe.transpose(gen[c % 2][:, R * j:R * j + R], xn[:, j, 128 * c:128 * c + 128], ident[:])
                    mm.then_inc(gen_full, 1)

            def product(out, lhs, rhs, n=KC):
                steps = [(a, b, k) for a, b in ((0, 0), (0, 1), (1, 0)) for k in range(n)]
                for q, (a, b, k) in enumerate(steps):
                    mm = pe.matmul(out, lhs(a, k), rhs(b, k), start=q == 0, stop=q == len(steps) - 1)
                return mm

            pe.wait_ge(const_ready, CONSTS)
            pe.wait_ge(w_lo, len(pieces))
            with pe.Fori(0, NIT) as i:
                transposes(i, T1, 0)
                pe.wait_ge(gen_free[0], i * GF + 2)
                pe.wait_ge(gen_free[1], i * GF + 2)
                for m in range(8):
                    bank_free(i, QK + m)
                    product(gen[m % 2][:, 0:TOK], lambda a, k: wqkv[a][:, k, 128 * m:128 * m + 128],
                            lambda b, k: xT[b][:, k, :]).then_inc(gen_full, 1)
                for j in range(TPI):
                    bank_free(i, V + j)
                    product(gen[j % 2][0:R, :], lambda a, k: xT[a][:, k, R * j:R * j + R],
                            lambda b, k: wqkv[b][:, k, 2 * C:3 * C]).then_inc(gen_full, 1)

                def scores(n):
                    b, g = divmod(n, 4)
                    if n == 0:
                        for e in range(2):
                            pe.wait_ge(gen_free[e], i * GF + 8)
                    for r in range(4):
                        if n >= 1:
                            pe.wait_ge(s_made, i * 32 + 4 * (n - 1) + r + 1)
                        t0 = b * T
                        pe.matmul(sc[r][0:R, 0:T], kT[:, g, t0:t0 + R], qz[:, g, r, t0:t0 + T], start=True, stop=True)
                        pe.matmul(sc[r][0:R, T:NPAIR], kT[:, g, t0 + R:t0 + T], qz[:, g, r, t0 + R:t0 + T],
                                  start=True, stop=True).then_inc(sc_full, 1)

                def values(n):
                    b, g = divmod(n, 4)
                    pe.wait_ge(num_made, i * NG + n + 1)
                    if n >= 2:
                        pe.wait_ge(o_made, i * NG + n - 1)
                    for den in range(2):
                        for st in range(2):
                            for r in range(4):
                                h = 4 * g + r
                                lhs = ones[:] if den else v[:, 2 * b + st, 32 * h:32 * h + 32]
                                o0 = den * T
                                if st == 0:
                                    mm = pe.matmul(pvb[n % 2][32 * r:32 * r + 32, o0:o0 + T], lhs, num[:, n % 2, r, 0:T],
                                                   start=True, stop=False, tile_position=(0, 32 * r))
                                else:
                                    mm = pe.matmul(pvb[n % 2][32 * r:32 * r + 32, o0 + R:o0 + T], lhs,
                                                   num[:, n % 2, r, T:NPAIR], start=False, stop=True, tile_position=(0, 32 * r))
                    mm.then_inc(pv_full, 1)

                for n in range(NG + 1):
                    if n < NG:
                        scores(n)
                    if n >= 1:
                        values(n - 1)
                pe.wait_ge(xT_lo, i * KC + KC)
                for j in range(TPI):
                    bank_free(i, OUT + j)
                    product(gen[j % 2][0:R, :], lambda a, k: xT[a][:, k, R * j:R * j + R],
                            lambda b, k: wout[b][:, k, :]).then_inc(gen_full, 1)
                transposes(i, T2, 1)
                pe.wait_ge(gen_free[0], i * GF + 10)
                pe.wait_ge(gen_free[1], i * GF + 10)
                for m in range(KC):
                    bank_free(i, Q2 + m)
                    product(gen[m % 2][:, 0:TOK], lambda a, k: wq2[a][:, k, 128 * m:128 * m + 128],
                            lambda b, k: xT[b][:, k, :]).then_inc(gen_full, 1)


def cross_attention(nc, ctxT, mask, q2_dram, x1_dram, w_k, w_v, w_o, b_o, w_r, bias, out, xn_dram, table_dram):
    NJ = J // JB
    mask = mask.bitcast(U8).rearrange("(i j) -> i j", j=J)
    NH = 2 * H2
    x1_v = x1_dram.rearrange("(i j r) c -> i r j c", j=2, r=R)
    out_v = out[0:B * T].rearrange("(i j r) c -> i r j c", j=2, r=R)
    xn_v = xn_dram[0:B * T].rearrange("(i j r) c -> i r j c", j=2, r=R)
    with ExitStack() as ctx:
        sb = lambda n, s, d=F32: ctx.enter_context(nc.sbuf_tensor("c_" + n, s, d))
        sem = lambda n: ctx.enter_context(nc.semaphore("c_" + n))
        wk = [sb(f"wk{k}", [128, CC, C], F32R) for k in "hl"]
        wv = [sb(f"wv{k}", [128, CC, C], F32R) for k in "hl"]
        wo = [sb(f"wo{k}", [128, KC, C], F32R) for k in "hl"]
        wr = sb("wr", [128, KC, E])
        bo, bi = sb("bo", [R, C]), sb("bi", [R, C])
        ident = sb("ident", [R, R])
        craw = sb("craw", [128, CC, J])
        cT = [sb(f"cT{k}", [128, CC, J], F32R) for k in "hl"]
        kT = [sb(f"kT{k}", [128, KC, J], F32R) for k in "hl"]
        v = sb("v", [JB, NJ, C])
        q2 = sb("q2", [128, KC, T])
        qz = [sb(f"qz{k}", [128, H2, T], F32R) for k in "hl"]
        m8 = sb("m8", [R, J], U8)
        mb = sb("mb", [R, J])
        NS = 3
        s_sb = sb("s_sb", [R, NS, J])
        mx, nmx, den, rec = (sb(n, [R, NH]) for n in ("mx", "nmx", "den", "rec"))
        pT = sb("pT", [JB, 2, NJ, T])
        oT = [sb(f"oT{k}", [128, KC, T], F32R) for k in "hl"]
        x1 = sb("x1", [R, 2, C])
        xo = sb("xo", [R, 2, C])
        xn = sb("xn", [R, 2, C])
        xnT = sb("xnT", [128, 2, KC * R])
        stats, mv, rstd, nt = sb("stats", [R, 2, 6]), sb("mv", [R, 2, 2]), sb("rstd", [R, 2]), sb("nt", [R, 2, 2])
        eps = sb("eps", [R, 1])
        L2 = [R, 2, E]
        lg, sc, rank, sel, off, inv, base = (sb(n, L2) for n in ("lg", "sc", "rank", "sel", "off", "inv", "base"))
        selb = sb("selb", L2, BF16)
        lmx, lsum, lrec = (sb(n, [R, 2]) for n in ("lmx", "lsum", "lrec"))
        gt, ge = sb("gt", [R, 2, E, E]), sb("ge", [R, 2, E, E])
        lower = sb("lower", [R, E, E])
        before = sb("before", [R, R], BF16)
        onesb = sb("onesb", [R, R], BF16)
        e896 = sb("e896", [R, E])
        kk = sb("kk", [R, 2, E])
        oh, ohs = sb("oh", [R, 2, 2, E]), sb("ohs", [R, 2, 2, E])
        slotf, slotu = sb("slotf", [R, 4]), sb("slotu", [R, 4], U32)
        tok, tstep = sb("tok", [R, 4]), sb("tstep", [R, 4])
        pay = sb("pay", [R, 4, 2])
        trash = sb("trash", [128, E, CAP // 128, 2])
        zero = sb("zero", [128, C])

        ROUTE = 21
        psum = ctx.enter_context(nc.psum_tensor("c_psum", [128, 8, 512], F32))
        bank = [psum[:, 0:2], psum[:, 2:4]]
        pt = [psum[:, 4], psum[:, 5]]
        ob = [psum[:, 6], psum[:, 7]]
        JH = J // 2
        HW = JH + 1

        def keys(u, n):
            flat = psum[0:n].rearrange("p b c -> p (b c)")
            return flat[:, 1024 * (u % 2):1024 * (u % 2) + 1026].rearrange("p (a j) -> p a j", a=2)[:, :, 0:JH]

        UK, UV, US, UO = 0, 4, 7, 23
        UT, UR = 24, 25
        USES, PER = 26, 13

        w_loaded = [sem(f"w_loaded{k}") for k in range(3)]
        w_hi, w_lo = sem("w_hi"), sem("w_lo")
        small_loaded, const_set, const_ready, zeroed = sem("small_loaded"), sem("const_set"), sem("const_ready"), sem("zeroed")
        trash_set, trash_ready, trash_stored = sem("trash_set"), sem("trash_ready"), sem("trash_stored")
        c_loaded, q_loaded, m_loaded, x_loaded = sem("c_loaded"), sem("q_loaded"), sem("m_loaded"), sem("x_loaded")
        xn_stored, out_stored = sem("xn_stored"), sem("out_stored")
        c_hi, c_lo, qz_hi, qz_lo, mb_made = sem("c_hi"), sem("c_lo"), sem("qz_hi"), sem("qz_lo"), sem("mb_made")
        full = sem("full")
        free = [sem("free0"), sem("free1")]
        k_hi = sem("k_hi")
        s_made, nmx_made, nmx_clear, e_made, rec_made, p_made = (sem(n) for n in ("s_made", "nmx_made", "nmx_clear", "e_made", "rec_made", "p_made"))
        pt_full = sem("pt_full")
        pt_read = [sem("pt_read0"), sem("pt_read1")]
        pv_full, o_hi, o_lo = sem("pv_full"), sem("o_hi"), sem("o_lo")
        x1b_made, xo_made = sem("x1b_made"), sem("xo_made")
        stats_made, mv_made, root_made, rstd_made, xn_made = (sem(n) for n in ("stats_made", "mv_made", "root_made", "rstd_made", "xn_made"))
        newton = sem("newton")
        xnT_made = sem("xnT_made")
        lg_made, le_made, route, sel_made, pre_full, slots_made, sent = (sem(n) for n in ("lg_made", "le_made", "route", "sel_made", "pre_full", "slots_made", "sent"))

        pieces = [(w_k, wk, k) for k in range(CC)] + [(w_v, wv, k) for k in range(CC)] + [(w_o, wo, k) for k in range(KC)]
        block = ctx.enter_context(nc.Block())

        def count(u):
            return u // 2 + 1

        @block.sync
        def _(sp):
            for n, (src, dst, k) in enumerate(pieces):
                if n >= 3:
                    sp.wait_ge(w_lo, n - 2)
                sp.dma_start(craw[:, n % 3, 0:C], src[:, k, :]).then_inc(w_loaded[n % 3], 16)
            for dst, src in ((wr[:], w_r), (bo[:], b_o.partition_broadcast(R)), (bi[:], bias.partition_broadcast(R))):
                sp.dma_start(dst, src).then_inc(small_loaded, 16)
            sp.wait_ge(trash_ready, 2)
            sp.dma_start(table_dram.rearrange("(e p n) w -> p e n w", e=E, n=CAP // 128), trash[:]).then_inc(trash_stored, 16)
            for k in range(CAP // 128):
                r0 = B * T + 128 * k
                sp.dma_start(xn_dram[r0:r0 + 128, :], zero[:]).then_inc(trash_stored, 16)
                sp.dma_start(out[r0:r0 + 128, :], zero[:]).then_inc(trash_stored, 16)
            sp.wait_ge(w_lo, 10)
            sp.dma_start(craw[:], ctxT[0]).then_inc(c_loaded, 16)
            sp.dma_start(q2[:], q2_dram[0]).then_inc(q_loaded, 16)
            sp.dma_start(m8[:], mask[0:1].rearrange("a j -> (a j)").partition_broadcast(R)).then_inc(m_loaded, 16)
            sp.dma_start(x1[:], x1_v[0]).then_inc(x_loaded, 16)
            with sp.Fori(1, B) as i:
                sp.wait_ge(c_lo, i * CC)
                sp.dma_start(craw[:], ctxT[bass.ds(i, 1)].rearrange("a p k j -> (a p) k j")).then_inc(c_loaded, 16)
                sp.wait_ge(small_loaded, 48)
                sp.wait_ge(mb_made, i)
                sp.dma_start(m8[:], mask[bass.ds(i, 1)].rearrange("a j -> (a j)").partition_broadcast(R)).then_inc(m_loaded, 16)
                sp.wait_ge(qz_lo, i * 2)
                sp.dma_start(q2[:], q2_dram[bass.ds(i, 1)].rearrange("a p k t -> (a p) k t")).then_inc(q_loaded, 16)
                sp.wait_ge(small_loaded, 48)
                sp.wait_ge(xo_made, i)
                sp.dma_start(out_v[bass.ds(i - 1, 1)].rearrange("a r j c -> (a r) j c"), xo[:]).then_inc(out_stored, 16)
                sp.wait_ge(small_loaded, 48)
                sp.wait_ge(xn_made, i * 2)
                sp.dma_start(xn_v[bass.ds(i - 1, 1)].rearrange("a r j c -> (a r) j c"), xn[:]).then_inc(xn_stored, 16)
                sp.dma_start(x1[:], x1_v[bass.ds(i, 1)].rearrange("a r j c -> (a r) j c")).then_inc(x_loaded, 16)
            sp.wait_ge(xo_made, B)
            sp.dma_start(out_v[B - 1], xo[:]).then_inc(out_stored, 16)
            sp.wait_ge(xn_made, B * 2)
            sp.dma_start(xn_v[B - 1], xn[:]).then_inc(xn_stored, 16)
            sp.wait_ge(out_stored, 16 * B)
            sp.wait_ge(xn_stored, 16 * B)
            sp.wait_ge(sent, 64 * B)

        @block.gpsimd
        def _(pool):
            n = 0
            for t, val in ((ident, 1.0), (onesb, 1.0), (before, 1.0), (lower, 1.0), (eps, LN_EPS), (tstep, float(T)), (base, 0.0)):
                pool.memset(t[:], val).then_inc(const_set, 1)
            for j in range(2):
                pool.memset(kk[:, j, :], float(j)).then_inc(const_set, 1)
                pool.iota(tok[:, 2 * j:2 * j + 2], [[0, 2]], base=j * R - T, channel_multiplier=1,
                          allow_small_or_imprecise_dtypes=True).then_inc(const_set, 1)
            pool.iota(e896[:], [[CAP, E]], base=0, channel_multiplier=0, allow_small_or_imprecise_dtypes=True).then_inc(const_set, 1)
            pool.wait_ge(const_set, 12)
            pool.affine_select(out=ident[:], in_=ident[:], pattern=[[1, R]], compare_op=ALU.is_equal, fill=0.0,
                               base=0, channel_multiplier=-1).then_inc(const_ready, 1)
            pool.affine_select(out=before[:], in_=before[:], pattern=[[1, R]], compare_op=ALU.is_gt, fill=0.0,
                               base=0, channel_multiplier=-1).then_inc(const_ready, 1)
            pool.affine_select(out=lower[:], in_=lower[:], pattern=[[1, E], [-1, E]], compare_op=ALU.is_gt, fill=0.0,
                               base=0, channel_multiplier=0).then_inc(const_ready, 1)
            pool.memset(trash[:], 0.0).then_inc(trash_set, 1)
            pool.memset(zero[:], 0.0).then_inc(trash_ready, 1)
            pool.wait_ge(trash_set, 1)
            pool.iota(trash[:, :, :, 0].bitcast(I32), [[0, E], [1, CAP // 128]], base=B * T,
                      channel_multiplier=CAP // 128).then_inc(trash_ready, 1)
            pool.wait_ge(trash_stored, 16 * 15)

            with pool.Fori(0, B) as i:
                pool.wait_ge(x_loaded, i * 16 + 16)
                pool.wait_ge(small_loaded, 48)
                pool.tensor_tensor(x1[:], x1[:], bo[:, None, :].broadcast_to([R, 2, C]), ALU.add).then_inc(x1b_made, 1)
                for h in range(NH):
                    pool.wait_ge(rec_made, i * NH + h + 1)
                    pool.tensor_tensor(s_sb[:, h % NS, :], s_sb[:, h % NS, :], rec[:, h:h + 1].broadcast_to([R, J]), ALU.mult).then_inc(p_made, 1)
                pool.wait_ge(out_stored, i * 16)
                pool.wait_ge(free[UO % 2], i * PER + count(UO))
                pool.wait_ge(slots_made, i + 1)
                pool.tensor_tensor(xo[:], x1[:], bi[:, None, :].broadcast_to([R, 2, C]), ALU.add).then_inc(xo_made, 1)
                for q in range(4):
                    pool.indirect_dma_start(out=table_dram, out_offset=bass.IndirectOffsetOnAxis(ap=slotu[:, q:q + 1], axis=0),
                                            in_=pay[:, q, :], in_offset=None, bounds_check=E * CAP - 1, oob_is_err=False).then_inc(sent, 16)

        @block.vector
        def _(dve):
            for n, (src, dst, k) in enumerate(pieces):
                dve.wait_ge(w_loaded[n % 3], 16 * (n // 3 + 1))
                dve.tensor_copy(dst[0][:, k, :], craw[:, n % 3, 0:C]).then_inc(w_hi, 1)
                dve.wait_ge(w_hi, n + 1)
                dve.tensor_tensor(dst[1][:, k, :], craw[:, n % 3, 0:C], dst[0][:, k, :].bitcast(F32), ALU.subtract).then_inc(w_lo, 1)
            for k in range(2):
                dve.memset(qz[k][:].bitcast(F32), 0.0).then_inc(zeroed, 1)
            dve.wait_ge(zeroed, 2)
            dve.wait_ge(const_ready, 3)
            dve.wait_ge(const_set, 12)
            dve.wait_ge(small_loaded, 48)

            with dve.Fori(1, B + 1) as turn:
                i = turn - 1
                for k in range(CC):
                    dve.wait_ge(c_hi, i * CC + k + 1)
                    dve.tensor_tensor(cT[1][:, k, :], craw[:, k, :], cT[0][:, k, :].bitcast(F32), ALU.subtract).then_inc(c_lo, 1)
                for e in range(2):
                    dve.wait_ge(qz_hi, i * 2 + e + 1)
                    p0 = 64 * e
                    dve.tensor_tensor(qz[1][p0:p0 + 64, e::2, :], q2[p0:p0 + 64], qz[0][p0:p0 + 64, e::2, :].bitcast(F32),
                                      ALU.subtract).then_inc(qz_lo, 1)
                for m in range(KC):
                    u = UK + m
                    dve.wait_ge(k_hi, i * KC + m + 1)
                    dve.tensor_tensor(kT[1][:, m, :].rearrange("p (a j) -> p a j", a=2), keys(u, 128),
                                      kT[0][:, m, :].bitcast(F32).rearrange("p (a j) -> p a j", a=2), ALU.subtract).then_inc(free[u % 2], 1)
                dve.wait_ge(m_loaded, i * 16 + 16)
                dve.tensor_scalar(mb[:], m8[:], 1.0, FLT_MAX, ALU.subtract, ALU.mult).then_inc(mb_made, 1)

                def masked(h):
                    u = US + h
                    if h == 0:
                        dve.wait_ge(mb_made, turn)
                        dve.wait_ge(full, i * USES + US + 1)
                        dve.memset(nmx[:, 0:1], 0.0).then_inc(nmx_clear, 1)
                    half = lambda t: t.rearrange("p (a j) -> p a j", a=2)
                    nc.vector.tensor_tensor_reduce(out=half(s_sb[:, h % NS, :]), in0=keys(u, R), in1=half(mb[:]),
                                                   scale=1.0, scalar=-FLT_MAX, op0=ALU.add, op1=ALU.max,
                                                   accum_out=mx[:, h:h + 1]).then_inc(free[u % 2], 1)
                    dve.wait_ge(free[u % 2], i * PER + count(u))
                    dve.tensor_scalar(nmx[:, h:h + 1], mx[:, h:h + 1], -1.0, None, ALU.mult).then_inc(nmx_made, 1)

                def lo_of_output(m):
                    dve.wait_ge(o_hi, i * KC + m + 1)
                    dve.tensor_tensor(oT[1][:, m, :], ob[m % 2][:, 0:T], oT[0][:, m, :].bitcast(F32), ALU.subtract).then_inc(o_lo, 1)

                masked(0)
                for h in range(NH):
                    dve.wait_ge(e_made, i * NH + h + 1)
                    if h + 1 < NH:
                        dve.wait_ge(full, i * USES + US + h + 2)
                        if h + 1 >= NS:
                            dve.wait_ge(pt_full, i * (2 * NH) + 2 * (h + 2 - NS))
                    dve.reciprocal(rec[:, h:h + 1], den[:, h:h + 1]).then_inc(rec_made, 1)
                    if h + 1 < NH:
                        masked(h + 1)
                    dve.wait_ge(pt_full, i * (2 * NH) + 2 * h + 2)
                    if h % 4 == 0:
                        dve.wait_ge(pv_full, i * KC + h // 4)
                    dve.tensor_copy(pT[:, (h // 2) % 2, 3:6, (h % 2) * R:(h % 2) * R + R],
                                    pt[1][0:JB, 0:3 * R].rearrange("p (k t) -> p k t", k=3)).then_inc(pt_read[1], 1)
                    if h % 4 == 1 and h > 1:
                        lo_of_output(h // 4 - 1)
                lo_of_output(KC - 1)
                dve.wait_ge(x1b_made, turn)
                dve.wait_ge(full, i * USES + UO + 1)
                dve.tensor_tensor(x1[:], x1[:], bank[UO % 2][0:R], ALU.add).then_inc(free[UO % 2], 1)
                dve.wait_ge(free[UO % 2], i * PER + count(UO))
                for j in range(2):
                    ins = dve.bn_stats(stats[:, j, :], x1[:, j, :])
                ins.then_inc(stats_made, 1)
                dve.wait_ge(small_loaded, 48)
                dve.wait_ge(stats_made, turn)
                for j in range(2):
                    dve.bn_aggr(mv[:, j, :], stats[:, j, :]).then_inc(mv_made, 1)
                dve.wait_ge(root_made, turn)
                dve.tensor_tensor(nt[:, 0, :], rstd[:], rstd[:], ALU.mult).then_inc(newton, 1)
                dve.wait_ge(newton, i * 3 + 1)
                dve.scalar_tensor_tensor(nt[:, 1, :], mv[:, :, 1], LN_EPS, nt[:, 0, :], ALU.add, ALU.mult).then_inc(newton, 1)
                dve.wait_ge(newton, i * 3 + 2)
                dve.tensor_scalar(nt[:, 0, :], nt[:, 1, :], -0.5, 1.5, ALU.mult, ALU.add).then_inc(newton, 1)
                dve.wait_ge(newton, i * 3 + 3)
                dve.tensor_tensor(rstd[:], rstd[:], nt[:, 0, :], ALU.mult).then_inc(rstd_made, 1)
                dve.wait_ge(rstd_made, turn)
                dve.wait_ge(xn_stored, i * 16)
                for j in range(2):
                    dve.tensor_scalar(xn[:, j, :], x1[:, j, :], mv[:, j, 0:1], rstd[:, j:j + 1], ALU.subtract, ALU.mult).then_inc(xn_made, 1)

                steps = [0]

                def then(ins):
                    steps[0] += 1
                    ins.then_inc(route, 1)
                    dve.wait_ge(route, i * ROUTE + steps[0])

                def over(t, shape):
                    return t.broadcast_to(shape)

                L = bank[UR % 2][0:R, 0, 0:2 * E].rearrange("p (j e) -> p j e", j=2)
                dve.wait_ge(full, i * USES + UR + 1)
                then(dve.tensor_reduce(lmx[:], L, AX.X, ALU.max))
                dve.tensor_tensor(lg[:], L, over(lmx[:, :, None], L2), ALU.subtract).then_inc(lg_made, 1)
                dve.wait_ge(le_made, turn)
                then(dve.tensor_reduce(lsum[:], lg[:], AX.X, ALU.add))
                then(dve.reciprocal(lrec[:], lsum[:]))
                then(dve.tensor_tensor(sc[:], lg[:], over(lrec[:, :, None], L2), ALU.mult))
                L4 = [R, 2, E, E]
                other, own = over(sc[:, :, None, :], L4), over(sc[:, :, :, None], L4)
                dve.tensor_tensor(ge[:], other, own, ALU.is_equal).then_inc(route, 1)
                steps[0] += 1
                then(dve.tensor_tensor(gt[:], other, own, ALU.is_gt))
                then(dve.tensor_tensor(ge[:], ge[:], over(lower[:, None], L4), ALU.mult))
                then(dve.tensor_tensor(gt[:], gt[:], ge[:], ALU.add))
                then(dve.tensor_reduce(rank[:], gt[:], AX.X, ALU.add))
                then(dve.tensor_scalar(sel[:], rank[:], 2.0, None, ALU.is_lt))
                dve.tensor_copy(selb[:], sel[:]).then_inc(sel_made, 1)
                dve.wait_ge(pre_full, turn)
                pre = bank[UR % 2][0:R, 1, 0:3 * E].rearrange("p (j e) -> p j e", j=3)
                then(dve.tensor_tensor(off[:], pre[:, 0:2], base[:], ALU.add))
                dve.tensor_tensor(base[:], base[:], over(pre[:, 2:3], L2), ALU.add).then_inc(free[UR % 2], 1)
                then(dve.tensor_scalar(inv[:], off[:], float(CAP), float(2 * E * CAP), ALU.is_ge, ALU.mult))
                then(dve.tensor_tensor(off[:], off[:], over(e896[:, None], L2), ALU.add))
                then(dve.tensor_tensor(off[:], off[:], inv[:], ALU.add))
                K4 = [R, 2, 2, E]
                then(dve.tensor_tensor(oh[:], over(rank[:, :, None, :], K4), over(kk[:, None], K4), ALU.is_equal))
                then(dve.tensor_tensor(ohs[:], oh[:], over(off[:, :, None, :], K4), ALU.mult))
                then(dve.tensor_reduce(slotf[:].rearrange("p (j k) -> p j k", j=2), ohs[:], AX.X, ALU.add))
                then(dve.tensor_tensor(ohs[:], oh[:], over(sc[:, :, None, :], K4), ALU.mult))
                then(dve.tensor_tensor(tok[:], tok[:], tstep[:], ALU.add))
                dve.wait_ge(sent, i * 64)
                then(dve.tensor_reduce(pay[:, :, 1].rearrange("p (j k) -> p j k", j=2), ohs[:], AX.X, ALU.add))
                then(dve.tensor_copy(pay[:, :, 0].bitcast(I32), tok[:]))
                assert steps[0] == ROUTE, steps
                dve.tensor_copy(slotu[:], slotf[:]).then_inc(slots_made, 1)

        @block.scalar
        def _(act):
            act.wait_ge(zeroed, 2)
            act.wait_ge(const_set, 12)
            with act.Fori(0, B) as i:
                act.wait_ge(c_loaded, i * 16 + 16)
                for k in range(CC):
                    act.copy(cT[0][:, k, :], craw[:, k, :]).then_inc(c_hi, 1)
                act.wait_ge(q_loaded, i * 16 + 16)
                act.wait_ge(pv_full, i * KC)
                for e in range(2):
                    act.copy(qz[0][64 * e:64 * e + 64, e::2, :], q2[64 * e:64 * e + 64]).then_inc(qz_hi, 1)
                for m in range(KC):
                    u = UK + m
                    act.wait_ge(full, i * USES + u + 1)
                    act.copy(kT[0][:, m, :].rearrange("p (a j) -> p a j", a=2), keys(u, 128)).then_inc(k_hi, 1)
                for m in range(NJ // 2):
                    u = UV + m
                    act.wait_ge(full, i * USES + u + 1)
                    act.copy(v[:, 2 * m:2 * m + 2, :], bank[u % 2][0:JB]).then_inc(free[u % 2], 1)

                def exponential(h):
                    act.wait_ge(nmx_made, i * NH + h + 1)
                    act.activation(s_sb[:, h % NS, :], s_sb[:, h % NS, :], ACT.Exp, bias=nmx[:, h:h + 1],
                                   accum_out=den[:, h:h + 1]).then_inc(e_made, 1)

                def hi_of_output(m):
                    act.wait_ge(pv_full, i * KC + m + 1)
                    act.copy(oT[0][:, m, :], ob[m % 2][:, 0:T]).then_inc(o_hi, 1)

                exponential(0)
                for h in range(NH):
                    if h + 1 < NH:
                        exponential(h + 1)
                    act.wait_ge(pt_full, i * (2 * NH) + 2 * h + 1)
                    if h % 4 == 0:
                        act.wait_ge(pv_full, i * KC + h // 4)
                    act.copy(pT[:, (h // 2) % 2, 0:3, (h % 2) * R:(h % 2) * R + R],
                             pt[0][0:JB, 0:3 * R].rearrange("p (k t) -> p k t", k=3)).then_inc(pt_read[0], 1)
                    if h % 4 == 1 and h > 1:
                        hi_of_output(h // 4 - 1)
                hi_of_output(KC - 1)
                act.wait_ge(mv_made, i * 2 + 2)
                act.activation(rstd[:], mv[:, :, 1], ACT.Abs_reciprocal_sqrt, bias=eps[:]).then_inc(root_made, 1)
                act.wait_ge(full, i * USES + UT + 1)
                act.copy(xnT[:], bank[UT % 2][:, :, 0:KC * R]).then_inc(free[UT % 2], 1)
                act.wait_ge(lg_made, i + 1)
                act.activation(lg[:], lg[:], ACT.Exp).then_inc(le_made, 1)

        @block.tensor
        def _(pe):
            def product(out, lhs, rhs, n):
                steps = [(a, b, k) for a, b in ((0, 0), (0, 1), (1, 0)) for k in range(n)]
                for q, (a, b, k) in enumerate(steps):
                    mm = pe.matmul(out, lhs(a, k), rhs(b, k), start=q == 0, stop=q == len(steps) - 1)
                return mm

            pe.wait_ge(w_lo, len(pieces))
            pe.wait_ge(const_ready, 3)
            pe.wait_ge(const_set, 12)
            pe.wait_ge(small_loaded, 48)
            with pe.Fori(0, B) as i:
                def bank_free(u):
                    pe.wait_ge(free[u % 2], i * PER + u // 2)

                pe.wait_ge(c_lo, i * CC + CC)
                for m in range(KC):
                    u = UK + m
                    bank_free(u)
                    for a in range(2):
                        mm = product(bank[u % 2][:, a, 0:HW], lambda x, k: wk[x][:, k, 128 * m:128 * m + 128],
                                     lambda y, k: cT[y][:, k, a * (J - HW):a * (J - HW) + HW], CC)
                    mm.then_inc(full, 1)
                for m in range(NJ // 2):
                    u = UV + m
                    bank_free(u)
                    for a in range(2):
                        j = 2 * m + a
                        mm = product(bank[u % 2][0:JB, a, :], lambda x, k: cT[x][:, k, JB * j:JB * j + JB],
                                     lambda y, k: wv[y][:, k, :], CC)
                    mm.then_inc(full, 1)

                def scores(h):
                    u, head, t0 = US + h, h // 2, (h % 2) * R
                    bank_free(u)
                    if h == 0:
                        pe.wait_ge(qz_lo, i * 2 + 2)
                        pe.wait_ge(free[0], i * PER + 2)
                        pe.wait_ge(free[1], i * PER + 2)
                    for a in range(2):
                        mm = product(bank[u % 2][0:R, a, 0:HW], lambda x, k: qz[x][:, head, t0:t0 + R],
                                     lambda y, k: kT[y][:, head // 2, a * (J - HW):a * (J - HW) + HW], 1)
                    mm.then_inc(full, 1)

                def transposes(h):
                    pe.wait_ge(p_made, i * NH + h + 1)
                    for x in range(2):
                        pe.wait_ge(pt_read[x], i * NH + h)
                        for k in range(3):
                            j = 3 * x + k
                            mm = pe.transpose(pt[x][0:JB, R * k:R * k + R], s_sb[:, h % NS, JB * j:JB * j + JB], ident[:])
                        mm.then_inc(pt_full, 1)

                def values(m):
                    for x in range(2):
                        pe.wait_ge(pt_read[x], i * NH + 4 * m + 4)
                    pe.wait_ge(o_lo, i * KC + max(m - 1, 0))
                    for j in range(NJ):
                        for e in range(2):
                            head = 2 * m + e
                            mm = pe.matmul(ob[m % 2][64 * e:64 * e + 64, 0:T], v[:, j, 64 * head:64 * head + 64], pT[:, e, j, :],
                                           start=j == 0, stop=j == NJ - 1, tile_position=(0, 64 * e))
                    mm.then_inc(pv_full, 1)

                scores(0)
                scores(1)
                for h in range(NH):
                    transposes(h)
                    if h + 2 < NH:
                        scores(h + 2)
                    if h % 4 == 0 and h > 0:
                        values(h // 4 - 1)
                values(KC - 1)
                bank_free(UO)
                pe.wait_ge(o_lo, i * KC + KC)
                for j in range(2):
                    mm = product(bank[UO % 2][0:R, j, :], lambda x, k: oT[x][:, k, R * j:R * j + R], lambda y, k: wo[y][:, k, :], KC)
                mm.then_inc(full, 1)
                bank_free(UT)
                pe.wait_ge(xn_made, i * 2 + 2)
                for j in range(2):
                    for k in range(KC):
                        mm = pe.transpose(bank[UT % 2][:, j, R * k:R * k + R], xn[:, j, 128 * k:128 * k + 128], ident[:])
                mm.then_inc(full, 1)
                bank_free(UR)
                pe.wait_ge(free[UT % 2], i * PER + count(UT))
                for j in range(2):
                    for k in range(KC):
                        mm = pe.matmul(bank[UR % 2][0:R, 0, E * j:E * j + E], xnT[:, j, R * k:R * k + R], wr[:, k, :],
                                       start=k == 0, stop=k == KC - 1)
                mm.then_inc(full, 1)
                pe.wait_ge(sel_made, i + 1)
                pre = bank[UR % 2][0:R, 1]
                pe.matmul(pre[:, 0:E], before[:], selb[:, 0, :], start=True, stop=True)
                pe.matmul(pre[:, E:2 * E], before[:], selb[:, 1, :], start=True, stop=False)
                pe.matmul(pre[:, E:2 * E], onesb[:], selb[:, 0, :], start=False, stop=True)
                pe.matmul(pre[:, 2 * E:3 * E], onesb[:], selb[:, 0, :], start=True, stop=False)
                pe.matmul(pre[:, 2 * E:3 * E], onesb[:], selb[:, 1, :], start=False, stop=True).then_inc(pre_full, 1)


def experts(nc, w1, w2, xn_dram, table_dram, out):
    FB = F // 128
    NT = CAP // 128
    HC = CAP // 2
    NW = E * FB
    PAIRS = E // 2
    NSLOT = 4
    w2_v = w2.rearrange("(g b p) c -> g p b c", b=2, p=128)
    tab_v = table_dram.rearrange("(e t p) w -> e p t w", e=E, p=128)
    with ExitStack() as ctx:
        sb = lambda n, s, d=F32: ctx.enter_context(nc.sbuf_tensor("f_" + n, s, d))
        sem = lambda n: ctx.enter_context(nc.semaphore("f_" + n))
        ident = sb("ident", [128, 128])
        raw1 = sb("raw1", [128, 2, 2, C])
        raw2 = sb("raw2", [128, 2, 2, C])
        w1s = [sb(f"w1{k}", [128, NSLOT, KC, 128], F32R) for k in "hl"]
        w2s = [sb(f"w2{k}", [128, NSLOT, C], F32R) for k in "hl"]
        meta = sb("meta", [128, 2, NT, 2])
        xg = sb("xg", [128, NT, C])
        xT = [[sb(f"xT{k}{p}", [128, KC, CAP], F32R) for k in "hl"] for p in range(2)]
        hf = sb("hf", [128, 2, HC])
        hs = [sb(f"h{k}", [128, 2, CAP], F32R) for k in "hl"]
        ys = sb("ys", [128, NT, C])
        Y = [ctx.enter_context(nc.psum_tensor(f"f_y{k}", [128, 512], F32)) for k in range(NT)]
        H = ctx.enter_context(nc.psum_tensor("f_h", [128, 512], F32))

        const_set, const_ready = sem("const_set"), sem("const_ready")
        loaded = [sem("loaded0"), sem("loaded1")]
        w_hi, w_lo = sem("w_hi"), sem("w_lo")
        meta_loaded, gathered, scattered = sem("meta_loaded"), sem("gathered"), sem("scattered")
        full, free = sem("full"), sem("free")
        x_hi = sem("x_hi")
        h_hi, h_lo = sem("h_hi"), sem("h_lo")
        y_done, yt_done, ys_made = sem("y_done"), sem("yt_done"), sem("ys_made")

        FIRST_T = 5
        order = []
        for j in range(FB):
            order.append(("h", 2 * j))
            if FIRST_T <= j < FIRST_T + NT:
                order.append(("t", j - FIRST_T))
            order.append(("h", 2 * j + 1))
        use = {key: n for n, key in enumerate(order)}
        USES = len(order)
        GATHER_J = 3
        BL = 2 * FB

        block = ctx.enter_context(nc.Block())

        @block.sync
        def _(sp):
            sp.dma_start(meta[:, 0], tab_v[0]).then_inc(meta_loaded, 16)

            def load(g, a, b):
                sp.dma_start(raw1[:, g % 2].rearrange("p b c -> p (b c)"), a).then_inc(loaded[g % 2], 16)
                sp.dma_start(raw2[:, g % 2], b).then_inc(loaded[g % 2], 16)

            for g in range(2):
                load(g, w1[g], w2_v[g])
            with sp.Fori(0, PAIRS) as it:
                for g in range(FB):
                    if g % (FB // 2) == 1:
                        p = g // (FB // 2)
                        nxt = sp.snap((it * 2 + p + 1) % E)
                        sp.wait_ge(const_ready, 1)
                        sp.wait_ge(scattered, (it * 2 + p) * (16 * NT))
                        sp.dma_start(meta[:, (p + 1) % 2], tab_v[bass.ds(nxt, 1)].rearrange("a p t w -> (a p) t w")).then_inc(meta_loaded, 16)
                    src = sp.snap((it * FB + g + 2) % (NW // 2))
                    sp.wait_ge(const_ready, 1)
                    sp.wait_ge(w_lo, it * (4 * FB) + 4 * g + 4)
                    load(g + 2, w1[bass.ds(src, 1)].rearrange("a p n -> (a p) n"), w2_v[bass.ds(src, 1)].rearrange("a p b c -> (a p) b c"))
            sp.wait_ge(scattered, E * 16 * NT)
            for g in range(2):
                sp.wait_ge(loaded[g], 32 * (NW // 4 + 1))
            sp.wait_ge(meta_loaded, 16 * (E + 1))
            sp.wait_ge(gathered, 16 * NT * (E + 1))

        @block.gpsimd
        def _(pool):
            pool.memset(ident[:], 1.0).then_inc(const_set, 1)
            pool.wait_ge(const_set, 1)
            pool.affine_select(out=ident[:], in_=ident[:], pattern=[[1, 128]], compare_op=ALU.is_equal, fill=0.0,
                               base=0, channel_multiplier=-1).then_inc(const_ready, 1)

            def gather(p):
                for t in range(NT):
                    pool.indirect_dma_start(out=xg[:, t, :], out_offset=None, in_=xn_dram,
                                            in_offset=bass.IndirectOffsetOnAxis(ap=meta[:, p, t, 0:1].bitcast(U32), axis=0)).then_inc(gathered, 16)

            def scatter(p):
                for t in range(NT):
                    pool.indirect_dma_start(out=out, out_offset=bass.IndirectOffsetOnAxis(ap=meta[:, p, t, 0:1].bitcast(U32), axis=0),
                                            in_=ys[:, t, :], in_offset=None, compute_op=ALU.add).then_inc(scattered, 16)

            def split(n, w, base):
                g = n // 2
                pool.wait_ge(w_hi, base + 2 * n + 1)
                pool.tensor_tensor(w1s[1][:, n % NSLOT].rearrange("p k c -> p (k c)"), raw1[:, g % 2, n % 2, :],
                                   w1s[0][:, n % NSLOT].rearrange("p k c -> p (k c)").bitcast(F32), ALU.subtract).then_inc(w_lo, 1)
                for s, val in w:
                    pool.wait_ge(s, val)
                pool.wait_ge(w_hi, base + 2 * n + 2)
                pool.tensor_tensor(w2s[1][:, n % NSLOT], raw2[:, g % 2, n % 2, :], w2s[0][:, n % NSLOT].bitcast(F32),
                                   ALU.subtract).then_inc(w_lo, 1)

            pool.wait_ge(meta_loaded, 16)
            gather(0)
            for n in range(2):
                split(n, (), 0)

            with pool.Fori(0, PAIRS) as it:
                for l in range(BL):
                    p, j = divmod(l, FB)
                    w = ()
                    if j == GATHER_J:
                        w = ((meta_loaded, it * 32 + 16 * p + 32), (free, it * (2 * USES) + p * USES + NT))
                    if j == FB - 1:
                        w = ((ys_made, it * (2 * NT) + NT * (p + 1)), (scattered, (it * 2 + p) * (16 * NT)))
                    split(l + 2, w, it * (2 * BL))
                    if j == GATHER_J:
                        gather((p + 1) % 2)
                    if j == FB - 1:
                        scatter(p)

        @block.vector
        def _(dve):
            def split(n, it):
                g = n // 2
                dve.wait_ge(loaded[g % 2], it * (16 * FB) + 32 * (g // 2) + 32)
                dve.tensor_copy(w1s[0][:, n % NSLOT].rearrange("p k c -> p (k c)"), raw1[:, g % 2, n % 2, :]).then_inc(w_hi, 1)
                dve.tensor_copy(w2s[0][:, n % NSLOT], raw2[:, g % 2, n % 2, :]).then_inc(w_hi, 1)

            def rows_lo(p, t, count):
                dve.wait_ge(x_hi, count)
                dve.tensor_tensor(xT[p][1][:, :, 128 * t:128 * t + 128], H[:].rearrange("p (k s) -> p k s", k=KC),
                                  xT[p][0][:, :, 128 * t:128 * t + 128].bitcast(F32), ALU.subtract).then_inc(free, 1)

            for n in range(2):
                split(n, 0)
            for t in range(NT):
                rows_lo(0, t, t + 1)
            with dve.Fori(0, PAIRS) as it:
                for l in range(BL):
                    p, j = divmod(l, FB)
                    for c in range(2):
                        dve.wait_ge(free, it * (2 * USES) + p * USES + NT + use["h", 2 * j + c] + 1)
                        dve.wait_ge(y_done, it * BL + max(l - 1, 0))
                        dve.tensor_copy(hs[0][:, l % 2, c * HC:c * HC + HC], hf[:, c, :]).then_inc(h_hi, 1)
                        dve.wait_ge(h_hi, it * (2 * BL) + 2 * l + c + 1)
                        dve.tensor_tensor(hs[1][:, l % 2, c * HC:c * HC + HC], hf[:, c, :],
                                          hs[0][:, l % 2, c * HC:c * HC + HC].bitcast(F32), ALU.subtract).then_inc(h_lo, 1)
                        t = j - FIRST_T
                        if c == 0 and 0 <= t < NT:
                            rows_lo((p + 1) % 2, t, it * (2 * NT) + p * NT + NT + t + 1)
                    split(l + 2, it)

        @block.scalar
        def _(act):
            def rows_hi(p, t, count):
                act.wait_ge(full, count)
                act.copy(xT[p][0][:, :, 128 * t:128 * t + 128], H[:].rearrange("p (k s) -> p k s", k=KC)).then_inc(x_hi, 1)

            for t in range(NT):
                rows_hi(0, t, t + 1)
            with act.Fori(0, PAIRS) as it:
                for l in range(BL):
                    p, j = divmod(l, FB)
                    for c in range(2):
                        base = it * (2 * USES) + p * USES + NT
                        act.wait_ge(full, base + use["h", 2 * j + c] + 1)
                        act.wait_ge(h_lo, it * (2 * BL) + max(2 * l + c - 1, 0))
                        act.activation(hf[:, c, :], H[:, 0:HC], ACT.Gelu_apprx_tanh).then_inc(free, 1)
                        t = j - FIRST_T
                        if c == 0 and 0 <= t < NT:
                            rows_hi((p + 1) % 2, t, base + use["t", t] + 1)
                    if j == FB - 1:
                        act.wait_ge(scattered, (it * 2 + p) * (16 * NT))
                        for t in range(NT):
                            act.wait_ge(yt_done, it * (2 * NT) + p * NT + t + 1)
                            act.activation(ys[:, t, :], Y[t][:], ACT.Copy, scale=meta[:, p, t, 1:2]).then_inc(ys_made, 1)

        @block.tensor
        def _(pe):
            THREE = ((0, 0), (0, 1), (1, 0))

            def rows(t):
                for k in range(KC):
                    mm = pe.transpose(H[:, 128 * k:128 * k + 128], xg[:, t, 128 * k:128 * k + 128], ident[:])
                mm.then_inc(full, 1)

            pe.wait_ge(const_ready, 1)
            pe.wait_ge(gathered, 16 * NT)
            for t in range(NT):
                if t:
                    pe.wait_ge(free, t)
                rows(t)
            with pe.Fori(0, PAIRS) as it:
                for l in range(BL):
                    p, j = divmod(l, FB)
                    base = it * (2 * USES) + p * USES + NT

                    def hidden(c):
                        pe.wait_ge(free, base + use["h", 2 * j + c])
                        if c == 0:
                            pe.wait_ge(w_lo, it * (2 * BL) + 2 * l + 1)
                        for q, (a, b) in enumerate(THREE):
                            for k in range(KC):
                                mm = pe.matmul(H[:, 0:HC], w1s[a][:, l % NSLOT, k, :], xT[p][b][:, k, c * HC:c * HC + HC],
                                               start=q + k == 0, stop=(q, k) == (2, KC - 1))
                        mm.then_inc(full, 1)

                    def outputs(l, tiles):
                        p, j = divmod(l, FB)
                        for t in tiles:
                            if t == 0:
                                pe.wait_ge(w_lo, it * (2 * BL) + 2 * l + 2)
                                pe.wait_ge(h_lo, it * (2 * BL) + 2 * l + (2 if j < FB - 1 else 1))
                                if j == 0:
                                    pe.wait_ge(ys_made, it * (2 * NT) + p * NT)
                            if j == FB - 1 and t == 3:
                                pe.wait_ge(h_lo, it * (2 * BL) + 2 * l + 2)
                            for q, (a, b) in enumerate(THREE):
                                mm = pe.matmul(Y[t][:], hs[a][:, l % 2, 128 * t:128 * t + 128], w2s[b][:, l % NSLOT, :],
                                               start=j == 0 and q == 0, stop=j == FB - 1 and q == 2)
                            if j == FB - 1:
                                mm.then_inc(yt_done, 1)
                        if NT - 1 in tiles:
                            if j == FB - 1:
                                pe.wait_ge(yt_done, it * (2 * NT) + p * NT + NT)
                                pe.sem_inc(y_done, 1)
                            else:
                                mm.then_inc(y_done, 1)

                    hidden(0)
                    if j > 0:
                        outputs(l - 1, (0, 1))
                    t = j - FIRST_T
                    if 0 <= t < NT:
                        if t == 0:
                            pe.wait_ge(gathered, it * (2 * 16 * NT) + (p + 2) * (16 * NT))
                        pe.wait_ge(free, base + use["t", t])
                        rows(t)
                    if j > 0:
                        outputs(l - 1, (2, 3))
                    hidden(1)
                    if j > 0:
                        outputs(l - 1, (4, 5, 6))
                    if j == FB - 1:
                        outputs(l, range(NT))


def decoder_block(nc, x, w_qkvT, w_outT, slopes, w_qT, w_k, w_v, w_o, b_o, ctxT, mask, w_r, w1, w2, bias, out):
    scratch = lambda name, shape: nc.dram_tensor(name, shape, F32, kind="Internal").ap()
    x1_dram = scratch("x1_dram", [B * T, C])
    q2_dram = scratch("q2_dram", [B, 128, KC, T])
    xn_dram = scratch("xn_dram", [B * T + CAP, C])
    table_dram = scratch("table_dram", [E * CAP, 2])
    self_attention(nc, x, w_qkvT, w_outT, w_qT, slopes, x1_dram, q2_dram)
    cross_attention(nc, ctxT, mask, q2_dram, x1_dram, w_k, w_v, w_o, b_o, w_r, bias, out, xn_dram, table_dram)
    experts(nc, w1, w2, xn_dram, table_dram, out)


def kernel(**inputs):
    import numpy as _np
    import concourse.bacc as _bacc
    from concourse import mybir as _mybir
    from concourse.bass_utils import run_bass_kernel_spmd as _run

    def rows_on_partitions(w):
        return w.reshape(-1, 128, w.shape[1]).transpose(1, 0, 2)

    g = {name: _np.asarray(a) for name, a in inputs.items()}
    laid = {
        "x": g["x"].reshape(B * T, C),
        "w_qkvT": rows_on_partitions(g["L0_attn_w_qkv"].T),
        "w_outT": rows_on_partitions(g["L0_attn_w_out"].T),
        "slopes": g["L0_attn_alibi_slopes"],
        "w_qT": rows_on_partitions(g["L0_xattn_W_q"]),
        "w_k": rows_on_partitions(g["L0_xattn_W_k"]),
        "w_v": rows_on_partitions(g["L0_xattn_W_v"]),
        "w_o": rows_on_partitions(g["L0_xattn_W_o"]),
        "b_o": g["L0_xattn_b_o"],
        "ctxT": g["ctx_768"].transpose(0, 2, 1).reshape(B, CC, 128, J).transpose(0, 2, 1, 3),
        "mask": g["mask_BxS2_bk0"].reshape(-1).view(_np.int32),
        "w_r": rows_on_partitions(g["L0_ffn_w_router"]),
        "w1": g["L0_ffn_w1"].reshape(E, KC, 128, F // 256, 2, 128).transpose(0, 3, 2, 4, 1, 5).reshape(E * F // 256, 128, 2 * C),
        "w2": g["L0_ffn_w2"].reshape(E * F, C),
        "bias": g["L0_ffn_bias"].reshape(C),
    }
    nc = _bacc.Bacc("TRN2", target_bir_lowering=False, num_devices=1)
    arrays, args = {}, []
    for name, a in laid.items():
        a = _np.ascontiguousarray(a)
        arrays[f"in_{name}"] = a
        args.append(nc.dram_tensor(f"in_{name}", a.shape, _mybir.dt.from_np(a.dtype), kind="ExternalInput").ap())
    args.append(nc.dram_tensor("out_x", (B * T + CAP, C), F32, kind="ExternalOutput").ap())
    decoder_block(nc, *args)
    r = _run(nc, [arrays], core_ids=[0])
    return r.results[0]["out_x"][:B * T].reshape(B, T, C)
```

```python
from contextlib import ExitStack

import concourse.bass as bass
from concourse import mybir

F32, F32R, BF16 = mybir.dt.float32, mybir.dt.float32r, mybir.dt.bfloat16
I32, U32, U8 = mybir.dt.int32, mybir.dt.uint32, mybir.dt.uint8
ALU, ACT, AX = mybir.AluOpType, mybir.ActivationFunctionType, mybir.AxisListType

B, T, C = 16, 224, 512
KC = C // 128
R = T // 2
TPI = 4
TOK = TPI * R
H1, D1 = 16, 32
H2, D2 = 8, 64
LN_EPS, RS_EPS = 1e-5, 1e-6
FLT_MAX = 3.4028234663852886e38
J, CC, JB = 750, 3, 125
E, CAP, F = 8, 896, 2048




def self_attention(nc, x, w_qkvT, w_outT, w_qT, slopes, x1_dram, q2_dram):
    NIT = B * T // TOK
    x_v = x.rearrange("(i j r) c -> i r j c", j=TPI, r=R)
    x1_v = x1_dram.rearrange("(i j r) c -> i r j c", j=TPI, r=R)
    q2_v = q2_dram.rearrange("(i b) p k t -> i b p k t", b=2)
    NG = 8
    NPAIR = T + R
    with ExitStack() as ctx:
        sb = lambda n, s, d=F32: ctx.enter_context(nc.sbuf_tensor("a_" + n, s, d))
        sem = lambda n: ctx.enter_context(nc.semaphore("a_" + n))
        wqkv = [sb(f"wqkv{k}", [128, KC, 3 * C], F32R) for k in "hl"]
        wout = [sb(f"wout{k}", [128, KC, C], F32R) for k in "hl"]
        wq2 = [sb(f"wq2{k}", [128, KC, C], F32R) for k in "hl"]
        ident = sb("ident", [R, R])
        dist = sb("dist", [R, NPAIR])
        keep = sb("keep", [R, NPAIR])
        slope = sb("slope", [R, H1])
        ones = sb("ones", [R, 32])
        eps = sb("eps", [128, 3])
        x_in = sb("x_in", [R, TPI, C])
        xr = sb("xr", [R, TPI, C])
        work = sb("work", [128, TPI * C])
        xn = work[0:R, :].rearrange("p (j c) -> p j c", j=TPI)
        oT = work[:, 0:KC * TOK].rearrange("p (k t) -> p k t", k=KC)
        xT = [sb(f"xT{k}", [128, KC, TOK], F32R) for k in "hl"]
        stats = sb("stats", [R, TPI, 6])
        mv = sb("mv", [R, TPI, 2])
        rstd = sb("rstd", [R, TPI])
        nt = sb("nt", [R, 2, TPI])
        qz = sb("qz", [128, KC, 4, TOK])
        kT = sb("kT", [128, KC, TOK])
        v = sb("v", [R, TPI, C])
        s_sb = sb("s_sb", [R, 2, 4, NPAIR])
        r_sb = sb("r_sb", [R, 2, 4, NPAIR])
        u_sb = sb("u_sb", [R, 2, 4, NPAIR])
        num = u_sb
        q_sb = sb("q_sb", [R, 4, NPAIR])
        rden = sb("rden", [128, 2, T])
        dt = sb("dt", [128, 2, T])
        q2 = kT
        bank = [ctx.enter_context(nc.psum_tensor(f"a_bank{k}", [128, 512], F32)) for k in range(8)]
        gen, sc, pvb = bank[0:2], bank[2:6], bank[6:8]

        w_hi, w_lo = sem("w_hi"), sem("w_lo")
        w_loaded = [sem(f"w_loaded{k}") for k in range(4)]
        const_set, const_ready, zeroed, slope_loaded = sem("const_set"), sem("const_ready"), sem("zeroed"), sem("slope_loaded")
        x_loaded, xr_loaded, x1_stored, q2_stored = sem("x_loaded"), sem("xr_loaded"), sem("x1_stored"), sem("q2_stored")
        stats_made = [sem("stats_made0"), sem("stats_made1")]
        mv_made, root_made, rstd_made, xn_made = sem("mv_made"), sem("root_made"), sem("rstd_made"), sem("xn_made")
        newton = [sem(f"newton{k}") for k in range(3)]
        gen_full = sem("gen_full")
        gen_free = [sem("gen_free0"), sem("gen_free1")]
        xT_hi, xT_lo = sem("xT_hi"), sem("xT_lo")
        q_made, k_made, v_made = sem("q_made"), sem("k_made"), sem("v_made")
        qkv_done = sem("qkv_done")
        sc_full, s_made, u_made, r_made, p_made, num_made = (sem(n) for n in ("sc_full", "s_made", "u_made", "r_made", "p_made", "num_made"))
        rr_made, m_made, p2_made, y_made = sem("rr_made"), sem("m_made"), sem("p2_made"), sem("y_made")
        pv_full, rs_made, rden_made, o_made = sem("pv_full"), sem("rs_made"), sem("rden_made"), sem("o_made")
        x1_made, q2_made = sem("x1_made"), sem("q2_made")

        T1, QK, V, OUT, T2, Q2 = 0, 4, 12, 16, 20, 24
        USES = 28
        pieces = [(w_qkvT[:, k, :], wqkv, slice(k, k + 1), 3 * C) for k in range(KC)]
        pieces += [(w_outT[:, k, :], wout, slice(k, k + 1), C) for k in range(KC)]
        pieces += [(w_qT[:, k, :], wq2, slice(k, k + 1), C) for k in range(KC)]
        stage = qz[:, :, :, :].rearrange("p a b c -> p (a b c)")
        NST = 4

        block = ctx.enter_context(nc.Block())

        @block.sync
        def _(sp):
            sp.dma_start(slope[:], slopes.partition_broadcast(R)).then_inc(slope_loaded, 16)
            for n, (src, dst, ks, w) in enumerate(pieces):
                if n >= NST:
                    sp.wait_ge(w_lo, n - NST + 1)
                sp.dma_start(stage[:, (n % NST) * 3 * C:(n % NST) * 3 * C + w], src).then_inc(w_loaded[n % NST], 16)
                if n == 0:
                    sp.dma_start(x_in[:], x_v[0]).then_inc(x_loaded, 16)
                    sp.dma_start(xr[:], x_v[0]).then_inc(xr_loaded, 16)
            with sp.Fori(1, NIT) as i:
                sp.wait_ge(xn_made, i * (2 * TPI) - TPI)
                sp.dma_start(x_in[:], x_v[bass.ds(i, 1)].rearrange("a r j c -> (a r) j c")).then_inc(x_loaded, 16)
                sp.wait_ge(x_loaded, 16)
                sp.wait_ge(x1_made, i * TPI)
                sp.dma_start(x1_v[bass.ds(i - 1, 1)].rearrange("a r j c -> (a r) j c"), xr[:]).then_inc(x1_stored, 16)
                sp.wait_ge(q2_made, i * KC)
                for b in range(2):
                    sp.dma_start(q2_v[bass.ds(i - 1, 1), b].rearrange("a p k t -> (a p) k t"), q2[:, :, b * T:b * T + T]).then_inc(q2_stored, 16)
                sp.wait_ge(slope_loaded, 16)
                sp.wait_ge(x1_stored, i * 16)
                sp.wait_ge(slope_loaded, 16)
                sp.wait_ge(xn_made, i * (2 * TPI))
                sp.dma_start(xr[:], x_v[bass.ds(i, 1)].rearrange("a r j c -> (a r) j c")).then_inc(xr_loaded, 16)
            sp.wait_ge(x1_made, NIT * TPI)
            sp.dma_start(x1_v[NIT - 1], xr[:]).then_inc(x1_stored, 16)
            sp.wait_ge(q2_made, NIT * KC)
            for b in range(2):
                sp.dma_start(q2_v[NIT - 1, b], q2[:, :, b * T:b * T + T]).then_inc(q2_stored, 16)
            sp.wait_ge(x1_stored, NIT * 16)
            sp.wait_ge(q2_stored, NIT * 32)

        @block.gpsimd
        def _(pool):
            pool.iota(dist[:, 0:T], [[-1, T]], base=0, channel_multiplier=1, allow_small_or_imprecise_dtypes=True).then_inc(const_set, 1)
            pool.iota(dist[:, T:], [[-1, R]], base=0, channel_multiplier=1, allow_small_or_imprecise_dtypes=True).then_inc(const_set, 1)
            pool.memset(keep[:], -1.0).then_inc(const_set, 1)
            pool.memset(ident[:], 1.0).then_inc(const_set, 1)
            pool.memset(ones[:], 1.0).then_inc(const_set, 1)
            pool.memset(eps[:, 0:1], LN_EPS).then_inc(const_set, 1)
            pool.memset(eps[:, 1:2], 1.0).then_inc(const_set, 1)
            pool.memset(eps[:, 2:3], 4 * RS_EPS).then_inc(const_set, 1)
            pool.wait_ge(const_set, 8)
            for a, w in ((0, T), (T, R)):
                pool.affine_select(out=keep[:, a:a + w], in_=keep[:, a:a + w], pattern=[[1, w]], compare_op=ALU.is_ge,
                                   fill=0.0, base=0, channel_multiplier=-1).then_inc(const_ready, 1)
            pool.affine_select(out=ident[:], in_=ident[:], pattern=[[1, R]], compare_op=ALU.is_equal, fill=0.0,
                               base=0, channel_multiplier=-1).then_inc(const_ready, 1)
            with pool.Fori(0, NIT) as i:
                for n in range(NG):
                    pool.wait_ge(r_made, i * NG + n + 1)
                    pool.tensor_tensor(s_sb[:, n % 2], s_sb[:, n % 2], r_sb[:, n % 2], ALU.mult).then_inc(p_made, 1)

        CONSTS = 3

        def split_lo(eng, lo, src, hi, inc):
            eng.tensor_tensor(lo, src, hi.bitcast(F32), ALU.subtract).then_inc(inc, 1)

        @block.vector
        def _(dve):
            for n, (src, dst, ks, w) in enumerate(pieces):
                st = stage[:, (n % NST) * 3 * C:(n % NST) * 3 * C + w]
                dve.wait_ge(w_loaded[n % NST], 16 * (n // NST + 1))
                dve.tensor_copy(dst[0][:, ks.start, :], st).then_inc(w_hi, 1)
                dve.wait_ge(w_hi, n + 1)
                dve.tensor_tensor(dst[1][:, ks.start, :], st, dst[0][:, ks.start, :].bitcast(F32), ALU.subtract).then_inc(w_lo, 1)
            dve.wait_ge(w_lo, len(pieces))
            dve.memset(stage, 0.0).then_inc(zeroed, 1)

            def layernorm(i, turn, src, half):
                for j in range(TPI):
                    ins = dve.bn_stats(stats[:, j, :], src[:, j, :])
                ins.then_inc(stats_made[half], 1)
                dve.wait_ge(const_ready, CONSTS)
                dve.wait_ge(stats_made[half], turn)
                for j in range(TPI):
                    dve.bn_aggr(mv[:, j, :], stats[:, j, :]).then_inc(mv_made, 1)
                dve.wait_ge(root_made, i * 2 + half + 1)
                dve.tensor_tensor(nt[:, 0, :], rstd[:], rstd[:], ALU.mult).then_inc(newton[0], 1)
                dve.wait_ge(newton[0], i * 2 + half + 1)
                dve.scalar_tensor_tensor(nt[:, 1, :], mv[:, :, 1], LN_EPS, nt[:, 0, :], ALU.add, ALU.mult).then_inc(newton[1], 1)
                dve.wait_ge(newton[1], i * 2 + half + 1)
                dve.tensor_scalar(nt[:, 0, :], nt[:, 1, :], -0.5, 1.5, ALU.mult, ALU.add).then_inc(newton[2], 1)
                dve.wait_ge(newton[2], i * 2 + half + 1)
                dve.tensor_tensor(rstd[:], rstd[:], nt[:, 0, :], ALU.mult).then_inc(rstd_made, 1)
                for j in range(TPI):
                    if j == 0:
                        dve.wait_ge(gen_full, i * USES + (T1 if half == 0 else T2))
                        dve.wait_ge(rstd_made, i * 2 + half + 1)
                    dve.tensor_scalar(xn[:, j, :], src[:, j, :], mv[:, j, 0:1], rstd[:, j:j + 1], ALU.subtract, ALU.mult).then_inc(xn_made, 1)

            def transposed_lo(i, base, half):
                for c in range(KC):
                    dve.wait_ge(xT_hi, i * (3 * KC) + half * KC + c + 1)
                    dve.tensor_tensor(xT[1][:, c, :], gen[c % 2][:, 0:TOK], xT[0][:, c, :].bitcast(F32),
                                      ALU.subtract).then_inc(gen_free[c % 2], 1)

            dve.wait_ge(slope_loaded, 16)
            with dve.Fori(1, NIT + 1) as turn:
                i = turn - 1
                dve.wait_ge(x_loaded, i * 16 + 16)
                layernorm(i, turn, x_in, 0)
                transposed_lo(i, T1, 0)
                for m in range(KC):
                    u = QK + KC + m
                    dve.wait_ge(gen_full, i * USES + u + 1)
                    if m == 0:
                        dve.wait_ge(q2_stored, i * 32)
                    dve.tensor_copy(kT[:, m, :], gen[u % 2][:, 0:TOK]).then_inc(gen_free[u % 2], 1)

                def score(n):
                    b, g = divmod(n, 4)
                    if n == 0:
                        dve.wait_ge(num_made, i * NG)
                    elif n >= 2:
                        dve.wait_ge(num_made, i * NG + n - 1)
                    for r in range(4):
                        dve.wait_ge(sc_full, i * 32 + 4 * n + r + 1)
                        dve.scalar_tensor_tensor(s_sb[:, n % 2, r, :], dist[:], slope[:, 4 * g + r:4 * g + r + 1],
                                                 sc[r][0:R, 0:NPAIR], ALU.mult, ALU.add).then_inc(s_made, 1)

                def numerator(n):
                    dve.wait_ge(rr_made, i * NG + n + 1)
                    dve.scalar_tensor_tensor(u_sb[:, n % 2], u_sb[:, n % 2], 1.0, q_sb[:], ALU.add, ALU.mult).then_inc(m_made, 1)
                    dve.wait_ge(p_made, i * NG + n + 1)
                    dve.wait_ge(m_made, i * NG + n + 1)
                    dve.scalar_tensor_tensor(s_sb[:, n % 2], u_sb[:, n % 2], 3.0, s_sb[:, n % 2], ALU.subtract, ALU.mult).then_inc(p2_made, 1)
                    dve.wait_ge(p2_made, i * NG + n + 1)
                    dve.scalar_tensor_tensor(num[:, n % 2], s_sb[:, n % 2], 2.0,
                                             keep[:, None, :].broadcast_to([R, 4, NPAIR]), ALU.subtract, ALU.mult).then_inc(num_made, 1)

                def output(n):
                    b, g = divmod(n, 4)
                    dve.wait_ge(rden_made, i * NG + n + 1)
                    dve.wait_ge(o_made, i * NG + n)
                    dve.scalar_tensor_tensor(dt[:, 0, :], pvb[n % 2][:, T:2 * T], 4 * RS_EPS, rden[:, n % 2], ALU.add, ALU.mult).then_inc(y_made, 1)
                    dve.tensor_tensor(dt[:, 1, :], pvb[n % 2][:, 0:T], rden[:, n % 2], ALU.mult).then_inc(y_made, 1)
                    dve.wait_ge(y_made, i * (2 * NG) + 2 * n + 2)
                    dve.scalar_tensor_tensor(oT[:, g, b * T:(b + 1) * T], dt[:, 0, :], 2.0, dt[:, 1, :], ALU.subtract, ALU.mult).then_inc(o_made, 1)

                for n in range(NG + 2):
                    if n < NG:
                        score(n)
                    if 1 <= n <= NG:
                        numerator(n - 1)
                    if n >= 2:
                        output(n - 2)
                for c in range(KC):
                    dve.wait_ge(xT_hi, i * (3 * KC) + KC + c + 1)
                    dve.tensor_tensor(xT[1][:, c, :], oT[:, c, :], xT[0][:, c, :].bitcast(F32), ALU.subtract).then_inc(xT_lo, 1)
                for j in range(TPI):
                    u = OUT + j
                    if j == 0:
                        dve.wait_ge(xr_loaded, i * 16 + 16)
                    dve.wait_ge(gen_full, i * USES + u + 1)
                    dve.tensor_tensor(xr[:, j, :], xr[:, j, :], gen[u % 2][0:R, :], ALU.subtract).then_inc(x1_made, 1)
                dve.wait_ge(x1_made, i * TPI + TPI)
                layernorm(i, turn, xr, 1)
                transposed_lo(i, T2, 2)

        @block.scalar
        def _(act):
            act.wait_ge(const_ready, CONSTS)

            def rstd_of(i, half):
                act.wait_ge(mv_made, i * (2 * TPI) + half * TPI + TPI)
                act.activation(rstd[:], mv[:, :, 1], ACT.Abs_reciprocal_sqrt, bias=eps[0:R, 0:1]).then_inc(root_made, 1)

            def transposed_hi(i, base):
                for c in range(KC):
                    act.wait_ge(gen_full, i * USES + base + c + 1)
                    act.copy(xT[0][:, c, :], gen[c % 2][:, 0:TOK]).then_inc(xT_hi, 1)

            with act.Fori(0, NIT) as i:
                rstd_of(i, 0)
                transposed_hi(i, T1)
                act.wait_ge(zeroed, 1)
                for m in range(KC):
                    u = QK + m
                    act.wait_ge(gen_full, i * USES + u + 1)
                    for r in range(4):
                        ins = act.mul(qz[32 * r:32 * r + 32, m, r, :], gen[u % 2][32 * r:32 * r + 32, 0:TOK], D1 ** -0.5)
                        ins.then_inc(gen_free[u % 2] if r == 3 else q_made, 1)
                for j in range(TPI):
                    u = V + j
                    act.wait_ge(gen_full, i * USES + u + 1)
                    act.copy(v[:, j, :], gen[u % 2][0:R, :]).then_inc(gen_free[u % 2], 1)

                def root(n):
                    if n >= 2:
                        act.wait_ge(pv_full, i * NG + n - 1)
                    act.wait_ge(s_made, i * 32 + 4 * n + 4)
                    act.activation(u_sb[:, n % 2], s_sb[:, n % 2], ACT.Square).then_inc(u_made, 1)
                    act.wait_ge(u_made, i * NG + n + 1)
                    act.activation(r_sb[:, n % 2], u_sb[:, n % 2], ACT.Abs_reciprocal_sqrt, bias=eps[0:R, 1:2]).then_inc(r_made, 1)
                    act.wait_ge(r_made, i * NG + n + 1)
                    if n >= 1:
                        act.wait_ge(m_made, i * NG + n)
                    act.activation(q_sb[:], r_sb[:, n % 2], ACT.Square).then_inc(rr_made, 1)

                def reciprocal(n):
                    act.wait_ge(pv_full, i * NG + n + 1)
                    if n >= 2:
                        act.wait_ge(o_made, i * NG + n - 1)
                    act.activation(rden[:, n % 2], pvb[n % 2][:, T:2 * T], ACT.Abs_reciprocal_sqrt, bias=eps[:, 2:3]).then_inc(rs_made, 1)
                    act.wait_ge(rs_made, i * NG + n + 1)
                    act.activation(rden[:, n % 2], rden[:, n % 2], ACT.Square).then_inc(rden_made, 1)

                for n in range(NG + 2):
                    if n < NG:
                        root(n)
                    if n >= 2:
                        reciprocal(n - 2)
                for c in range(KC):
                    act.wait_ge(o_made, i * NG + 4 + c + 1)
                    act.copy(xT[0][:, c, :], oT[:, c, :]).then_inc(xT_hi, 1)
                rstd_of(i, 1)
                transposed_hi(i, T2)
                for m in range(KC):
                    u = Q2 + m
                    act.wait_ge(gen_full, i * USES + u + 1)
                    act.mul(q2[:, m, :], gen[u % 2][:, 0:TOK], D2 ** -0.5).then_inc(q2_made, 1)

        @block.tensor
        def _(pe):
            def bank_free(i, u):
                b, k = u % 2, u // 2
                if u < OUT:
                    if u // 2 == 0:
                        pe.wait_ge(q2_made, i * KC)
                    else:
                        pe.wait_ge(gen_free[b], i * GF + k)
                elif u < OUT + 2:
                    pe.wait_ge(gen_free[b], i * GF + 8)
                elif u < T2:
                    pe.wait_ge(x1_made, i * TPI + u - OUT - 1)
                elif u < T2 + 2:
                    pe.wait_ge(x1_made, i * TPI + u - OUT - 1)
                elif u < Q2 + 2:
                    pe.wait_ge(gen_free[b], i * GF + 8 + (u - T2) // 2)
                else:
                    pe.wait_ge(q2_made, i * KC + u - Q2 - 1)

            GF = 10

            def transposes(i, base, half):
                pe.wait_ge(xn_made, i * (2 * TPI) + half * TPI + TPI)
                for c in range(KC):
                    bank_free(i, base + c)
                    for j in range(TPI):
                        mm = pe.transpose(gen[c % 2][:, R * j:R * j + R], xn[:, j, 128 * c:128 * c + 128], ident[:])
                    mm.then_inc(gen_full, 1)

            def product(out, lhs, rhs, n=KC):
                steps = [(a, b, k) for a, b in ((0, 0), (0, 1), (1, 0)) for k in range(n)]
                for q, (a, b, k) in enumerate(steps):
                    mm = pe.matmul(out, lhs(a, k), rhs(b, k), start=q == 0, stop=q == len(steps) - 1)
                return mm

            pe.wait_ge(const_ready, CONSTS)
            pe.wait_ge(w_lo, len(pieces))
            with pe.Fori(0, NIT) as i:
                transposes(i, T1, 0)
                pe.wait_ge(gen_free[0], i * GF + 2)
                pe.wait_ge(gen_free[1], i * GF + 2)
                for m in range(8):
                    bank_free(i, QK + m)
                    product(gen[m % 2][:, 0:TOK], lambda a, k: wqkv[a][:, k, 128 * m:128 * m + 128],
                            lambda b, k: xT[b][:, k, :]).then_inc(gen_full, 1)
                for j in range(TPI):
                    bank_free(i, V + j)
                    product(gen[j % 2][0:R, :], lambda a, k: xT[a][:, k, R * j:R * j + R],
                            lambda b, k: wqkv[b][:, k, 2 * C:3 * C]).then_inc(gen_full, 1)

                def scores(n):
                    b, g = divmod(n, 4)
                    if n == 0:
                        for e in range(2):
                            pe.wait_ge(gen_free[e], i * GF + 8)
                    for r in range(4):
                        if n >= 1:
                            pe.wait_ge(s_made, i * 32 + 4 * (n - 1) + r + 1)
                        t0 = b * T
                        pe.matmul(sc[r][0:R, 0:T], kT[:, g, t0:t0 + R], qz[:, g, r, t0:t0 + T], start=True, stop=True)
                        pe.matmul(sc[r][0:R, T:NPAIR], kT[:, g, t0 + R:t0 + T], qz[:, g, r, t0 + R:t0 + T],
                                  start=True, stop=True).then_inc(sc_full, 1)

                def values(n):
                    b, g = divmod(n, 4)
                    pe.wait_ge(num_made, i * NG + n + 1)
                    if n >= 2:
                        pe.wait_ge(o_made, i * NG + n - 1)
                    for den in range(2):
                        for st in range(2):
                            for r in range(4):
                                h = 4 * g + r
                                lhs = ones[:] if den else v[:, 2 * b + st, 32 * h:32 * h + 32]
                                o0 = den * T
                                if st == 0:
                                    mm = pe.matmul(pvb[n % 2][32 * r:32 * r + 32, o0:o0 + T], lhs, num[:, n % 2, r, 0:T],
                                                   start=True, stop=False, tile_position=(0, 32 * r))
                                else:
                                    mm = pe.matmul(pvb[n % 2][32 * r:32 * r + 32, o0 + R:o0 + T], lhs,
                                                   num[:, n % 2, r, T:NPAIR], start=False, stop=True, tile_position=(0, 32 * r))
                    mm.then_inc(pv_full, 1)

                for n in range(NG + 1):
                    if n < NG:
                        scores(n)
                    if n >= 1:
                        values(n - 1)
                pe.wait_ge(xT_lo, i * KC + KC)
                for j in range(TPI):
                    bank_free(i, OUT + j)
                    product(gen[j % 2][0:R, :], lambda a, k: xT[a][:, k, R * j:R * j + R],
                            lambda b, k: wout[b][:, k, :]).then_inc(gen_full, 1)
                transposes(i, T2, 1)
                pe.wait_ge(gen_free[0], i * GF + 10)
                pe.wait_ge(gen_free[1], i * GF + 10)
                for m in range(KC):
                    bank_free(i, Q2 + m)
                    product(gen[m % 2][:, 0:TOK], lambda a, k: wq2[a][:, k, 128 * m:128 * m + 128],
                            lambda b, k: xT[b][:, k, :]).then_inc(gen_full, 1)


def cross_attention(nc, ctxT, mask, q2_dram, x1_dram, w_k, w_v, w_o, b_o, w_r, bias, out, xn_dram, table_dram):
    NJ = J // JB
    mask = mask.bitcast(U8).rearrange("(i j) -> i j", j=J)
    NH = 2 * H2
    NM = H2 // 2
    x1_v = x1_dram.rearrange("(i j r) c -> i r j c", j=2, r=R)
    out_v = out[0:B * T].rearrange("(i j r) c -> i r j c", j=2, r=R)
    xn_v = xn_dram[0:B * T].rearrange("(i j r) c -> i r j c", j=2, r=R)
    with ExitStack() as ctx:
        sb = lambda n, s, d=F32: ctx.enter_context(nc.sbuf_tensor("c_" + n, s, d))
        sem = lambda n: ctx.enter_context(nc.semaphore("c_" + n))
        wk = [sb(f"wk{k}", [128, CC, C], F32R) for k in "hl"]
        wv = [sb(f"wv{k}", [128, CC, C], F32R) for k in "hl"]
        wo = [sb(f"wo{k}", [128, KC, C], F32R) for k in "hl"]
        wr = sb("wr", [128, KC, E])
        bo, bi = sb("bo", [R, C]), sb("bi", [R, C])
        ident = sb("ident", [R, R])
        craw = sb("craw", [128, CC, J])
        cT = [sb(f"cT{k}", [128, CC, J], F32R) for k in "hl"]
        kT = [sb(f"kT{k}", [128, NM, J], F32R) for k in "hl"]
        v = [sb(f"v{k}", [JB, NJ, C], F32R) for k in "hl"]
        q2 = sb("q2", [128, KC, T])
        qz = [sb(f"qz{k}", [128, H2, T], F32R) for k in "hl"]
        m8 = sb("m8", [R, J], U8)
        mb = sb("mb", [R, J])
        s_sb = sb("s_sb", [R, 4, J])
        mx, nmx, den, rec = (sb(n, [R, NH]) for n in ("mx", "nmx", "den", "rec"))
        pT = [sb(f"pT{k}", [JB, 2, NJ, T], F32R) for k in "hl"]
        oT = [sb(f"oT{k}", [128, KC, T], F32R) for k in "hl"]
        x1 = sb("x1", [R, 2, C])
        xo = sb("xo", [R, 2, C])
        xn = sb("xn", [R, 2, C])
        xnT = sb("xnT", [128, 2, KC * R])
        stats, mv, rstd, nt = sb("stats", [R, 2, 6]), sb("mv", [R, 2, 2]), sb("rstd", [R, 2]), sb("nt", [R, 2, 2])
        eps = sb("eps", [R, 1])
        L2 = [R, 2, E]
        lg, sc, rank, sel, off, inv, base = (sb(n, L2) for n in ("lg", "sc", "rank", "sel", "off", "inv", "base"))
        selb = sb("selb", L2, BF16)
        lmx, lsum, lrec = (sb(n, [R, 2]) for n in ("lmx", "lsum", "lrec"))
        gt, ge = sb("gt", [R, 2, E, E]), sb("ge", [R, 2, E, E])
        lower = sb("lower", [R, E, E])
        before = sb("before", [R, R], BF16)
        onesb = sb("onesb", [R, R], BF16)
        e896 = sb("e896", [R, E])
        kk = sb("kk", [R, 2, E])
        oh, ohs = sb("oh", [R, 2, 2, E]), sb("ohs", [R, 2, 2, E])
        slotf, slotu = sb("slotf", [R, 4]), sb("slotu", [R, 4], U32)
        tok, tstep = sb("tok", [R, 4]), sb("tstep", [R, 4])
        pay = sb("pay", [R, 4, 2])
        trash = sb("trash", [128, E, CAP // 128, 2])
        zero = sb("zero", [128, C])

        ROUTE = 21

        psum = ctx.enter_context(nc.psum_tensor("c_psum", [128, 8, 512], F32))
        scb = [psum[:, 0:2], psum[:, 2:4]]
        ptb = psum[:, 4:6]
        ob, gen = psum[:, 6], psum[:, 7]
        JH = J // 2
        HW = JH + 1

        def score_view(h):
            flat = psum[0:R].rearrange("p b c -> p (b c)")
            return flat[:, 1024 * (h % 2):1024 * (h % 2) + 1026].rearrange("p (a j) -> p a j", a=2)[:, :, 0:JH]

        K, V = (lambda m, a: ("K", m, a)), (lambda g, a: ("V", g, a))
        PLAN = {2: ([V(1, 0)], [V(1, 1)], []), 3: ([], [V(1, 2)], [("OUT", 0, 0)]), 4: ([], [("OUT", 1, 0)], []),
                6: ([K(0, 0)], [("XT", 0, 0)], []), 7: ([], [K(0, 1)], [("XT", 1, 0)]), 8: ([K(1, 0)], [("RT", 0, 0)], []),
                9: ([], [K(1, 1)], []), 10: ([V(0, 0)], [("PRE", 0, 0)], []), 11: ([], [V(0, 1)], []),
                12: ([K(2, 0)], [V(0, 2)], []), 13: ([], [K(2, 1)], []), 14: ([], [K(3, 0)], []), 15: ([], [K(3, 1)], [])}
        START = [K(m, a) for m in range(NM) for a in range(2)] + [V(0, a) for a in range(3)]

        def units(kind, s, slots=(0, 1, 2)):
            def has(unit):
                projection, late = unit[0] in ("K", "V"), unit[:2] == ("V", 1)
                return {"first": projection, "mid": True, "last": late or not projection, "end": not projection}[kind]
            return [u for slot in slots for u in (PLAN[s][slot] if s in PLAN else []) if has(u)]

        ORDER = {k: [u for s in range(NH) for u in units(k, s)] for k in ("first", "mid", "last", "end")}
        ORDER["start"] = START
        SPLIT = {k: [u for u in us if u[0] in ("K", "V")] for k, us in ORDER.items()}

        def projections(kind, s, slot):
            return [u for u in units(kind, s, (slot,)) if u[0] in ("K", "V")]

        def number(lists, i, kind, unit):
            n, first, mid, last = (len(lists[k]) for k in ("start", "first", "mid", "last"))
            at = lists[kind].index(unit)
            if kind == "start":
                return at
            if kind == "first":
                return n + at
            if kind == "end":
                return n + first + (B - 2) * mid + last + at
            return i * mid + (n + first - mid + at)

        K0, KW = (0, HW), (HW, J - HW)

        def unit_places(unit):
            what, m, a = unit
            if what == "K":
                return lambda part: kT[part][:, m, K0[a]:K0[a] + KW[a]], gen[:, 0:KW[a]]
            if what == "V":
                return lambda part: v[part][:, 2 * a:2 * a + 2, 256 * m:256 * m + 256], gen[0:JB].rearrange("p (b c) -> p b c", b=2)

        def probs_view(part, h):
            t0 = (h % 2) * R
            return pT[part][:, (h // 2) % 2, :, t0:t0 + R].rearrange("p (b k) t -> p b k t", b=2)

        pt_view = ptb[0:JB, :, 0:3 * R].rearrange("p b (k t) -> p b k t", k=3)

        w_loaded = [sem(f"w_loaded{k}") for k in range(3)]
        w_hi, w_lo = sem("w_hi"), sem("w_lo")
        small_loaded, const_set, const_ready, zeroed = sem("small_loaded"), sem("const_set"), sem("const_ready"), sem("zeroed")
        trash_set, trash_ready, trash_stored = sem("trash_set"), sem("trash_ready"), sem("trash_stored")
        c_loaded, q_loaded, m_loaded, x_loaded = sem("c_loaded"), sem("q_loaded"), sem("m_loaded"), sem("x_loaded")
        xn_stored, out_stored = sem("xn_stored"), sem("out_stored")
        c_hi, c_lo, qz_hi, qz_lo, mb_made = sem("c_hi"), sem("c_lo"), sem("qz_hi"), sem("qz_lo"), sem("mb_made")
        gen_full, gen_hi, gen_free = sem("gen_full"), sem("gen_hi"), sem("gen_free")
        s_full, s_masked, nmx_made, e_made = sem("s_full"), sem("s_masked"), sem("nmx_made"), sem("e_made")
        pt_full, p_hi, p_lo = sem("pt_full"), sem("p_hi"), sem("p_lo")
        rec_made, p_made = sem("rec_made"), sem("p_made")
        pv_full, o_hi, o_lo = sem("pv_full"), sem("o_hi"), sem("o_lo")
        x1b_made, xo_made = sem("x1b_made"), sem("xo_made")
        stats_made, mv_made, root_made, rstd_made, xn_made = (sem(n) for n in ("stats_made", "mv_made", "root_made", "rstd_made", "xn_made"))
        newton = sem("newton")
        lg_made, le_made, route, sel_made, slots_made, sent = (sem(n) for n in ("lg_made", "le_made", "route", "sel_made", "slots_made", "sent"))

        pieces = [(w_k, wk, k) for k in range(CC)] + [(w_v, wv, k) for k in range(CC)] + [(w_o, wo, k) for k in range(KC)]
        block = ctx.enter_context(nc.Block())

        def iterations(eng, body):
            body(0, "first")
            with eng.Fori(1, B - 1) as i:
                body(i, "mid")
            body(B - 1, "last")

        def step(i, s):
            return (i, s) if s < NH else (i + 1, s - NH)

        def has_step(kind, s):
            return s < NH or kind != "last"

        def wait_apart(eng, semaphore, value):
            eng.wait_ge(small_loaded, 48)
            eng.wait_ge(semaphore, value)

        @block.sync
        def _(sp):
            for n, (src, dst, k) in enumerate(pieces):
                if n >= 3:
                    sp.wait_ge(w_lo, n - 2)
                sp.dma_start(craw[:, n % 3, 0:C], src[:, k, :]).then_inc(w_loaded[n % 3], 16)
            for dst, src in ((wr[:], w_r), (bo[:], b_o.partition_broadcast(R)), (bi[:], bias.partition_broadcast(R))):
                sp.dma_start(dst, src).then_inc(small_loaded, 16)
            sp.wait_ge(w_lo, 10)
            one = lambda t, i: t[i] if isinstance(i, int) else t[bass.ds(i, 1)]

            def flat(t, names):
                return t if len(t.shape) == 3 else t.rearrange(f"a {names} -> (a {names[0]}) {names[2:]}")

            def load_context(i):
                sp.dma_start(craw[:], flat(one(ctxT, i), "p k j")).then_inc(c_loaded, 16)

            def load_mask(i):
                row = mask[i:i + 1] if isinstance(i, int) else mask[bass.ds(i, 1)]
                sp.dma_start(m8[:], row.rearrange("a j -> (a j)").partition_broadcast(R)).then_inc(m_loaded, 16)

            def load_queries(i):
                sp.dma_start(q2[:], flat(one(q2_dram, i), "p k t")).then_inc(q_loaded, 16)

            load_context(0)
            load_queries(0)
            load_mask(0)
            sp.dma_start(x1[:], x1_v[0]).then_inc(x_loaded, 16)
            sp.wait_ge(trash_ready, 2)
            sp.dma_start(table_dram.rearrange("(e p n) w -> p e n w", e=E, n=CAP // 128), trash[:]).then_inc(trash_stored, 16)
            for k in range(CAP // 128):
                r0 = B * T + 128 * k
                sp.dma_start(xn_dram[r0:r0 + 128, :], zero[:]).then_inc(trash_stored, 16)
                sp.dma_start(out[r0:r0 + 128, :], zero[:]).then_inc(trash_stored, 16)
            sp.wait_ge(c_lo, CC)
            load_context(1)
            sp.wait_ge(qz_lo, 4)
            load_queries(1)
            sp.wait_ge(mb_made, 1)
            load_mask(1)

            def store(i):
                wait_apart(sp, xo_made, i)
                sp.dma_start(flat(one(out_v, i - 1), "r j c"), xo[:]).then_inc(out_stored, 16)
                wait_apart(sp, xn_made, i * 2)
                sp.dma_start(flat(one(xn_v, i - 1), "r j c"), xn[:]).then_inc(xn_stored, 16)

            def body(i, kind, more):
                if more:
                    wait_apart(sp, c_lo, i * CC + 2 * CC)
                    load_context(i + 2)
                if kind != "first":
                    store(i)
                    sp.dma_start(x1[:], flat(one(x1_v, i), "r j c")).then_inc(x_loaded, 16)
                if more:
                    wait_apart(sp, qz_lo, i * 4 + 8)
                    load_queries(i + 2)
                    wait_apart(sp, mb_made, i + 2)
                    load_mask(i + 2)

            body(0, "first", True)
            with sp.Fori(1, B - 2) as i:
                body(i, "mid", True)
            for i in range(B - 2, B):
                body(i, "last", False)
            store(B)
            sp.wait_ge(out_stored, 16 * B)
            sp.wait_ge(xn_stored, 16 * B)
            sp.wait_ge(sent, 64 * B)

        @block.gpsimd
        def _(pool):
            for t, val in ((ident, 1.0), (onesb, 1.0), (before, 1.0), (lower, 1.0), (eps, LN_EPS), (tstep, float(T)), (base, 0.0)):
                pool.memset(t[:], val).then_inc(const_set, 1)
            for j in range(2):
                pool.memset(kk[:, j, :], float(j)).then_inc(const_set, 1)
                pool.iota(tok[:, 2 * j:2 * j + 2], [[0, 2]], base=j * R - T, channel_multiplier=1,
                          allow_small_or_imprecise_dtypes=True).then_inc(const_set, 1)
            pool.iota(e896[:], [[CAP, E]], base=0, channel_multiplier=0, allow_small_or_imprecise_dtypes=True).then_inc(const_set, 1)
            pool.wait_ge(const_set, 12)
            pool.affine_select(out=ident[:], in_=ident[:], pattern=[[1, R]], compare_op=ALU.is_equal, fill=0.0,
                               base=0, channel_multiplier=-1).then_inc(const_ready, 1)
            pool.affine_select(out=before[:], in_=before[:], pattern=[[1, R]], compare_op=ALU.is_gt, fill=0.0,
                               base=0, channel_multiplier=-1).then_inc(const_ready, 1)
            pool.affine_select(out=lower[:], in_=lower[:], pattern=[[1, E], [-1, E]], compare_op=ALU.is_gt, fill=0.0,
                               base=0, channel_multiplier=0).then_inc(const_ready, 1)
            pool.memset(trash[:], 0.0).then_inc(trash_set, 1)
            pool.memset(zero[:], 0.0).then_inc(trash_ready, 1)
            pool.wait_ge(trash_set, 1)
            pool.iota(trash[:, :, :, 0].bitcast(I32), [[0, E], [1, CAP // 128]], base=B * T,
                      channel_multiplier=CAP // 128).then_inc(trash_ready, 1)

            def split_context(i, *ks):
                for k in ks or range(CC):
                    pool.wait_ge(c_hi, i * CC + k + 1)
                    pool.tensor_tensor(cT[1][:, k, :], craw[:, k, :], cT[0][:, k, :].bitcast(F32), ALU.subtract).then_inc(c_lo, 1)

            def add_bias(i):
                pool.wait_ge(x_loaded, i * 16 + 16)
                pool.tensor_tensor(x1[:], x1[:], bo[:, None, :].broadcast_to([R, 2, C]), ALU.add).then_inc(x1b_made, 1)

            def tail(i, kind, s):
                if s == 8:
                    pool.wait_ge(out_stored, i * 16 - 16)
                    pool.wait_ge(gen_free, number(ORDER, i, kind, ("OUT", 1, 0)) + 1)
                    pool.tensor_tensor(xo[:], x1[:], bi[:, None, :].broadcast_to([R, 2, C]), ALU.add).then_inc(xo_made, 1)
                if s == 14 and kind != "end":
                    add_bias(i)
                if s != 12:
                    return
                wait_apart(pool, slots_made, i)
                for q in range(4):
                    pool.indirect_dma_start(out=table_dram, out_offset=bass.IndirectOffsetOnAxis(ap=slotu[:, q:q + 1], axis=0),
                                            in_=pay[:, q, :], in_offset=None, bounds_check=E * CAP - 1, oob_is_err=False).then_inc(sent, 16)

            def normalise(i, h):
                pool.wait_ge(rec_made, i * NH + h + 1)
                pool.tensor_tensor(s_sb[:, h % 4, :], s_sb[:, h % 4, :], rec[:, h:h + 1].broadcast_to([R, J]), ALU.mult).then_inc(p_made, 1)

            split_context(0)
            pool.wait_ge(small_loaded, 48)
            add_bias(0)
            pool.wait_ge(trash_stored, 16 * 15)
            normalise(0, 0)

            def body(i, kind):
                for s in range(NH):
                    if has_step(kind, s + 1):
                        normalise(*step(i, s + 1))
                    if s in (4, 5) and kind != "last":
                        split_context(i + 1, *((0, 1) if s == 4 else (2,)))
                    if kind != "first":
                        tail(i, kind, s)

            iterations(pool, body)
            for s in range(NH):
                tail(B, "end", s)

        @block.vector
        def _(dve):
            for n, (src, dst, k) in enumerate(pieces):
                dve.wait_ge(w_loaded[n % 3], 16 * (n // 3 + 1))
                dve.tensor_copy(dst[0][:, k, :], craw[:, n % 3, 0:C]).then_inc(w_hi, 1)
                dve.wait_ge(w_hi, n + 1)
                dve.tensor_tensor(dst[1][:, k, :], craw[:, n % 3, 0:C], dst[0][:, k, :].bitcast(F32), ALU.subtract).then_inc(w_lo, 1)
            for k in range(2):
                dve.memset(qz[k][:].bitcast(F32), 0.0).then_inc(zeroed, 1)
            dve.wait_ge(zeroed, 2)
            dve.wait_ge(const_ready, 3)
            dve.wait_ge(const_set, 12)
            dve.wait_ge(small_loaded, 48)

            def mask_of(i):
                dve.wait_ge(m_loaded, i * 16 + 16)
                dve.tensor_scalar(mb[:], m8[:], 1.0, FLT_MAX, ALU.subtract, ALU.mult).then_inc(mb_made, 1)

            def inverse_sum(i, h):
                dve.wait_ge(e_made, i * NH + h + 1)
                dve.reciprocal(rec[:, h:h + 1], den[:, h:h + 1]).then_inc(rec_made, 1)

            def masked(i, h):
                half = lambda t: t.rearrange("p (a j) -> p a j", a=2)
                nc.vector.tensor_tensor_reduce(out=half(s_sb[:, h % 4, :]), in0=score_view(h), in1=half(mb[:]),
                                               scale=1.0, scalar=-FLT_MAX, op0=ALU.add, op1=ALU.max,
                                               accum_out=mx[:, h:h + 1]).then_inc(s_masked, 1)
                dve.wait_ge(s_masked, i * NH + h + 1)
                dve.tensor_scalar(nmx[:, h:h + 1], mx[:, h:h + 1], -1.0, None, ALU.mult).then_inc(nmx_made, 1)

            def lo_of_queries(i, g):
                for e in range(2):
                    p0 = 64 * e
                    dve.wait_ge(qz_hi, i * 4 + 2 * g + e + 1)
                    dve.tensor_tensor(qz[1][p0:p0 + 64, 4 * g + e:4 * g + 4:2, :], q2[p0:p0 + 64, 2 * g:2 * g + 2],
                                      qz[0][p0:p0 + 64, 4 * g + e:4 * g + 4:2, :].bitcast(F32), ALU.subtract).then_inc(qz_lo, 1)

            def lo_of_unit(i, kind, unit):
                what, m, a = unit
                dve.wait_ge(gen_hi, number(SPLIT, i, kind, unit) + 1)
                dst, src = unit_places(unit)
                dve.tensor_tensor(dst(1), src, dst(0).bitcast(F32), ALU.subtract).then_inc(gen_free, 1)

            def lo_of_probs(i, h):
                dve.wait_ge(p_hi, i * NH + h + 1)
                dve.tensor_tensor(probs_view(1, h), pt_view, probs_view(0, h).bitcast(F32), ALU.subtract).then_inc(p_lo, 1)

            def lo_of_outputs(i, m):
                for e in range(2):
                    p0 = 64 * e
                    dve.wait_ge(o_hi, i * H2 + 2 * m + e + 1)
                    dve.tensor_tensor(oT[1][p0:p0 + 64, m, :], ob[p0:p0 + 64, e * T:e * T + T], oT[0][p0:p0 + 64, m, :].bitcast(F32),
                                      ALU.subtract).then_inc(o_lo, 1)

            def residual(i, kind, j):
                if j == 0:
                    wait_apart(dve, x1b_made, i)
                dve.wait_ge(gen_full, number(ORDER, i, kind, ("OUT", j, 0)) + 1)
                dve.tensor_tensor(x1[:, j, :], x1[:, j, :], gen[0:R, :], ALU.add).then_inc(gen_free, 1)
                if j == 0:
                    return
                for j in range(2):
                    wait_apart(dve, gen_free, number(ORDER, i, kind, ("OUT", j, 0)) + 1)
                    ins = dve.bn_stats(stats[:, j, :], x1[:, j, :])
                ins.then_inc(stats_made, 1)
                wait_apart(dve, stats_made, i)
                for j in range(2):
                    dve.bn_aggr(mv[:, j, :], stats[:, j, :]).then_inc(mv_made, 1)

            def layernorm(i):
                dve.wait_ge(root_made, i)
                dve.tensor_tensor(nt[:, 0, :], rstd[:], rstd[:], ALU.mult).then_inc(newton, 1)
                dve.wait_ge(newton, i * 3 - 2)
                dve.scalar_tensor_tensor(nt[:, 1, :], mv[:, :, 1], LN_EPS, nt[:, 0, :], ALU.add, ALU.mult).then_inc(newton, 1)
                dve.wait_ge(newton, i * 3 - 1)
                dve.tensor_scalar(nt[:, 0, :], nt[:, 1, :], -0.5, 1.5, ALU.mult, ALU.add).then_inc(newton, 1)
                dve.wait_ge(newton, i * 3)
                dve.tensor_tensor(rstd[:], rstd[:], nt[:, 0, :], ALU.mult).then_inc(rstd_made, 1)
                dve.wait_ge(xn_stored, i * 16 - 16)
                dve.wait_ge(rstd_made, i)
                for j in range(2):
                    dve.tensor_scalar(xn[:, j, :], x1[:, j, :], mv[:, j, 0:1], rstd[:, j:j + 1], ALU.subtract, ALU.mult).then_inc(xn_made, 1)

            SPLIT_AT = 10

            def routing(i, kind, part):
                done = [0] if part == 0 else [SPLIT_AT]

                def then(ins):
                    done[0] += 1
                    ins.then_inc(route, 1)
                    dve.wait_ge(route, (i - 1) * ROUTE + done[0])

                def over(t, shape):
                    return t.broadcast_to(shape)

                if part == 0:
                    L = gen[0:R, 0:2 * E].rearrange("p (j e) -> p j e", j=2)
                    dve.wait_ge(gen_full, number(ORDER, i, kind, ("RT", 0, 0)) + 1)
                    then(dve.tensor_reduce(lmx[:], L, AX.X, ALU.max))
                    dve.tensor_tensor(lg[:], L, over(lmx[:, :, None], L2), ALU.subtract).then_inc(gen_free, 1)
                    dve.wait_ge(le_made, i)
                    then(dve.tensor_reduce(lsum[:], lg[:], AX.X, ALU.add))
                    then(dve.reciprocal(lrec[:], lsum[:]))
                    then(dve.tensor_tensor(sc[:], lg[:], over(lrec[:, :, None], L2), ALU.mult))
                    L4 = [R, 2, E, E]
                    other, own = over(sc[:, :, None, :], L4), over(sc[:, :, :, None], L4)
                    dve.tensor_tensor(ge[:], other, own, ALU.is_equal).then_inc(route, 1)
                    done[0] += 1
                    then(dve.tensor_tensor(gt[:], other, own, ALU.is_gt))
                    then(dve.tensor_tensor(ge[:], ge[:], over(lower[:, None], L4), ALU.mult))
                    then(dve.tensor_tensor(gt[:], gt[:], ge[:], ALU.add))
                    then(dve.tensor_reduce(rank[:], gt[:], AX.X, ALU.add))
                    then(dve.tensor_scalar(sel[:], rank[:], 2.0, None, ALU.is_lt))
                    dve.tensor_copy(selb[:], sel[:]).then_inc(sel_made, 1)
                    assert done[0] == SPLIT_AT
                else:
                    dve.wait_ge(gen_full, number(ORDER, i, kind, ("PRE", 0, 0)) + 1)
                    pre = gen[0:R, 0:3 * E].rearrange("p (j e) -> p j e", j=3)
                    then(dve.tensor_tensor(off[:], pre[:, 0:2], base[:], ALU.add))
                    dve.tensor_tensor(base[:], base[:], over(pre[:, 2:3], L2), ALU.add).then_inc(gen_free, 1)
                    then(dve.tensor_scalar(inv[:], off[:], float(CAP), float(2 * E * CAP), ALU.is_ge, ALU.mult))
                    then(dve.tensor_tensor(off[:], off[:], over(e896[:, None], L2), ALU.add))
                    then(dve.tensor_tensor(off[:], off[:], inv[:], ALU.add))
                    K4 = [R, 2, 2, E]
                    then(dve.tensor_tensor(oh[:], over(rank[:, :, None, :], K4), over(kk[:, None], K4), ALU.is_equal))
                    then(dve.tensor_tensor(ohs[:], oh[:], over(off[:, :, None, :], K4), ALU.mult))
                    then(dve.tensor_reduce(slotf[:].rearrange("p (j k) -> p j k", j=2), ohs[:], AX.X, ALU.add))
                    then(dve.tensor_tensor(ohs[:], oh[:], over(sc[:, :, None, :], K4), ALU.mult))
                    then(dve.tensor_tensor(tok[:], tok[:], tstep[:], ALU.add))
                    dve.wait_ge(sent, i * 64 - 64)
                    then(dve.tensor_reduce(pay[:, :, 1].rearrange("p (j k) -> p j k", j=2), ohs[:], AX.X, ALU.add))
                    then(dve.tensor_copy(pay[:, :, 0].bitcast(I32), tok[:]))
                    assert done[0] == ROUTE
                    dve.tensor_copy(slotu[:], slotf[:]).then_inc(slots_made, 1)

            def tail(i, kind, s):
                if s == 2:
                    lo_of_outputs(i - 1, NM - 1)
                elif s in (3, 4):
                    residual(i, kind, s - 3)
                elif s == 5:
                    layernorm(i)
                elif s == 8:
                    routing(i, kind, 0)
                elif s == 10:
                    routing(i, kind, 1)

            for g in range(2):
                lo_of_queries(0, g)
            for unit in START:
                lo_of_unit(0, "start", unit)
            mask_of(0)
            dve.wait_ge(mb_made, 1)
            dve.wait_ge(s_full, 1)
            masked(0, 0)
            dve.wait_ge(s_full, 2)
            inverse_sum(0, 0)
            masked(0, 1)

            def body(i, kind):
                for s in range(NH):
                    if has_step(kind, s + 2):
                        if s + 2 == NH:
                            mask_of(i + 1)
                            dve.wait_ge(mb_made, i + 2)
                        dve.wait_ge(s_full, i * NH + s + 3)
                    if has_step(kind, s + 1):
                        inverse_sum(*step(i, s + 1))
                    if has_step(kind, s + 2):
                        masked(*step(i, s + 2))
                    for unit in projections(kind, s, 0):
                        lo_of_unit(i, kind, unit)
                    if s > 0:
                        lo_of_probs(i, s - 1)
                    elif kind != "first":
                        lo_of_probs(i - 1, NH - 1)
                    for unit in projections(kind, s, 1):
                        lo_of_unit(i, kind, unit)
                    if s in (6, 10, 14):
                        lo_of_outputs(i, s // 4 - 1)
                    if kind != "first":
                        tail(i, kind, s)
                    if s in (8, 15) and kind != "last":
                        lo_of_queries(i + 1, s // 9)

            iterations(dve, body)
            lo_of_probs(B - 1, NH - 1)
            for s in range(NH):
                tail(B, "end", s)

        @block.scalar
        def _(act):
            act.wait_ge(zeroed, 2)
            act.wait_ge(const_set, 12)

            def hi_of_context(i):
                act.wait_ge(c_loaded, i * 16 + 16)
                for k in range(CC):
                    act.copy(cT[0][:, k, :], craw[:, k, :]).then_inc(c_hi, 1)

            def hi_of_queries(i, g):
                act.wait_ge(q_loaded, i * 16 + 16)
                for e in range(2):
                    act.copy(qz[0][64 * e:64 * e + 64, 4 * g + e:4 * g + 4:2, :],
                             q2[64 * e:64 * e + 64, 2 * g:2 * g + 2]).then_inc(qz_hi, 1)

            def hi_of_unit(i, kind, unit):
                act.wait_ge(gen_full, number(ORDER, i, kind, unit) + 1)
                dst, src = unit_places(unit)
                act.copy(dst(0), src).then_inc(gen_hi, 1)

            def hi_of_probs(i, h):
                act.wait_ge(pt_full, i * NH + h + 1)
                act.copy(probs_view(0, h), pt_view).then_inc(p_hi, 1)

            def hi_of_outputs(i, m):
                act.wait_ge(pv_full, i * NM + m + 1)
                for e in range(2):
                    act.copy(oT[0][64 * e:64 * e + 64, m, :], ob[64 * e:64 * e + 64, e * T:e * T + T]).then_inc(o_hi, 1)

            def exponential(i, h):
                act.wait_ge(nmx_made, i * NH + h + 1)
                act.activation(s_sb[:, h % 4, :], s_sb[:, h % 4, :], ACT.Exp, bias=nmx[:, h:h + 1],
                               accum_out=den[:, h:h + 1]).then_inc(e_made, 1)

            def tail(i, kind, s):
                if s == 2:
                    hi_of_outputs(i - 1, NM - 1)
                elif s == 4:
                    act.wait_ge(mv_made, i * 2)
                    act.activation(rstd[:], mv[:, :, 1], ACT.Abs_reciprocal_sqrt, bias=eps[:]).then_inc(root_made, 1)
                elif s in (6, 7):
                    act.wait_ge(gen_full, number(ORDER, i, kind, ("XT", s - 6, 0)) + 1)
                    act.copy(xnT[:, s - 6, :], gen[:, 0:KC * R]).then_inc(gen_free, 1)
                elif s == 8:
                    act.wait_ge(gen_free, number(ORDER, i, kind, ("RT", 0, 0)) + 1)
                    act.activation(lg[:], lg[:], ACT.Exp).then_inc(le_made, 1)

            hi_of_context(0)
            for g in range(2):
                hi_of_queries(0, g)
            for unit in START:
                hi_of_unit(0, "start", unit)
            exponential(0, 0)
            exponential(0, 1)

            def body(i, kind):
                for s in range(NH):
                    for unit in projections(kind, s, 0):
                        hi_of_unit(i, kind, unit)
                    if s > 0:
                        hi_of_probs(i, s - 1)
                    elif kind != "first":
                        hi_of_probs(i - 1, NH - 1)
                    if has_step(kind, s + 2):
                        exponential(*step(i, s + 2))
                    for unit in projections(kind, s, 1):
                        hi_of_unit(i, kind, unit)
                    if s == 4 and kind != "last":
                        act.wait_ge(gen_full, number(ORDER, i, kind, V(1, 2)) + 1)
                        hi_of_context(i + 1)
                    if s in (6, 10, 14):
                        hi_of_outputs(i, s // 4 - 1)
                    if kind != "first":
                        tail(i, kind, s)
                    if s in (8, 15) and kind != "last":
                        act.wait_ge(s_full, i * NH + s + 1)
                        hi_of_queries(i + 1, s // 9)

            iterations(act, body)
            hi_of_probs(B - 1, NH - 1)
            for s in range(NH):
                tail(B, "end", s)

        @block.tensor
        def _(pe):
            def product(out, lhs, rhs, n):
                steps = [(a, b, k) for a, b in ((0, 0), (0, 1), (1, 0)) for k in range(n)]
                for q, (a, b, k) in enumerate(steps):
                    mm = pe.matmul(out, lhs(a, k), rhs(b, k), start=q == 0, stop=q == len(steps) - 1)
                return mm

            def scores(i, h):
                head, t0 = h // 2, (h % 2) * R
                pe.wait_ge(s_masked, i * NH + (h - 1) if h >= 2 else (i - 1) * NH + NH + h - 1) if not (isinstance(i, int) and i == 0 and h < 2) else None
                if h % 8 == 0:
                    pe.wait_ge(qz_lo, i * 4 + (4 if h else 2))
                for a in range(2):
                    mm = product(scb[h % 2][0:R, a, 0:HW], lambda x, k: qz[x][:, head, t0:t0 + R],
                                 lambda y, k: kT[y][:, head // 2, a * (J - HW):a * (J - HW) + HW], 1)
                mm.then_inc(s_full, 1)

            def transposes(i, h):
                pe.wait_ge(p_made, i * NH + h + 1)
                pe.wait_ge(p_lo, i * NH + h)
                for j in range(NJ):
                    mm = pe.transpose(ptb[0:JB, j // 3, R * (j % 3):R * (j % 3) + R], s_sb[:, h % 4, JB * j:JB * j + JB], ident[:])
                mm.then_inc(pt_full, 1)

            def values(i, head):
                m, e = head // 2, head % 2
                pe.wait_ge(p_lo, i * NH + 2 * head + 2)
                if e == 0:
                    pe.wait_ge(o_lo, i * H2 + 2 * m)
                mm = product(ob[:, e * T:e * T + T], lambda x, k: v[x][:, k, 128 * m:128 * m + 128],
                             lambda y, k: pT[y][:, e, k, :], NJ)
                if e:
                    mm.then_inc(pv_full, 1)

            def unit_of(i, kind, unit):
                what, m, a = unit
                pe.wait_ge(gen_free, number(ORDER, i, kind, unit))
                if unit == K(0, 0):
                    pe.wait_ge(c_lo, CC if kind == "start" else i * CC + 2 * CC)
                if what == "K":
                    mm = product(gen[:, 0:KW[a]], lambda x, k: wk[x][:, k, 128 * m:128 * m + 128],
                                 lambda y, k: cT[y][:, k, K0[a]:K0[a] + KW[a]], CC)
                elif what == "V":
                    for b in range(2):
                        j = 2 * a + b
                        mm = product(gen[0:JB, 256 * b:256 * b + 256], lambda x, k: cT[x][:, k, JB * j:JB * j + JB],
                                     lambda y, k: wv[y][:, k, 256 * m:256 * m + 256], CC)
                elif what == "OUT":
                    if m == 0:
                        pe.wait_ge(o_lo, i * H2)
                    mm = product(gen[0:R, :], lambda x, k: oT[x][:, k, R * m:R * m + R], lambda y, k: wo[y][:, k, :], KC)
                elif what == "XT":
                    if m == 0:
                        pe.wait_ge(xn_made, i * 2)
                    for k in range(KC):
                        mm = pe.transpose(gen[:, R * k:R * k + R], xn[:, m, 128 * k:128 * k + 128], ident[:])
                elif what == "RT":
                    for j in range(2):
                        for k in range(KC):
                            mm = pe.matmul(gen[0:R, E * j:E * j + E], xnT[:, j, R * k:R * k + R], wr[:, k, :], start=k == 0, stop=k == KC - 1)
                else:
                    pe.wait_ge(sel_made, i)
                    pre = gen[0:R]
                    pe.matmul(pre[:, 0:E], before[:], selb[:, 0, :], start=True, stop=True)
                    pe.matmul(pre[:, E:2 * E], before[:], selb[:, 1, :], start=True, stop=False)
                    pe.matmul(pre[:, E:2 * E], onesb[:], selb[:, 0, :], start=False, stop=True)
                    pe.matmul(pre[:, 2 * E:3 * E], onesb[:], selb[:, 0, :], start=True, stop=False)
                    mm = pe.matmul(pre[:, 2 * E:3 * E], onesb[:], selb[:, 1, :], start=False, stop=True)
                mm.then_inc(gen_full, 1)

            pe.wait_ge(w_lo, len(pieces))
            pe.wait_ge(const_ready, 3)
            pe.wait_ge(const_set, 12)
            pe.wait_ge(small_loaded, 48)
            for unit in START:
                unit_of(0, "start", unit)
            scores(0, 0)
            scores(0, 1)

            def body(i, kind):
                for s in range(NH):
                    if has_step(kind, s + 2):
                        scores(*step(i, s + 2))
                    for unit in units(kind, s, (0,)):
                        unit_of(i, kind, unit)
                    if s > 0:
                        transposes(i, s - 1)
                    elif kind != "first":
                        transposes(i - 1, NH - 1)
                    for unit in units(kind, s, (1,)):
                        unit_of(i, kind, unit)
                    if s >= 3 and s % 2:
                        values(i, (s - 3) // 2)
                    elif s == 1 and kind != "first":
                        values(i - 1, H2 - 1)
                    for unit in units(kind, s, (2,)):
                        unit_of(i, kind, unit)

            iterations(pe, body)
            transposes(B - 1, NH - 1)
            values(B - 1, H2 - 1)
            for unit in ORDER["end"]:
                unit_of(B, "end", unit)


def experts(nc, w1, w2, xn_dram, table_dram, out):
    FB = F // 128
    NT = CAP // 128
    HC = CAP // 2
    NW = E * FB
    PAIRS = E // 2
    NSLOT = 4
    w2_v = w2.rearrange("(g b p) c -> g p b c", b=2, p=128)
    tab_v = table_dram.rearrange("(e t p) w -> e p t w", e=E, p=128)
    with ExitStack() as ctx:
        sb = lambda n, s, d=F32: ctx.enter_context(nc.sbuf_tensor("f_" + n, s, d))
        sem = lambda n: ctx.enter_context(nc.semaphore("f_" + n))
        ident = sb("ident", [128, 128])
        raw1 = sb("raw1", [128, 2, 2, C])
        raw2 = sb("raw2", [128, 2, 2, C])
        w1s = [sb(f"w1{k}", [128, NSLOT, KC, 128], F32R) for k in "hl"]
        w2s = [sb(f"w2{k}", [128, NSLOT, C], F32R) for k in "hl"]
        meta = sb("meta", [128, 2, NT, 2])
        xg = sb("xg", [128, NT, C])
        xT = [[sb(f"xT{k}{p}", [128, KC, CAP], F32R) for k in "hl"] for p in range(2)]
        hf = sb("hf", [128, 2, HC])
        hs = [sb(f"h{k}", [128, 2, CAP], F32R) for k in "hl"]
        ys = sb("ys", [128, NT, C])
        Y = [ctx.enter_context(nc.psum_tensor(f"f_y{k}", [128, 512], F32)) for k in range(NT)]
        H = ctx.enter_context(nc.psum_tensor("f_h", [128, 512], F32))

        const_set, const_ready = sem("const_set"), sem("const_ready")
        loaded = [sem("loaded0"), sem("loaded1")]
        w_hi, w_lo = sem("w_hi"), sem("w_lo")
        meta_loaded, gathered, scattered = sem("meta_loaded"), sem("gathered"), sem("scattered")
        full, free = sem("full"), sem("free")
        x_hi = sem("x_hi")
        h_hi, h_lo = sem("h_hi"), sem("h_lo")
        y_done, yt_done, ys_made = sem("y_done"), sem("yt_done"), sem("ys_made")

        FIRST_T = 5
        order = []
        for j in range(FB):
            order.append(("h", 2 * j))
            if FIRST_T <= j < FIRST_T + NT:
                order.append(("t", j - FIRST_T))
            order.append(("h", 2 * j + 1))
        use = {key: n for n, key in enumerate(order)}
        USES = len(order)
        GATHER_J = 3
        BL = 2 * FB

        block = ctx.enter_context(nc.Block())

        @block.sync
        def _(sp):
            sp.dma_start(meta[:, 0], tab_v[0]).then_inc(meta_loaded, 16)

            def load(g, a, b):
                sp.dma_start(raw1[:, g % 2].rearrange("p b c -> p (b c)"), a).then_inc(loaded[g % 2], 16)
                sp.dma_start(raw2[:, g % 2], b).then_inc(loaded[g % 2], 16)

            for g in range(2):
                load(g, w1[g], w2_v[g])
            with sp.Fori(0, PAIRS) as it:
                for g in range(FB):
                    if g % (FB // 2) == 1:
                        p = g // (FB // 2)
                        nxt = sp.snap((it * 2 + p + 1) % E)
                        sp.wait_ge(const_ready, 1)
                        sp.wait_ge(scattered, (it * 2 + p) * (16 * NT))
                        sp.dma_start(meta[:, (p + 1) % 2], tab_v[bass.ds(nxt, 1)].rearrange("a p t w -> (a p) t w")).then_inc(meta_loaded, 16)
                    src = sp.snap((it * FB + g + 2) % (NW // 2))
                    sp.wait_ge(const_ready, 1)
                    sp.wait_ge(w_lo, it * (4 * FB) + 4 * g + 4)
                    load(g + 2, w1[bass.ds(src, 1)].rearrange("a p n -> (a p) n"), w2_v[bass.ds(src, 1)].rearrange("a p b c -> (a p) b c"))
            sp.wait_ge(scattered, E * 16 * NT)
            for g in range(2):
                sp.wait_ge(loaded[g], 32 * (NW // 4 + 1))
            sp.wait_ge(meta_loaded, 16 * (E + 1))
            sp.wait_ge(gathered, 16 * NT * (E + 1))

        @block.gpsimd
        def _(pool):
            pool.memset(ident[:], 1.0).then_inc(const_set, 1)
            pool.wait_ge(const_set, 1)
            pool.affine_select(out=ident[:], in_=ident[:], pattern=[[1, 128]], compare_op=ALU.is_equal, fill=0.0,
                               base=0, channel_multiplier=-1).then_inc(const_ready, 1)

            def gather(p):
                for t in range(NT):
                    pool.indirect_dma_start(out=xg[:, t, :], out_offset=None, in_=xn_dram,
                                            in_offset=bass.IndirectOffsetOnAxis(ap=meta[:, p, t, 0:1].bitcast(U32), axis=0)).then_inc(gathered, 16)

            def scatter(p):
                for t in range(NT):
                    pool.indirect_dma_start(out=out, out_offset=bass.IndirectOffsetOnAxis(ap=meta[:, p, t, 0:1].bitcast(U32), axis=0),
                                            in_=ys[:, t, :], in_offset=None, compute_op=ALU.add).then_inc(scattered, 16)

            def split(n, w, base):
                g = n // 2
                pool.wait_ge(w_hi, base + 2 * n + 1)
                pool.tensor_tensor(w1s[1][:, n % NSLOT].rearrange("p k c -> p (k c)"), raw1[:, g % 2, n % 2, :],
                                   w1s[0][:, n % NSLOT].rearrange("p k c -> p (k c)").bitcast(F32), ALU.subtract).then_inc(w_lo, 1)
                for s, val in w:
                    pool.wait_ge(s, val)
                pool.wait_ge(w_hi, base + 2 * n + 2)
                pool.tensor_tensor(w2s[1][:, n % NSLOT], raw2[:, g % 2, n % 2, :], w2s[0][:, n % NSLOT].bitcast(F32),
                                   ALU.subtract).then_inc(w_lo, 1)

            pool.wait_ge(meta_loaded, 16)
            gather(0)
            for n in range(2):
                split(n, (), 0)

            with pool.Fori(0, PAIRS) as it:
                for l in range(BL):
                    p, j = divmod(l, FB)
                    w = ()
                    if j == GATHER_J:
                        w = ((meta_loaded, it * 32 + 16 * p + 32), (free, it * (2 * USES) + p * USES + NT))
                    if j == FB - 1:
                        w = ((ys_made, it * (2 * NT) + NT * (p + 1)), (scattered, (it * 2 + p) * (16 * NT)))
                    split(l + 2, w, it * (2 * BL))
                    if j == GATHER_J:
                        gather((p + 1) % 2)
                    if j == FB - 1:
                        scatter(p)

        @block.vector
        def _(dve):
            def split(n, it):
                g = n // 2
                dve.wait_ge(loaded[g % 2], it * (16 * FB) + 32 * (g // 2) + 32)
                dve.tensor_copy(w1s[0][:, n % NSLOT].rearrange("p k c -> p (k c)"), raw1[:, g % 2, n % 2, :]).then_inc(w_hi, 1)
                dve.tensor_copy(w2s[0][:, n % NSLOT], raw2[:, g % 2, n % 2, :]).then_inc(w_hi, 1)

            def rows_lo(p, t, count):
                dve.wait_ge(x_hi, count)
                dve.tensor_tensor(xT[p][1][:, :, 128 * t:128 * t + 128], H[:].rearrange("p (k s) -> p k s", k=KC),
                                  xT[p][0][:, :, 128 * t:128 * t + 128].bitcast(F32), ALU.subtract).then_inc(free, 1)

            for n in range(2):
                split(n, 0)
            for t in range(NT):
                rows_lo(0, t, t + 1)
            with dve.Fori(0, PAIRS) as it:
                for l in range(BL):
                    p, j = divmod(l, FB)
                    for c in range(2):
                        dve.wait_ge(free, it * (2 * USES) + p * USES + NT + use["h", 2 * j + c] + 1)
                        dve.wait_ge(y_done, it * BL + max(l - 1, 0))
                        dve.tensor_copy(hs[0][:, l % 2, c * HC:c * HC + HC], hf[:, c, :]).then_inc(h_hi, 1)
                        dve.wait_ge(h_hi, it * (2 * BL) + 2 * l + c + 1)
                        dve.tensor_tensor(hs[1][:, l % 2, c * HC:c * HC + HC], hf[:, c, :],
                                          hs[0][:, l % 2, c * HC:c * HC + HC].bitcast(F32), ALU.subtract).then_inc(h_lo, 1)
                        t = j - FIRST_T
                        if c == 0 and 0 <= t < NT:
                            rows_lo((p + 1) % 2, t, it * (2 * NT) + p * NT + NT + t + 1)
                    split(l + 2, it)

        @block.scalar
        def _(act):
            def rows_hi(p, t, count):
                act.wait_ge(full, count)
                act.copy(xT[p][0][:, :, 128 * t:128 * t + 128], H[:].rearrange("p (k s) -> p k s", k=KC)).then_inc(x_hi, 1)

            for t in range(NT):
                rows_hi(0, t, t + 1)
            with act.Fori(0, PAIRS) as it:
                for l in range(BL):
                    p, j = divmod(l, FB)
                    for c in range(2):
                        base = it * (2 * USES) + p * USES + NT
                        act.wait_ge(full, base + use["h", 2 * j + c] + 1)
                        act.wait_ge(h_lo, it * (2 * BL) + max(2 * l + c - 1, 0))
                        act.activation(hf[:, c, :], H[:, 0:HC], ACT.Gelu_apprx_tanh).then_inc(free, 1)
                        t = j - FIRST_T
                        if c == 0 and 0 <= t < NT:
                            rows_hi((p + 1) % 2, t, base + use["t", t] + 1)
                    if j == FB - 1:
                        act.wait_ge(scattered, (it * 2 + p) * (16 * NT))
                        for t in range(NT):
                            act.wait_ge(yt_done, it * (2 * NT) + p * NT + t + 1)
                            act.activation(ys[:, t, :], Y[t][:], ACT.Copy, scale=meta[:, p, t, 1:2]).then_inc(ys_made, 1)

        @block.tensor
        def _(pe):
            THREE = ((0, 0), (0, 1), (1, 0))

            def rows(t):
                for k in range(KC):
                    mm = pe.transpose(H[:, 128 * k:128 * k + 128], xg[:, t, 128 * k:128 * k + 128], ident[:])
                mm.then_inc(full, 1)

            pe.wait_ge(const_ready, 1)
            pe.wait_ge(gathered, 16 * NT)
            for t in range(NT):
                if t:
                    pe.wait_ge(free, t)
                rows(t)
            with pe.Fori(0, PAIRS) as it:
                for l in range(BL):
                    p, j = divmod(l, FB)
                    base = it * (2 * USES) + p * USES + NT

                    def hidden(c):
                        pe.wait_ge(free, base + use["h", 2 * j + c])
                        if c == 0:
                            pe.wait_ge(w_lo, it * (2 * BL) + 2 * l + 1)
                        for q, (a, b) in enumerate(THREE):
                            for k in range(KC):
                                mm = pe.matmul(H[:, 0:HC], w1s[a][:, l % NSLOT, k, :], xT[p][b][:, k, c * HC:c * HC + HC],
                                               start=q + k == 0, stop=(q, k) == (2, KC - 1))
                        mm.then_inc(full, 1)

                    def outputs(l, tiles):
                        p, j = divmod(l, FB)
                        for t in tiles:
                            if t == 0:
                                pe.wait_ge(w_lo, it * (2 * BL) + 2 * l + 2)
                                pe.wait_ge(h_lo, it * (2 * BL) + 2 * l + (2 if j < FB - 1 else 1))
                                if j == 0:
                                    pe.wait_ge(ys_made, it * (2 * NT) + p * NT)
                            if j == FB - 1 and t == 3:
                                pe.wait_ge(h_lo, it * (2 * BL) + 2 * l + 2)
                            for q, (a, b) in enumerate(THREE):
                                mm = pe.matmul(Y[t][:], hs[a][:, l % 2, 128 * t:128 * t + 128], w2s[b][:, l % NSLOT, :],
                                               start=j == 0 and q == 0, stop=j == FB - 1 and q == 2)
                            if j == FB - 1:
                                mm.then_inc(yt_done, 1)
                        if NT - 1 in tiles:
                            if j == FB - 1:
                                pe.wait_ge(yt_done, it * (2 * NT) + p * NT + NT)
                                pe.sem_inc(y_done, 1)
                            else:
                                mm.then_inc(y_done, 1)

                    hidden(0)
                    if j > 0:
                        outputs(l - 1, (0, 1))
                    t = j - FIRST_T
                    if 0 <= t < NT:
                        if t == 0:
                            pe.wait_ge(gathered, it * (2 * 16 * NT) + (p + 2) * (16 * NT))
                        pe.wait_ge(free, base + use["t", t])
                        rows(t)
                    if j > 0:
                        outputs(l - 1, (2, 3))
                    hidden(1)
                    if j > 0:
                        outputs(l - 1, (4, 5, 6))
                    if j == FB - 1:
                        outputs(l, range(NT))


def decoder_block(nc, x, w_qkvT, w_outT, slopes, w_qT, w_k, w_v, w_o, b_o, ctxT, mask, w_r, w1, w2, bias, out):
    scratch = lambda name, shape: nc.dram_tensor(name, shape, F32, kind="Internal").ap()
    x1_dram = scratch("x1_dram", [B * T, C])
    q2_dram = scratch("q2_dram", [B, 128, KC, T])
    xn_dram = scratch("xn_dram", [B * T + CAP, C])
    table_dram = scratch("table_dram", [E * CAP, 2])
    self_attention(nc, x, w_qkvT, w_outT, w_qT, slopes, x1_dram, q2_dram)
    cross_attention(nc, ctxT, mask, q2_dram, x1_dram, w_k, w_v, w_o, b_o, w_r, bias, out, xn_dram, table_dram)
    experts(nc, w1, w2, xn_dram, table_dram, out)


def kernel(**inputs):
    import numpy as _np
    import concourse.bacc as _bacc
    from concourse import mybir as _mybir
    from concourse.bass_utils import run_bass_kernel_spmd as _run

    def rows_on_partitions(w):
        return w.reshape(-1, 128, w.shape[1]).transpose(1, 0, 2)

    g = {name: _np.asarray(a) for name, a in inputs.items()}
    laid = {
        "x": g["x"].reshape(B * T, C),
        "w_qkvT": rows_on_partitions(g["L0_attn_w_qkv"].T),
        "w_outT": rows_on_partitions(g["L0_attn_w_out"].T),
        "slopes": g["L0_attn_alibi_slopes"],
        "w_qT": rows_on_partitions(g["L0_xattn_W_q"]),
        "w_k": rows_on_partitions(g["L0_xattn_W_k"]),
        "w_v": rows_on_partitions(g["L0_xattn_W_v"]),
        "w_o": rows_on_partitions(g["L0_xattn_W_o"]),
        "b_o": g["L0_xattn_b_o"],
        "ctxT": g["ctx_768"].transpose(0, 2, 1).reshape(B, CC, 128, J).transpose(0, 2, 1, 3),
        "mask": g["mask_BxS2_bk0"].reshape(-1).view(_np.int32),
        "w_r": rows_on_partitions(g["L0_ffn_w_router"]),
        "w1": g["L0_ffn_w1"].reshape(E, KC, 128, F // 256, 2, 128).transpose(0, 3, 2, 4, 1, 5).reshape(E * F // 256, 128, 2 * C),
        "w2": g["L0_ffn_w2"].reshape(E * F, C),
        "bias": g["L0_ffn_bias"].reshape(C),
    }
    nc = _bacc.Bacc("TRN2", target_bir_lowering=False, num_devices=1)
    arrays, args = {}, []
    for name, a in laid.items():
        a = _np.ascontiguousarray(a)
        arrays[f"in_{name}"] = a
        args.append(nc.dram_tensor(f"in_{name}", a.shape, _mybir.dt.from_np(a.dtype), kind="ExternalInput").ap())
    args.append(nc.dram_tensor("out_x", (B * T + CAP, C), F32, kind="ExternalOutput").ap())
    decoder_block(nc, *args)
    r = _run(nc, [arrays], core_ids=[0])
    return r.results[0]["out_x"][:B * T].reshape(B, T, C)
```

```python
from contextlib import ExitStack

import concourse.bass as bass
from concourse import mybir

F32, F32R, BF16 = mybir.dt.float32, mybir.dt.float32r, mybir.dt.bfloat16
I32, U32, U8 = mybir.dt.int32, mybir.dt.uint32, mybir.dt.uint8
ALU, ACT, AX = mybir.AluOpType, mybir.ActivationFunctionType, mybir.AxisListType

B, T, C = 16, 224, 512
KC = C // 128
R = T // 2
TPI = 4
TOK = TPI * R
H1, D1 = 16, 32
H2, D2 = 8, 64
LN_EPS, RS_EPS = 1e-5, 1e-6
FLT_MAX = 3.4028234663852886e38
J, CC, JB = 750, 3, 125
E, CAP, F = 8, 896, 2048




def self_attention(nc, x, w_qkvT, w_outT, w_qT, slopes, x1_dram, q2_dram):
    NIT = B * T // TOK
    x_v = x.rearrange("(i j r) c -> i r j c", j=TPI, r=R)
    x1_v = x1_dram.rearrange("(i j r) c -> i r j c", j=TPI, r=R)
    q2_v = q2_dram.rearrange("(i b) p k t -> i k p b t", b=2)
    NG = 8
    NPAIR = T + R
    with ExitStack() as ctx:
        sb = lambda n, s, d=F32: ctx.enter_context(nc.sbuf_tensor("a_" + n, s, d))
        sem = lambda n: ctx.enter_context(nc.semaphore("a_" + n))
        wqkv = [sb(f"wqkv{k}", [128, KC, 3 * C], F32R) for k in "hl"]
        wout = [sb(f"wout{k}", [128, KC, C], F32R) for k in "hl"]
        wq2 = [sb(f"wq2{k}", [128, KC, C], F32R) for k in "hl"]
        ident = sb("ident", [R, R])
        dist = sb("dist", [R, NPAIR])
        keep = sb("keep", [R, NPAIR])
        slope = sb("slope", [R, H1])
        ones = sb("ones", [R, 32])
        eps = sb("eps", [128, 3])
        x_in = sb("x_in", [R, TPI, C])
        xr = sb("xr", [R, TPI, C])
        work = sb("work", [128, TPI * C])
        xn = work[0:R, :].rearrange("p (j c) -> p j c", j=TPI)
        oT = work[:, 0:KC * TOK].rearrange("p (k t) -> p k t", k=KC)
        xT = [sb(f"xT{k}", [128, KC, TOK], F32R) for k in "hl"]
        stats = sb("stats", [R, TPI, 6])
        mv = sb("mv", [R, TPI, 2])
        rstd = sb("rstd", [R, TPI])
        nt = sb("nt", [R, 2, TPI])
        qz = sb("qz", [128, KC, 4, TOK])
        kT = sb("kT", [128, KC, TOK])
        v = sb("v", [R, TPI, C])
        s_sb = sb("s_sb", [R, 2, 4, NPAIR])
        r_sb = sb("r_sb", [R, 2, 4, NPAIR])
        u_sb = sb("u_sb", [R, 2, 4, NPAIR])
        num = u_sb
        q_sb = sb("q_sb", [R, 4, NPAIR])
        rden = sb("rden", [128, 2, T])
        dt = sb("dt", [128, 2, T])
        q2 = sb("q2", [128, TOK])
        bank = [ctx.enter_context(nc.psum_tensor(f"a_bank{k}", [128, 512], F32)) for k in range(8)]
        gen, sc, pvb = bank[0:2], bank[2:6], bank[6:8]

        w_hi, w_lo = sem("w_hi"), sem("w_lo")
        w_loaded = [sem(f"w_loaded{k}") for k in range(4)]
        const_set, const_ready, zeroed, slope_loaded = sem("const_set"), sem("const_ready"), sem("zeroed"), sem("slope_loaded")
        x_loaded, xr_loaded, x1_stored, q2_stored = sem("x_loaded"), sem("xr_loaded"), sem("x1_stored"), sem("q2_stored")
        stats_made = [sem("stats_made0"), sem("stats_made1")]
        stats_first = sem("stats_first")
        mv_made, root_made, rstd_made = sem("mv_made"), sem("root_made"), sem("rstd_made")
        xn_made = [sem("xn_made0"), sem("xn_made1")]
        newton = [sem(f"newton{k}") for k in range(3)]
        gen_full = sem("gen_full")
        gen_free = [sem("gen_free0"), sem("gen_free1")]
        xT_hi = [sem("xT_hi0"), sem("xT_hi1")]
        oT_hi, oT_lo = sem("oT_hi"), sem("oT_lo")
        q_made = sem("q_made")
        sc_full, s_made, u_made, r_made, p_made, num_made = (sem(n) for n in ("sc_full", "s_made", "u_made", "r_made", "p_made", "num_made"))
        rr_made, m_made, p2_made, y_made = sem("rr_made"), sem("m_made"), sem("p2_made"), sem("y_made")
        pv_full, rs_made, rden_made, o_made = sem("pv_full"), sem("rs_made"), sem("rden_made"), sem("o_made")

        T1, QK, V, T2, Q2, OUT = 0, 4, 12, 16, 20, 24
        USES = 28

        def use(i, u):
            if isinstance(i, int) and i == 0 and u < T2:
                return u
            if isinstance(i, int) and i == NIT:
                return i * USES - 8 + u - T2
            return i * USES - 8 + u

        def times(i, u):
            if isinstance(i, int):
                return use(i, u) // 2 + 1
            return i * (USES // 2) - 4 + u // 2 + 1

        pieces = [(w_qkvT[:, k, :], wqkv, slice(k, k + 1), 3 * C) for k in range(KC)]
        pieces += [(w_outT[:, k, :], wout, slice(k, k + 1), C) for k in range(KC)]
        pieces += [(w_qT[:, k, :], wq2, slice(k, k + 1), C) for k in range(KC)]
        stage = qz[:, :, :, :].rearrange("p a b c -> p (a b c)")
        NST = 4
        STAGE_DVE, STAGE_POOL = 5 * KC * TOK // 2, 3 * KC * TOK // 2

        block = ctx.enter_context(nc.Block())

        @block.sync
        def _(sp):
            sp.dma_start(slope[:], slopes.partition_broadcast(R)).then_inc(slope_loaded, 16)
            for n, (src, dst, ks, w) in enumerate(pieces):
                if n >= NST:
                    sp.wait_ge(w_lo, n - NST + 1)
                sp.dma_start(stage[:, (n % NST) * 3 * C:(n % NST) * 3 * C + w], src).then_inc(w_loaded[n % NST], 16)
                if n == 0:
                    sp.dma_start(x_in[:], x_v[0]).then_inc(x_loaded, 16)
                    sp.dma_start(xr[:], x_v[0]).then_inc(xr_loaded, 16)
            sp.wait_ge(gen_full, use(0, QK))
            sp.dma_start(x_in[:], x_v[1]).then_inc(x_loaded, 16)

            def store_x1(i):
                for j in (2, 3):
                    sp.wait_ge(slope_loaded, 16)
                    sp.wait_ge(gen_free[j % 2], times(i - 1, OUT + j))
                dst = x1_v[i - 1] if isinstance(i, int) else x1_v[bass.ds(i - 1, 1)].rearrange("a r j c -> (a r) j c")
                sp.dma_start(dst, xr[:]).then_inc(x1_stored, 16)

            def store_q2(i):
                for m in range(KC):
                    sp.wait_ge(slope_loaded, 16)
                    sp.wait_ge(gen_free[m % 2], times(i, Q2 + m))
                    dst = q2_v[i - 1, m] if isinstance(i, int) else q2_v[bass.ds(i - 1, 1), m].rearrange("a p b t -> (a p) b t")
                    sp.dma_start(dst, q2[:].rearrange("p (b t) -> p b t", b=2)).then_inc(q2_stored, 16)

            with sp.Fori(1, NIT) as i:
                store_x1(i)
                nxt = sp.snap((i + 1) % NIT)
                sp.wait_ge(slope_loaded, 16)
                sp.wait_ge(x1_stored, i * 16)
                sp.wait_ge(gen_full, use(i, QK))
                sp.dma_start(x_in[:], x_v[bass.ds(nxt, 1)].rearrange("a r j c -> (a r) j c")).then_inc(x_loaded, 16)
                sp.wait_ge(slope_loaded, 16)
                sp.wait_ge(xn_made[1], i * TPI)
                sp.dma_start(xr[:], x_v[bass.ds(i, 1)].rearrange("a r j c -> (a r) j c")).then_inc(xr_loaded, 16)
                store_q2(i)
            store_x1(NIT)
            store_q2(NIT)
            sp.wait_ge(x_loaded, (NIT + 1) * 16)
            sp.wait_ge(x1_stored, NIT * 16)
            sp.wait_ge(q2_stored, NIT * KC * 16)

        @block.gpsimd
        def _(pool):
            pool.iota(dist[:, 0:T], [[-1, T]], base=0, channel_multiplier=1, allow_small_or_imprecise_dtypes=True).then_inc(const_set, 1)
            pool.iota(dist[:, T:], [[-1, R]], base=0, channel_multiplier=1, allow_small_or_imprecise_dtypes=True).then_inc(const_set, 1)
            pool.memset(keep[:], -1.0).then_inc(const_set, 1)
            pool.memset(ident[:], 1.0).then_inc(const_set, 1)
            pool.memset(ones[:], 1.0).then_inc(const_set, 1)
            pool.memset(eps[:, 0:1], LN_EPS).then_inc(const_set, 1)
            pool.memset(eps[:, 1:2], 1.0).then_inc(const_set, 1)
            pool.memset(eps[:, 2:3], 4 * RS_EPS).then_inc(const_set, 1)
            pool.wait_ge(const_set, 8)
            for a, w in ((0, T), (T, R)):
                pool.affine_select(out=keep[:, a:a + w], in_=keep[:, a:a + w], pattern=[[1, w]], compare_op=ALU.is_ge,
                                   fill=0.0, base=0, channel_multiplier=-1).then_inc(const_ready, 1)
            pool.affine_select(out=ident[:], in_=ident[:], pattern=[[1, R]], compare_op=ALU.is_equal, fill=0.0,
                               base=0, channel_multiplier=-1).then_inc(const_ready, 1)
            pool.wait_ge(w_lo, len(pieces))
            pool.memset(stage[:, STAGE_DVE:STAGE_DVE + STAGE_POOL], 0.0).then_inc(zeroed, 1)
            with pool.Fori(0, NIT) as i:
                for n in range(NG):
                    pool.wait_ge(r_made, i * NG + n + 1)
                    pool.tensor_tensor(s_sb[:, n % 2], s_sb[:, n % 2], r_sb[:, n % 2], ALU.mult).then_inc(p_made, 1)

        CONSTS = 3

        def split_lo(eng, lo, src, hi, inc):
            eng.tensor_tensor(lo, src, hi.bitcast(F32), ALU.subtract).then_inc(inc, 1)

        @block.vector
        def _(dve):
            def split_piece(n):
                src, dst, ks, w = pieces[n]
                st = stage[:, (n % NST) * 3 * C:(n % NST) * 3 * C + w]
                dve.wait_ge(w_loaded[n % NST], 16 * (n // NST + 1))
                dve.tensor_copy(dst[0][:, ks.start, :], st).then_inc(w_hi, 1)
                dve.wait_ge(w_hi, n + 1)
                dve.tensor_tensor(dst[1][:, ks.start, :], st, dst[0][:, ks.start, :].bitcast(F32), ALU.subtract).then_inc(w_lo, 1)

            def layernorm(n, src, dst, xn_sem, before=None):
                for j in range(TPI):
                    dve.bn_aggr(mv[:, j, :], stats[:, j, :]).then_inc(mv_made, 1)
                dve.wait_ge(root_made, n + 1)
                dve.tensor_tensor(nt[:, 0, :], rstd[:], rstd[:], ALU.mult).then_inc(newton[0], 1)
                dve.wait_ge(newton[0], n + 1)
                dve.scalar_tensor_tensor(nt[:, 1, :], mv[:, :, 1], LN_EPS, nt[:, 0, :], ALU.add, ALU.mult).then_inc(newton[1], 1)
                dve.wait_ge(newton[1], n + 1)
                dve.tensor_scalar(nt[:, 0, :], nt[:, 1, :], -0.5, 1.5, ALU.mult, ALU.add).then_inc(newton[2], 1)
                dve.wait_ge(newton[2], n + 1)
                dve.tensor_tensor(rstd[:], rstd[:], nt[:, 0, :], ALU.mult).then_inc(rstd_made, 1)
                for j in range(TPI):
                    if j == 0:
                        if before:
                            dve.wait_ge(*before)
                        dve.wait_ge(rstd_made, n + 1)
                    dve.tensor_scalar(dst[:, j, :], src[:, j, :], mv[:, j, 0:1], rstd[:, j:j + 1], ALU.subtract, ALU.mult).then_inc(xn_sem, 1)

            def transposed_lo(i, base, half):
                for c in range(KC):
                    dve.wait_ge(xT_hi[half], i * KC + c + 1)
                    dve.tensor_tensor(xT[1][:, c, :], gen[c % 2][:, 0:TOK], xT[0][:, c, :].bitcast(F32),
                                      ALU.subtract).then_inc(gen_free[c % 2], 1)

            def first_layernorm(n, src_loaded, done, value):
                dve.wait_ge(x_loaded, src_loaded)
                for j in range(TPI):
                    ins = dve.bn_stats(stats[:, j, :], x_in[:, j, :])
                ins.then_inc(done, 1)
                dve.wait_ge(const_ready, CONSTS)
                dve.wait_ge(done, value)
                layernorm(n, x_in, x_in, xn_made[0])

            def second_layernorm(i):
                for j in range(TPI):
                    dve.wait_ge(gen_free[j % 2], times(i - 1, OUT + j))
                    ins = dve.bn_stats(stats[:, j, :], xr[:, j, :])
                ins.then_inc(stats_made[1], 1)
                dve.wait_ge(const_ready, CONSTS)
                dve.wait_ge(stats_made[1], i)
                layernorm(i * 2, xr, xn, xn_made[1])

            for n in range(KC):
                split_piece(n)
            dve.wait_ge(slope_loaded, 16)
            first_layernorm(0, 16, stats_first, 1)
            for n in range(KC, len(pieces)):
                split_piece(n)
            dve.wait_ge(w_lo, len(pieces))
            dve.memset(stage[:, 0:STAGE_DVE], 0.0).then_inc(zeroed, 1)

            def body(i, first):
                transposed_lo(i, T1, 0)
                if not first:
                    second_layernorm(i)
                for m in range(KC):
                    u = QK + KC + m
                    dve.wait_ge(gen_full, use(i, u) + 1)
                    dve.tensor_copy(kT[:, m, :], gen[u % 2][:, 0:TOK]).then_inc(gen_free[u % 2], 1)

                def score(n):
                    b, g = divmod(n, 4)
                    if n == 0:
                        dve.wait_ge(num_made, i * NG)
                    elif n >= 2:
                        dve.wait_ge(num_made, i * NG + n - 1)
                    for r in range(4):
                        dve.wait_ge(sc_full, i * 32 + 4 * n + r + 1)
                        dve.scalar_tensor_tensor(s_sb[:, n % 2, r, :], dist[:], slope[:, 4 * g + r:4 * g + r + 1],
                                                 sc[r][0:R, 0:NPAIR], ALU.mult, ALU.add).then_inc(s_made, 1)

                def numerator(n):
                    dve.wait_ge(rr_made, i * NG + n + 1)
                    dve.scalar_tensor_tensor(u_sb[:, n % 2], u_sb[:, n % 2], 1.0, q_sb[:], ALU.add, ALU.mult).then_inc(m_made, 1)
                    dve.wait_ge(p_made, i * NG + n + 1)
                    dve.wait_ge(m_made, i * NG + n + 1)
                    dve.scalar_tensor_tensor(s_sb[:, n % 2], u_sb[:, n % 2], 3.0, s_sb[:, n % 2], ALU.subtract, ALU.mult).then_inc(p2_made, 1)
                    dve.wait_ge(p2_made, i * NG + n + 1)
                    dve.scalar_tensor_tensor(num[:, n % 2], s_sb[:, n % 2], 2.0,
                                             keep[:, None, :].broadcast_to([R, 4, NPAIR]), ALU.subtract, ALU.mult).then_inc(num_made, 1)

                def output(n):
                    b, g = divmod(n, 4)
                    dve.wait_ge(rden_made, i * NG + n + 1)
                    dve.wait_ge(o_made, i * NG + n)
                    dve.scalar_tensor_tensor(dt[:, 0, :], pvb[n % 2][:, T:2 * T], 4 * RS_EPS, rden[:, n % 2], ALU.add, ALU.mult).then_inc(y_made, 1)
                    dve.tensor_tensor(dt[:, 1, :], pvb[n % 2][:, 0:T], rden[:, n % 2], ALU.mult).then_inc(y_made, 1)
                    dve.wait_ge(y_made, i * (2 * NG) + 2 * n + 2)
                    dve.scalar_tensor_tensor(oT[:, g, b * T:(b + 1) * T], dt[:, 0, :], 2.0, dt[:, 1, :], ALU.subtract, ALU.mult).then_inc(o_made, 1)

                def split_outputs(b):
                    for c in range(KC):
                        dve.wait_ge(oT_hi, i * (2 * KC) + KC * b + c + 1)
                        dve.tensor_tensor(xT[1][:, c, b * T:b * T + T], oT[:, c, b * T:b * T + T],
                                          xT[0][:, c, b * T:b * T + T].bitcast(F32), ALU.subtract).then_inc(oT_lo, 1)

                def residual(j):
                    u = OUT + j
                    if j == 0:
                        dve.wait_ge(xr_loaded, i * 16 + 16)
                    dve.wait_ge(gen_full, use(i, u) + 1)
                    dve.tensor_tensor(xr[:, j, :], xr[:, j, :], gen[u % 2][0:R, :], ALU.subtract).then_inc(gen_free[u % 2], 1)

                score(0)
                if first:
                    first_layernorm(1, 32, stats_first, 2)
                else:
                    first_layernorm(i * 2 + 1, i * 16 + 32, stats_made[0], i)
                score(1)
                if not first:
                    transposed_lo(i - 1, T2, 1)
                for n in range(1, NG + 2):
                    if 2 <= n < NG:
                        score(n)
                    if n <= NG:
                        numerator(n - 1)
                    if n == NG - 1:
                        split_outputs(0)
                    if n >= 2:
                        output(n - 2)
                    if n == NG:
                        residual(0)
                        residual(1)
                split_outputs(1)
                residual(2)
                residual(3)

            body(0, True)
            with dve.Fori(1, NIT) as i:
                body(i, False)
            second_layernorm(NIT)
            transposed_lo(NIT - 1, T2, 1)

        @block.scalar
        def _(act):
            act.wait_ge(const_ready, CONSTS)

            def rstd_of(n):
                act.wait_ge(mv_made, n * TPI + TPI)
                act.activation(rstd[:], mv[:, :, 1], ACT.Abs_reciprocal_sqrt, bias=eps[0:R, 0:1]).then_inc(root_made, 1)

            def transposed_hi(i, base, half):
                for c in range(KC):
                    act.wait_ge(gen_full, use(i, base + c) + 1)
                    act.copy(xT[0][:, c, :], gen[c % 2][:, 0:TOK]).then_inc(xT_hi[half], 1)

            def queries_out(i, m):
                u = Q2 + m
                act.wait_ge(gen_full, use(i, u) + 1)
                act.wait_ge(q2_stored, i * (16 * KC) - 16 * KC + 16 * m)
                act.mul(q2[:], gen[u % 2][:, 0:TOK], D2 ** -0.5).then_inc(gen_free[u % 2], 1)

            rstd_of(0)

            def body(i, first):
                transposed_hi(i, T1, 0)
                if not first:
                    rstd_of(i * 2)
                if first:
                    act.wait_ge(zeroed, 2)
                for m in range(KC):
                    u = QK + m
                    act.wait_ge(gen_full, use(i, u) + 1)
                    for r in range(4):
                        ins = act.mul(qz[32 * r:32 * r + 32, m, r, :], gen[u % 2][32 * r:32 * r + 32, 0:TOK], D1 ** -0.5)
                        ins.then_inc(gen_free[u % 2] if r == 3 else q_made, 1)

                def root(n):
                    if n >= 2:
                        act.wait_ge(pv_full, i * NG + n - 1)
                    act.wait_ge(s_made, i * 32 + 4 * n + 4)
                    act.activation(u_sb[:, n % 2], s_sb[:, n % 2], ACT.Square).then_inc(u_made, 1)
                    act.wait_ge(u_made, i * NG + n + 1)
                    act.activation(r_sb[:, n % 2], u_sb[:, n % 2], ACT.Abs_reciprocal_sqrt, bias=eps[0:R, 1:2]).then_inc(r_made, 1)
                    act.wait_ge(r_made, i * NG + n + 1)
                    if n >= 1:
                        act.wait_ge(m_made, i * NG + n)
                    act.activation(q_sb[:], r_sb[:, n % 2], ACT.Square).then_inc(rr_made, 1)

                def reciprocal(n):
                    act.wait_ge(pv_full, i * NG + n + 1)
                    if n >= 2:
                        act.wait_ge(o_made, i * NG + n - 1)
                    act.activation(rden[:, n % 2], pvb[n % 2][:, T:2 * T], ACT.Abs_reciprocal_sqrt, bias=eps[:, 2:3]).then_inc(rs_made, 1)
                    act.wait_ge(rs_made, i * NG + n + 1)
                    act.activation(rden[:, n % 2], rden[:, n % 2], ACT.Square).then_inc(rden_made, 1)

                def split_outputs(b):
                    for c in range(KC):
                        act.wait_ge(o_made, i * NG + 4 * b + c + 1)
                        act.copy(xT[0][:, c, b * T:b * T + T], oT[:, c, b * T:b * T + T]).then_inc(oT_hi, 1)

                def values_in(j):
                    u = V + j
                    act.wait_ge(gen_full, use(i, u) + 1)
                    act.copy(v[:, j, :], gen[u % 2][0:R, :]).then_inc(gen_free[u % 2], 1)

                root(0)
                values_in(0)
                values_in(1)
                rstd_of(i * 2 + 1)
                values_in(2)
                values_in(3)
                if not first:
                    transposed_hi(i, T2, 1)
                for n in range(1, NG + 2):
                    if n < NG:
                        root(n)
                    if n >= 2:
                        reciprocal(n - 2)
                    if n <= KC and not first:
                        queries_out(i, n - 1)
                    if n == NG - 2:
                        split_outputs(0)
                split_outputs(1)

            body(0, True)
            with act.Fori(1, NIT) as i:
                body(i, False)
            rstd_of(NIT * 2)
            transposed_hi(NIT, T2, 1)
            for m in range(KC):
                queries_out(NIT, m)

        @block.tensor
        def _(pe):
            def bank_free(i, u):
                if not (isinstance(i, int) and use(i, u) < 2):
                    pe.wait_ge(gen_free[u % 2], times(i, u) - 1)

            def transposes(i, base, half, src, count):
                pe.wait_ge(xn_made[half], count)
                for c in range(KC):
                    bank_free(i, base + c)
                    for j in range(TPI):
                        mm = pe.transpose(gen[c % 2][:, R * j:R * j + R], src[:, j, 128 * c:128 * c + 128], ident[:])
                    mm.then_inc(gen_full, 1)

            def product(out, lhs, rhs, n=KC):
                steps = [(a, b, k) for a, b in ((0, 0), (0, 1), (1, 0)) for k in range(n)]
                for q, (a, b, k) in enumerate(steps):
                    mm = pe.matmul(out, lhs(a, k), rhs(b, k), start=q == 0, stop=q == len(steps) - 1)
                return mm

            pe.wait_ge(const_ready, CONSTS)
            pe.wait_ge(w_lo, KC)

            def queries(i, m):
                for b in range(2):
                    if m == 0:
                        pe.wait_ge(gen_free[b], times(i, T2 + 2 + b))
                bank_free(i, Q2 + m)
                product(gen[m % 2][:, 0:TOK], lambda a, k: wq2[a][:, k, 128 * m:128 * m + 128],
                        lambda b, k: xT[b][:, k, :]).then_inc(gen_full, 1)

            def body(i, first):
                transposes(i, T1, 0, x_in, i * TPI + TPI)
                pe.wait_ge(gen_free[0], times(i, T1 + 2))
                pe.wait_ge(gen_free[1], times(i, T1 + 3))
                for m in range(8):
                    bank_free(i, QK + m)
                    product(gen[m % 2][:, 0:TOK], lambda a, k: wqkv[a][:, k, 128 * m:128 * m + 128],
                            lambda b, k: xT[b][:, k, :]).then_inc(gen_full, 1)

                def project_values(j):
                    bank_free(i, V + j)
                    product(gen[j % 2][0:R, :], lambda a, k: xT[a][:, k, R * j:R * j + R],
                            lambda b, k: wqkv[b][:, k, 2 * C:3 * C]).then_inc(gen_full, 1)

                def project_outputs(j):
                    pe.wait_ge(oT_lo, i * (2 * KC) + KC + KC * (j // 2))
                    bank_free(i, OUT + j)
                    product(gen[j % 2][0:R, :], lambda a, k: xT[a][:, k, R * j:R * j + R],
                            lambda b, k: wout[b][:, k, :]).then_inc(gen_full, 1)

                def scores(n):
                    b, g = divmod(n, 4)
                    if n == 0:
                        for e in range(2):
                            pe.wait_ge(gen_free[e], times(i, V - 2 + e))
                    for r in range(4):
                        if n >= 1:
                            pe.wait_ge(s_made, i * 32 + 4 * (n - 1) + r + 1)
                        t0 = b * T
                        pe.matmul(sc[r][0:R, 0:T], kT[:, g, t0:t0 + R], qz[:, g, r, t0:t0 + T], start=True, stop=True)
                        pe.matmul(sc[r][0:R, T:NPAIR], kT[:, g, t0 + R:t0 + T], qz[:, g, r, t0 + R:t0 + T],
                                  start=True, stop=True).then_inc(sc_full, 1)

                def values(n):
                    b, g = divmod(n, 4)
                    if n == 0:
                        for e in range(2):
                            pe.wait_ge(gen_free[e], times(i, V + 2 + e))
                    pe.wait_ge(num_made, i * NG + n + 1)
                    if n >= 2:
                        pe.wait_ge(o_made, i * NG + n - 1)
                    for den in range(2):
                        for st in range(2):
                            for r in range(4):
                                h = 4 * g + r
                                lhs = ones[:] if den else v[:, 2 * b + st, 32 * h:32 * h + 32]
                                o0 = den * T
                                if st == 0:
                                    mm = pe.matmul(pvb[n % 2][32 * r:32 * r + 32, o0:o0 + T], lhs, num[:, n % 2, r, 0:T],
                                                   start=True, stop=False, tile_position=(0, 32 * r))
                                else:
                                    mm = pe.matmul(pvb[n % 2][32 * r:32 * r + 32, o0 + R:o0 + T], lhs,
                                                   num[:, n % 2, r, T:NPAIR], start=False, stop=True, tile_position=(0, 32 * r))
                    mm.then_inc(pv_full, 1)

                scores(0)
                if first:
                    pe.wait_ge(w_lo, len(pieces))
                project_values(0)
                project_values(1)
                scores(1)
                project_values(2)
                project_values(3)
                if not first:
                    transposes(i, T2, 1, xn, i * TPI)
                for n in range(1, NG + 1):
                    if n + 1 < NG:
                        scores(n + 1)
                    values(n - 1)
                    if n <= KC and not first:
                        queries(i, n - 1)
                    if n == NG - 1:
                        project_outputs(0)
                        project_outputs(1)
                project_outputs(2)
                project_outputs(3)

            body(0, True)
            with pe.Fori(1, NIT) as i:
                body(i, False)
            transposes(NIT, T2, 1, xn, NIT * TPI)
            for m in range(KC):
                queries(NIT, m)


def cross_attention(nc, ctxT, mask, q2_dram, x1_dram, w_k, w_v, w_o, b_o, w_r, bias, out, xn_dram, table_dram):
    NJ = J // JB
    mask = mask.bitcast(U8).rearrange("(i j) -> i j", j=J)
    NH = 2 * H2
    NM = H2 // 2
    x1_v = x1_dram.rearrange("(i j r) c -> i r j c", j=2, r=R)
    out_v = out[0:B * T].rearrange("(i j r) c -> i r j c", j=2, r=R)
    xn_v = xn_dram[0:B * T].rearrange("(i j r) c -> i r j c", j=2, r=R)
    with ExitStack() as ctx:
        sb = lambda n, s, d=F32: ctx.enter_context(nc.sbuf_tensor("c_" + n, s, d))
        sem = lambda n: ctx.enter_context(nc.semaphore("c_" + n))
        wk = [sb(f"wk{k}", [128, CC, C], F32R) for k in "hl"]
        wv = [sb(f"wv{k}", [128, CC, C], F32R) for k in "hl"]
        wo = [sb(f"wo{k}", [128, KC, C], F32R) for k in "hl"]
        wr = sb("wr", [128, KC, E])
        bo, bi = sb("bo", [R, C]), sb("bi", [R, C])
        ident = sb("ident", [R, R])
        craw = sb("craw", [128, CC, J])
        cT = [sb(f"cT{k}", [128, CC, J], F32R) for k in "hl"]
        kT = [sb(f"kT{k}", [128, NM, J], F32R) for k in "hl"]
        v = [sb(f"v{k}", [JB, NJ, C], F32R) for k in "hl"]
        q2 = sb("q2", [128, KC, T])
        qz = [sb(f"qz{k}", [128, H2, T], F32R) for k in "hl"]
        m8 = sb("m8", [R, J], U8)
        mb = sb("mb", [R, J])
        s_sb = sb("s_sb", [R, 4, J])
        mx, nmx, den, rec = (sb(n, [R, NH]) for n in ("mx", "nmx", "den", "rec"))
        pT = [sb(f"pT{k}", [JB, 2, NJ, T], F32R) for k in "hl"]
        oT = [sb(f"oT{k}", [128, KC, T], F32R) for k in "hl"]
        x1 = sb("x1", [R, 2, C])
        xo = sb("xo", [R, 2, C])
        xn = sb("xn", [R, 2, C])
        xnT = sb("xnT", [128, 2, KC * R])
        stats, mv, rstd, nt = sb("stats", [R, 2, 6]), sb("mv", [R, 2, 2]), sb("rstd", [R, 2]), sb("nt", [R, 2, 2])
        eps = sb("eps", [R, 1])
        L2 = [R, 2, E]
        lg, sc, rank, sel, off, inv, base = (sb(n, L2) for n in ("lg", "sc", "rank", "sel", "off", "inv", "base"))
        selb = sb("selb", L2, BF16)
        lmx, lsum, lrec = (sb(n, [R, 2]) for n in ("lmx", "lsum", "lrec"))
        gt, ge = sb("gt", [R, 2, E, E]), sb("ge", [R, 2, E, E])
        lower = sb("lower", [R, E, E])
        before = sb("before", [R, R], BF16)
        onesb = sb("onesb", [R, R], BF16)
        e896 = sb("e896", [R, E])
        kk = sb("kk", [R, 2, E])
        oh, ohs = sb("oh", [R, 2, 2, E]), sb("ohs", [R, 2, 2, E])
        slotf, slotu = sb("slotf", [R, 4]), sb("slotu", [R, 4], U32)
        tok, tstep = sb("tok", [R, 4]), sb("tstep", [R, 4])
        pay = sb("pay", [R, 4, 2])
        trash = sb("trash", [128, E, CAP // 128, 2])
        zero = sb("zero", [128, C])

        ROUTE = 21

        psum = ctx.enter_context(nc.psum_tensor("c_psum", [128, 8, 512], F32))
        scb = [psum[:, 0:2], psum[:, 2:4]]
        ptb = psum[:, 4:6]
        ob, gen = psum[:, 6], psum[:, 7]
        JH = J // 2
        HW = JH + 1

        def score_view(h):
            flat = psum[0:R].rearrange("p b c -> p (b c)")
            return flat[:, 1024 * (h % 2):1024 * (h % 2) + 1026].rearrange("p (a j) -> p a j", a=2)[:, :, 0:JH]

        K, V = (lambda m, a: ("K", m, a)), (lambda g, a: ("V", g, a))
        PLAN = {1: ([], [], [V(1, 0)]), 2: ([], [V(1, 1)], []), 3: ([], [V(1, 2)], [("OUT", 0, 0)]), 4: ([], [("OUT", 1, 0)], []),
                5: ([], [K(0, 0)], []), 6: ([K(0, 1)], [], [("XT", 0, 0)]), 7: ([], [K(1, 0)], [("XT", 1, 0)]),
                8: ([K(1, 1)], [("RT", 0, 0)], []), 9: ([], [], [V(0, 0)]), 10: ([], [V(0, 1)], [("PRE", 0, 0)]),
                11: ([], [V(0, 2)], []), 12: ([], [K(2, 0)], []), 13: ([], [K(2, 1)], []), 14: ([], [K(3, 0)], []), 15: ([], [K(3, 1)], [])}
        START = [K(m, a) for m in range(NM) for a in range(2)] + [V(0, a) for a in range(3)]

        def units(kind, s, slots=(0, 1, 2)):
            def has(unit):
                projection, late = unit[0] in ("K", "V"), unit[:2] == ("V", 1)
                return {"first": projection, "mid": True, "last": late or not projection, "end": not projection}[kind]
            return [u for slot in slots for u in (PLAN[s][slot] if s in PLAN else []) if has(u)]

        ORDER = {k: [u for s in range(NH) for u in units(k, s)] for k in ("first", "mid", "last", "end")}
        ORDER["start"] = START
        SPLIT = {k: [u for u in us if u[0] in ("K", "V")] for k, us in ORDER.items()}

        def projections(kind, s, slot):
            return [u for u in units(kind, s, (slot,)) if u[0] in ("K", "V")]

        def number(lists, i, kind, unit):
            n, first, mid, last = (len(lists[k]) for k in ("start", "first", "mid", "last"))
            at = lists[kind].index(unit)
            if kind == "start":
                return at
            if kind == "first":
                return n + at
            if kind == "end":
                return n + first + (B - 2) * mid + last + at
            return i * mid + (n + first - mid + at)

        K0, KW = (0, HW), (HW, J - HW)

        def unit_places(unit):
            what, m, a = unit
            if what == "K":
                return lambda part: kT[part][:, m, K0[a]:K0[a] + KW[a]], gen[:, 0:KW[a]]
            if what == "V":
                return lambda part: v[part][:, 2 * a:2 * a + 2, 256 * m:256 * m + 256], gen[0:JB].rearrange("p (b c) -> p b c", b=2)

        def probs_view(part, h):
            t0 = (h % 2) * R
            return pT[part][:, (h // 2) % 2, :, t0:t0 + R].rearrange("p (b k) t -> p b k t", b=2)

        pt_view = ptb[0:JB, :, 0:3 * R].rearrange("p b (k t) -> p b k t", k=3)

        w_loaded = [sem(f"w_loaded{k}") for k in range(3)]
        w_hi, w_lo = sem("w_hi"), sem("w_lo")
        small_loaded, const_set, const_ready, zeroed = sem("small_loaded"), sem("const_set"), sem("const_ready"), sem("zeroed")
        trash_set, trash_ready, trash_stored = sem("trash_set"), sem("trash_ready"), sem("trash_stored")
        c_loaded, q_loaded, m_loaded, x_loaded = sem("c_loaded"), sem("q_loaded"), sem("m_loaded"), sem("x_loaded")
        xn_stored, out_stored = sem("xn_stored"), sem("out_stored")
        c_hi, c_lo, qz_hi, qz_lo, mb_made = sem("c_hi"), sem("c_lo"), sem("qz_hi"), sem("qz_lo"), sem("mb_made")
        gen_full, gen_hi, gen_free = sem("gen_full"), sem("gen_hi"), sem("gen_free")
        s_full, s_masked, nmx_made, e_made = sem("s_full"), sem("s_masked"), sem("nmx_made"), sem("e_made")
        pt_full, p_hi, p_lo = sem("pt_full"), sem("p_hi"), sem("p_lo")
        rec_made, p_made = sem("rec_made"), sem("p_made")
        pv_full, o_hi, o_lo = sem("pv_full"), sem("o_hi"), sem("o_lo")
        x1b_made, xo_made = sem("x1b_made"), sem("xo_made")
        stats_made, mv_made, root_made, rstd_made, xn_made = (sem(n) for n in ("stats_made", "mv_made", "root_made", "rstd_made", "xn_made"))
        newton = sem("newton")
        lg_made, le_made, route, sel_made, slots_made, sent = (sem(n) for n in ("lg_made", "le_made", "route", "sel_made", "slots_made", "sent"))

        pieces = [(w_k, wk, k) for k in range(CC)] + [(w_v, wv, k) for k in range(CC)] + [(w_o, wo, k) for k in range(KC)]
        block = ctx.enter_context(nc.Block())

        def iterations(eng, body):
            body(0, "first")
            with eng.Fori(1, B - 1) as i:
                body(i, "mid")
            body(B - 1, "last")

        def step(i, s):
            return (i, s) if s < NH else (i + 1, s - NH)

        def has_step(kind, s):
            return s < NH or kind != "last"

        def wait_apart(eng, semaphore, value):
            eng.wait_ge(small_loaded, 48)
            eng.wait_ge(semaphore, value)

        @block.sync
        def _(sp):
            for n, (src, dst, k) in enumerate(pieces):
                if n >= 3:
                    sp.wait_ge(w_lo, n - 2)
                sp.dma_start(craw[:, n % 3, 0:C], src[:, k, :]).then_inc(w_loaded[n % 3], 16)
            for dst, src in ((wr[:], w_r), (bo[:], b_o.partition_broadcast(R)), (bi[:], bias.partition_broadcast(R))):
                sp.dma_start(dst, src).then_inc(small_loaded, 16)
            sp.wait_ge(w_lo, 10)
            one = lambda t, i: t[i] if isinstance(i, int) else t[bass.ds(i, 1)]

            def flat(t, names):
                return t if len(t.shape) == 3 else t.rearrange(f"a {names} -> (a {names[0]}) {names[2:]}")

            def load_context(i):
                sp.dma_start(craw[:], flat(one(ctxT, i), "p k j")).then_inc(c_loaded, 16)

            def load_mask(i):
                row = mask[i:i + 1] if isinstance(i, int) else mask[bass.ds(i, 1)]
                sp.dma_start(m8[:], row.rearrange("a j -> (a j)").partition_broadcast(R)).then_inc(m_loaded, 16)

            def load_queries(i):
                sp.dma_start(q2[:], flat(one(q2_dram, i), "p k t")).then_inc(q_loaded, 16)

            load_context(0)
            load_queries(0)
            load_mask(0)
            sp.dma_start(x1[:], x1_v[0]).then_inc(x_loaded, 16)
            sp.wait_ge(trash_ready, 2)
            sp.dma_start(table_dram.rearrange("(e p n) w -> p e n w", e=E, n=CAP // 128), trash[:]).then_inc(trash_stored, 16)
            for k in range(CAP // 128):
                r0 = B * T + 128 * k
                sp.dma_start(xn_dram[r0:r0 + 128, :], zero[:]).then_inc(trash_stored, 16)
                sp.dma_start(out[r0:r0 + 128, :], zero[:]).then_inc(trash_stored, 16)
            sp.wait_ge(c_lo, CC)
            load_context(1)
            sp.wait_ge(qz_lo, 4)
            load_queries(1)
            sp.wait_ge(mb_made, 1)
            load_mask(1)

            def store(i):
                wait_apart(sp, xo_made, i)
                sp.dma_start(flat(one(out_v, i - 1), "r j c"), xo[:]).then_inc(out_stored, 16)
                wait_apart(sp, xn_made, i * 2)
                sp.dma_start(flat(one(xn_v, i - 1), "r j c"), xn[:]).then_inc(xn_stored, 16)

            def body(i, kind, more):
                if more:
                    wait_apart(sp, c_lo, i * CC + 2 * CC)
                    load_context(i + 2)
                if kind != "first":
                    store(i)
                    sp.dma_start(x1[:], flat(one(x1_v, i), "r j c")).then_inc(x_loaded, 16)
                if more:
                    wait_apart(sp, qz_lo, i * 4 + 8)
                    load_queries(i + 2)
                    wait_apart(sp, mb_made, i + 2)
                    load_mask(i + 2)

            body(0, "first", True)
            with sp.Fori(1, B - 2) as i:
                body(i, "mid", True)
            for i in range(B - 2, B):
                body(i, "last", False)
            store(B)
            sp.wait_ge(out_stored, 16 * B)
            sp.wait_ge(xn_stored, 16 * B)
            sp.wait_ge(sent, 64 * B)

        @block.gpsimd
        def _(pool):
            for t, val in ((ident, 1.0), (onesb, 1.0), (before, 1.0), (lower, 1.0), (eps, LN_EPS), (tstep, float(T)), (base, 0.0)):
                pool.memset(t[:], val).then_inc(const_set, 1)
            for j in range(2):
                pool.memset(kk[:, j, :], float(j)).then_inc(const_set, 1)
                pool.iota(tok[:, 2 * j:2 * j + 2], [[0, 2]], base=j * R - T, channel_multiplier=1,
                          allow_small_or_imprecise_dtypes=True).then_inc(const_set, 1)
            pool.iota(e896[:], [[CAP, E]], base=0, channel_multiplier=0, allow_small_or_imprecise_dtypes=True).then_inc(const_set, 1)
            pool.wait_ge(const_set, 12)
            pool.affine_select(out=ident[:], in_=ident[:], pattern=[[1, R]], compare_op=ALU.is_equal, fill=0.0,
                               base=0, channel_multiplier=-1).then_inc(const_ready, 1)
            pool.affine_select(out=before[:], in_=before[:], pattern=[[1, R]], compare_op=ALU.is_gt, fill=0.0,
                               base=0, channel_multiplier=-1).then_inc(const_ready, 1)
            pool.affine_select(out=lower[:], in_=lower[:], pattern=[[1, E], [-1, E]], compare_op=ALU.is_gt, fill=0.0,
                               base=0, channel_multiplier=0).then_inc(const_ready, 1)
            pool.memset(trash[:], 0.0).then_inc(trash_set, 1)
            pool.memset(zero[:], 0.0).then_inc(trash_ready, 1)
            pool.wait_ge(trash_set, 1)
            pool.iota(trash[:, :, :, 0].bitcast(I32), [[0, E], [1, CAP // 128]], base=B * T,
                      channel_multiplier=CAP // 128).then_inc(trash_ready, 1)

            def split_context(i, *ks):
                for k in ks or range(CC):
                    pool.wait_ge(c_hi, i * CC + k + 1)
                    pool.tensor_tensor(cT[1][:, k, :], craw[:, k, :], cT[0][:, k, :].bitcast(F32), ALU.subtract).then_inc(c_lo, 1)

            def add_bias(i):
                pool.wait_ge(x_loaded, i * 16 + 16)
                pool.tensor_tensor(x1[:], x1[:], bo[:, None, :].broadcast_to([R, 2, C]), ALU.add).then_inc(x1b_made, 1)

            def tail(i, kind, s):
                if s == 8:
                    pool.wait_ge(out_stored, i * 16 - 16)
                    pool.wait_ge(gen_free, number(ORDER, i, kind, ("OUT", 1, 0)) + 1)
                    pool.tensor_tensor(xo[:], x1[:], bi[:, None, :].broadcast_to([R, 2, C]), ALU.add).then_inc(xo_made, 1)
                if s == 14 and kind != "end":
                    add_bias(i)
                if s != 12:
                    return
                wait_apart(pool, slots_made, i)
                for q in range(4):
                    pool.indirect_dma_start(out=table_dram, out_offset=bass.IndirectOffsetOnAxis(ap=slotu[:, q:q + 1], axis=0),
                                            in_=pay[:, q, :], in_offset=None, bounds_check=E * CAP - 1, oob_is_err=False).then_inc(sent, 16)

            def normalise(i, h):
                pool.wait_ge(rec_made, i * NH + h + 1)
                pool.tensor_tensor(s_sb[:, h % 4, :], s_sb[:, h % 4, :], rec[:, h:h + 1].broadcast_to([R, J]), ALU.mult).then_inc(p_made, 1)

            split_context(0)
            pool.wait_ge(small_loaded, 48)
            add_bias(0)
            pool.wait_ge(trash_stored, 16 * 15)
            normalise(0, 0)

            def body(i, kind):
                for s in range(NH):
                    if has_step(kind, s + 1):
                        normalise(*step(i, s + 1))
                    if s in (3, 4) and kind != "last":
                        split_context(i + 1, *((0, 1) if s == 3 else (2,)))
                    if kind != "first":
                        tail(i, kind, s)

            iterations(pool, body)
            for s in range(NH):
                tail(B, "end", s)

        @block.vector
        def _(dve):
            for n, (src, dst, k) in enumerate(pieces):
                dve.wait_ge(w_loaded[n % 3], 16 * (n // 3 + 1))
                dve.tensor_copy(dst[0][:, k, :], craw[:, n % 3, 0:C]).then_inc(w_hi, 1)
                dve.wait_ge(w_hi, n + 1)
                dve.tensor_tensor(dst[1][:, k, :], craw[:, n % 3, 0:C], dst[0][:, k, :].bitcast(F32), ALU.subtract).then_inc(w_lo, 1)
            for k in range(2):
                dve.memset(qz[k][:].bitcast(F32), 0.0).then_inc(zeroed, 1)
            dve.wait_ge(zeroed, 2)
            dve.wait_ge(const_ready, 3)
            dve.wait_ge(const_set, 12)
            dve.wait_ge(small_loaded, 48)

            def mask_of(i):
                dve.wait_ge(m_loaded, i * 16 + 16)
                dve.tensor_scalar(mb[:], m8[:], 1.0, FLT_MAX, ALU.subtract, ALU.mult).then_inc(mb_made, 1)

            def inverse_sum(i, h):
                dve.wait_ge(e_made, i * NH + h + 1)
                dve.reciprocal(rec[:, h:h + 1], den[:, h:h + 1]).then_inc(rec_made, 1)

            def masked(i, h):
                half = lambda t: t.rearrange("p (a j) -> p a j", a=2)
                nc.vector.tensor_tensor_reduce(out=half(s_sb[:, h % 4, :]), in0=score_view(h), in1=half(mb[:]),
                                               scale=1.0, scalar=-FLT_MAX, op0=ALU.add, op1=ALU.max,
                                               accum_out=mx[:, h:h + 1]).then_inc(s_masked, 1)
                dve.wait_ge(s_masked, i * NH + h + 1)
                dve.tensor_scalar(nmx[:, h:h + 1], mx[:, h:h + 1], -1.0, None, ALU.mult).then_inc(nmx_made, 1)

            def lo_of_queries(i, g):
                for e in range(2):
                    p0 = 64 * e
                    dve.wait_ge(qz_hi, i * 4 + 2 * g + e + 1)
                    dve.tensor_tensor(qz[1][p0:p0 + 64, 4 * g + e:4 * g + 4:2, :], q2[p0:p0 + 64, 2 * g:2 * g + 2],
                                      qz[0][p0:p0 + 64, 4 * g + e:4 * g + 4:2, :].bitcast(F32), ALU.subtract).then_inc(qz_lo, 1)

            def lo_of_unit(i, kind, unit):
                what, m, a = unit
                dve.wait_ge(gen_hi, number(SPLIT, i, kind, unit) + 1)
                dst, src = unit_places(unit)
                dve.tensor_tensor(dst(1), src, dst(0).bitcast(F32), ALU.subtract).then_inc(gen_free, 1)

            def lo_of_probs(i, h):
                dve.wait_ge(p_hi, i * NH + h + 1)
                dve.tensor_tensor(probs_view(1, h), pt_view, probs_view(0, h).bitcast(F32), ALU.subtract).then_inc(p_lo, 1)

            def lo_of_outputs(i, m):
                for e in range(2):
                    p0 = 64 * e
                    dve.wait_ge(o_hi, i * H2 + 2 * m + e + 1)
                    dve.tensor_tensor(oT[1][p0:p0 + 64, m, :], ob[p0:p0 + 64, e * T:e * T + T], oT[0][p0:p0 + 64, m, :].bitcast(F32),
                                      ALU.subtract).then_inc(o_lo, 1)

            def residual(i, kind, j):
                if j == 0:
                    wait_apart(dve, x1b_made, i)
                dve.wait_ge(gen_full, number(ORDER, i, kind, ("OUT", j, 0)) + 1)
                dve.tensor_tensor(x1[:, j, :], x1[:, j, :], gen[0:R, :], ALU.add).then_inc(gen_free, 1)
                if j == 0:
                    return
                for j in range(2):
                    wait_apart(dve, gen_free, number(ORDER, i, kind, ("OUT", j, 0)) + 1)
                    ins = dve.bn_stats(stats[:, j, :], x1[:, j, :])
                ins.then_inc(stats_made, 1)
                wait_apart(dve, stats_made, i)
                for j in range(2):
                    dve.bn_aggr(mv[:, j, :], stats[:, j, :]).then_inc(mv_made, 1)

            def layernorm(i):
                dve.wait_ge(root_made, i)
                dve.tensor_tensor(nt[:, 0, :], rstd[:], rstd[:], ALU.mult).then_inc(newton, 1)
                dve.wait_ge(newton, i * 3 - 2)
                dve.scalar_tensor_tensor(nt[:, 1, :], mv[:, :, 1], LN_EPS, nt[:, 0, :], ALU.add, ALU.mult).then_inc(newton, 1)
                dve.wait_ge(newton, i * 3 - 1)
                dve.tensor_scalar(nt[:, 0, :], nt[:, 1, :], -0.5, 1.5, ALU.mult, ALU.add).then_inc(newton, 1)
                dve.wait_ge(newton, i * 3)
                dve.tensor_tensor(rstd[:], rstd[:], nt[:, 0, :], ALU.mult).then_inc(rstd_made, 1)
                dve.wait_ge(xn_stored, i * 16 - 16)
                dve.wait_ge(rstd_made, i)
                for j in range(2):
                    dve.tensor_scalar(xn[:, j, :], x1[:, j, :], mv[:, j, 0:1], rstd[:, j:j + 1], ALU.subtract, ALU.mult).then_inc(xn_made, 1)

            SPLIT_AT = 10

            def routing(i, kind, part):
                done = [0] if part == 0 else [SPLIT_AT]

                def then(ins):
                    done[0] += 1
                    ins.then_inc(route, 1)
                    dve.wait_ge(route, (i - 1) * ROUTE + done[0])

                def over(t, shape):
                    return t.broadcast_to(shape)

                if part == 0:
                    L = gen[0:R, 0:2 * E].rearrange("p (j e) -> p j e", j=2)
                    dve.wait_ge(gen_full, number(ORDER, i, kind, ("RT", 0, 0)) + 1)
                    then(dve.tensor_reduce(lmx[:], L, AX.X, ALU.max))
                    dve.tensor_tensor(lg[:], L, over(lmx[:, :, None], L2), ALU.subtract).then_inc(gen_free, 1)
                    dve.wait_ge(le_made, i)
                    then(dve.tensor_reduce(lsum[:], lg[:], AX.X, ALU.add))
                    then(dve.reciprocal(lrec[:], lsum[:]))
                    then(dve.tensor_tensor(sc[:], lg[:], over(lrec[:, :, None], L2), ALU.mult))
                    L4 = [R, 2, E, E]
                    other, own = over(sc[:, :, None, :], L4), over(sc[:, :, :, None], L4)
                    dve.tensor_tensor(ge[:], other, own, ALU.is_equal).then_inc(route, 1)
                    done[0] += 1
                    then(dve.tensor_tensor(gt[:], other, own, ALU.is_gt))
                    then(dve.tensor_tensor(ge[:], ge[:], over(lower[:, None], L4), ALU.mult))
                    then(dve.tensor_tensor(gt[:], gt[:], ge[:], ALU.add))
                    then(dve.tensor_reduce(rank[:], gt[:], AX.X, ALU.add))
                    then(dve.tensor_scalar(sel[:], rank[:], 2.0, None, ALU.is_lt))
                    dve.tensor_copy(selb[:], sel[:]).then_inc(sel_made, 1)
                    assert done[0] == SPLIT_AT
                else:
                    dve.wait_ge(gen_full, number(ORDER, i, kind, ("PRE", 0, 0)) + 1)
                    pre = gen[0:R, 0:3 * E].rearrange("p (j e) -> p j e", j=3)
                    then(dve.tensor_tensor(off[:], pre[:, 0:2], base[:], ALU.add))
                    dve.tensor_tensor(base[:], base[:], over(pre[:, 2:3], L2), ALU.add).then_inc(gen_free, 1)
                    then(dve.tensor_scalar(inv[:], off[:], float(CAP), float(2 * E * CAP), ALU.is_ge, ALU.mult))
                    then(dve.tensor_tensor(off[:], off[:], over(e896[:, None], L2), ALU.add))
                    then(dve.tensor_tensor(off[:], off[:], inv[:], ALU.add))
                    K4 = [R, 2, 2, E]
                    then(dve.tensor_tensor(oh[:], over(rank[:, :, None, :], K4), over(kk[:, None], K4), ALU.is_equal))
                    then(dve.tensor_tensor(ohs[:], oh[:], over(off[:, :, None, :], K4), ALU.mult))
                    then(dve.tensor_reduce(slotf[:].rearrange("p (j k) -> p j k", j=2), ohs[:], AX.X, ALU.add))
                    then(dve.tensor_tensor(ohs[:], oh[:], over(sc[:, :, None, :], K4), ALU.mult))
                    then(dve.tensor_tensor(tok[:], tok[:], tstep[:], ALU.add))
                    dve.wait_ge(sent, i * 64 - 64)
                    then(dve.tensor_reduce(pay[:, :, 1].rearrange("p (j k) -> p j k", j=2), ohs[:], AX.X, ALU.add))
                    then(dve.tensor_copy(pay[:, :, 0].bitcast(I32), tok[:]))
                    assert done[0] == ROUTE
                    dve.tensor_copy(slotu[:], slotf[:]).then_inc(slots_made, 1)

            def tail(i, kind, s):
                if s == 2:
                    lo_of_outputs(i - 1, NM - 1)
                elif s in (3, 4):
                    residual(i, kind, s - 3)
                elif s == 5:
                    layernorm(i)
                elif s == 8:
                    routing(i, kind, 0)
                elif s == 10:
                    routing(i, kind, 1)

            for g in range(2):
                lo_of_queries(0, g)
            for unit in START:
                lo_of_unit(0, "start", unit)
            mask_of(0)
            dve.wait_ge(mb_made, 1)
            dve.wait_ge(s_full, 1)
            masked(0, 0)
            dve.wait_ge(s_full, 2)
            inverse_sum(0, 0)
            masked(0, 1)

            def body(i, kind):
                for s in range(NH):
                    if has_step(kind, s + 2):
                        if s + 2 == NH:
                            mask_of(i + 1)
                            dve.wait_ge(mb_made, i + 2)
                        dve.wait_ge(s_full, i * NH + s + 3)
                    if has_step(kind, s + 1):
                        inverse_sum(*step(i, s + 1))
                    if has_step(kind, s + 2):
                        masked(*step(i, s + 2))
                    for unit in projections(kind, s, 0):
                        lo_of_unit(i, kind, unit)
                    if s > 0:
                        lo_of_probs(i, s - 1)
                    elif kind != "first":
                        lo_of_probs(i - 1, NH - 1)
                    for unit in projections(kind, s, 1) + projections(kind, s, 2):
                        lo_of_unit(i, kind, unit)
                    if s in (6, 10, 14):
                        lo_of_outputs(i, s // 4 - 1)
                    if kind != "first":
                        tail(i, kind, s)
                    if s in (8, 15) and kind != "last":
                        lo_of_queries(i + 1, s // 9)

            iterations(dve, body)
            lo_of_probs(B - 1, NH - 1)
            for s in range(NH):
                tail(B, "end", s)

        @block.scalar
        def _(act):
            act.wait_ge(zeroed, 2)
            act.wait_ge(const_set, 12)

            def hi_of_context(i):
                act.wait_ge(c_loaded, i * 16 + 16)
                for k in range(CC):
                    act.copy(cT[0][:, k, :], craw[:, k, :]).then_inc(c_hi, 1)

            def hi_of_queries(i, g):
                act.wait_ge(q_loaded, i * 16 + 16)
                for e in range(2):
                    act.copy(qz[0][64 * e:64 * e + 64, 4 * g + e:4 * g + 4:2, :],
                             q2[64 * e:64 * e + 64, 2 * g:2 * g + 2]).then_inc(qz_hi, 1)

            def hi_of_unit(i, kind, unit):
                act.wait_ge(gen_full, number(ORDER, i, kind, unit) + 1)
                dst, src = unit_places(unit)
                act.copy(dst(0), src).then_inc(gen_hi, 1)

            def hi_of_probs(i, h):
                act.wait_ge(pt_full, i * NH + h + 1)
                act.copy(probs_view(0, h), pt_view).then_inc(p_hi, 1)

            def hi_of_outputs(i, m):
                act.wait_ge(pv_full, i * NM + m + 1)
                for e in range(2):
                    act.copy(oT[0][64 * e:64 * e + 64, m, :], ob[64 * e:64 * e + 64, e * T:e * T + T]).then_inc(o_hi, 1)

            def exponential(i, h):
                act.wait_ge(nmx_made, i * NH + h + 1)
                act.activation(s_sb[:, h % 4, :], s_sb[:, h % 4, :], ACT.Exp, bias=nmx[:, h:h + 1],
                               accum_out=den[:, h:h + 1]).then_inc(e_made, 1)

            def tail(i, kind, s):
                if s == 2:
                    hi_of_outputs(i - 1, NM - 1)
                elif s == 4:
                    act.wait_ge(mv_made, i * 2)
                    act.activation(rstd[:], mv[:, :, 1], ACT.Abs_reciprocal_sqrt, bias=eps[:]).then_inc(root_made, 1)
                elif s in (6, 7):
                    act.wait_ge(gen_full, number(ORDER, i, kind, ("XT", s - 6, 0)) + 1)
                    act.copy(xnT[:, s - 6, :], gen[:, 0:KC * R]).then_inc(gen_free, 1)
                elif s == 8:
                    act.wait_ge(gen_free, number(ORDER, i, kind, ("RT", 0, 0)) + 1)
                    act.activation(lg[:], lg[:], ACT.Exp).then_inc(le_made, 1)

            hi_of_context(0)
            for g in range(2):
                hi_of_queries(0, g)
            for unit in START:
                hi_of_unit(0, "start", unit)
            exponential(0, 0)
            exponential(0, 1)

            def body(i, kind):
                for s in range(NH):
                    for unit in projections(kind, s, 0):
                        hi_of_unit(i, kind, unit)
                    if s > 0:
                        hi_of_probs(i, s - 1)
                    elif kind != "first":
                        hi_of_probs(i - 1, NH - 1)
                    if has_step(kind, s + 2):
                        exponential(*step(i, s + 2))
                    for unit in projections(kind, s, 1) + projections(kind, s, 2):
                        hi_of_unit(i, kind, unit)
                    if s == 3 and kind != "last":
                        act.wait_ge(gen_full, number(ORDER, i, kind, V(1, 2)) + 1)
                        hi_of_context(i + 1)
                    if s in (6, 10, 14):
                        hi_of_outputs(i, s // 4 - 1)
                    if kind != "first":
                        tail(i, kind, s)
                    if s in (8, 15) and kind != "last":
                        act.wait_ge(s_full, i * NH + s + 1)
                        hi_of_queries(i + 1, s // 9)

            iterations(act, body)
            hi_of_probs(B - 1, NH - 1)
            for s in range(NH):
                tail(B, "end", s)

        @block.tensor
        def _(pe):
            def product(out, lhs, rhs, n):
                steps = [(a, b, k) for a, b in ((0, 0), (0, 1), (1, 0)) for k in range(n)]
                for q, (a, b, k) in enumerate(steps):
                    mm = pe.matmul(out, lhs(a, k), rhs(b, k), start=q == 0, stop=q == len(steps) - 1)
                return mm

            def scores(i, h):
                head, t0 = h // 2, (h % 2) * R
                if not (isinstance(i, int) and i * NH + h < 2):
                    pe.wait_ge(s_masked, i * NH + (h - 1))
                if h % 8 == 0:
                    pe.wait_ge(qz_lo, i * 4 + (4 if h else 2))
                for a in range(2):
                    mm = product(scb[h % 2][0:R, a, 0:HW], lambda x, k: qz[x][:, head, t0:t0 + R],
                                 lambda y, k: kT[y][:, head // 2, a * (J - HW):a * (J - HW) + HW], 1)
                mm.then_inc(s_full, 1)

            def transposes(i, h):
                pe.wait_ge(p_made, i * NH + h + 1)
                pe.wait_ge(p_lo, i * NH + h)
                for j in range(NJ):
                    mm = pe.transpose(ptb[0:JB, j // 3, R * (j % 3):R * (j % 3) + R], s_sb[:, h % 4, JB * j:JB * j + JB], ident[:])
                mm.then_inc(pt_full, 1)

            def values(i, head):
                m, e = head // 2, head % 2
                pe.wait_ge(p_lo, i * NH + 2 * head + 2)
                if e == 0:
                    pe.wait_ge(o_lo, i * H2 + 2 * m)
                mm = product(ob[:, e * T:e * T + T], lambda x, k: v[x][:, k, 128 * m:128 * m + 128],
                             lambda y, k: pT[y][:, e, k, :], NJ)
                if e:
                    mm.then_inc(pv_full, 1)

            def unit_of(i, kind, unit):
                what, m, a = unit
                pe.wait_ge(gen_free, number(ORDER, i, kind, unit))
                if unit == K(0, 0):
                    pe.wait_ge(c_lo, CC if kind == "start" else i * CC + 2 * CC)
                if what == "K":
                    mm = product(gen[:, 0:KW[a]], lambda x, k: wk[x][:, k, 128 * m:128 * m + 128],
                                 lambda y, k: cT[y][:, k, K0[a]:K0[a] + KW[a]], CC)
                elif what == "V":
                    for b in range(2):
                        j = 2 * a + b
                        mm = product(gen[0:JB, 256 * b:256 * b + 256], lambda x, k: cT[x][:, k, JB * j:JB * j + JB],
                                     lambda y, k: wv[y][:, k, 256 * m:256 * m + 256], CC)
                elif what == "OUT":
                    if m == 0:
                        pe.wait_ge(o_lo, i * H2)
                    mm = product(gen[0:R, :], lambda x, k: oT[x][:, k, R * m:R * m + R], lambda y, k: wo[y][:, k, :], KC)
                elif what == "XT":
                    if m == 0:
                        pe.wait_ge(xn_made, i * 2)
                    for k in range(KC):
                        mm = pe.transpose(gen[:, R * k:R * k + R], xn[:, m, 128 * k:128 * k + 128], ident[:])
                elif what == "RT":
                    for j in range(2):
                        for k in range(KC):
                            mm = pe.matmul(gen[0:R, E * j:E * j + E], xnT[:, j, R * k:R * k + R], wr[:, k, :], start=k == 0, stop=k == KC - 1)
                else:
                    pe.wait_ge(sel_made, i)
                    pre = gen[0:R]
                    pe.matmul(pre[:, 0:E], before[:], selb[:, 0, :], start=True, stop=True)
                    pe.matmul(pre[:, E:2 * E], before[:], selb[:, 1, :], start=True, stop=False)
                    pe.matmul(pre[:, E:2 * E], onesb[:], selb[:, 0, :], start=False, stop=True)
                    pe.matmul(pre[:, 2 * E:3 * E], onesb[:], selb[:, 0, :], start=True, stop=False)
                    mm = pe.matmul(pre[:, 2 * E:3 * E], onesb[:], selb[:, 1, :], start=False, stop=True)
                mm.then_inc(gen_full, 1)

            pe.wait_ge(w_lo, len(pieces))
            pe.wait_ge(const_ready, 3)
            pe.wait_ge(const_set, 12)
            pe.wait_ge(small_loaded, 48)
            for unit in START:
                unit_of(0, "start", unit)
            scores(0, 0)
            scores(0, 1)

            def body(i, kind):
                for s in range(NH):
                    if has_step(kind, s + 2):
                        scores(*step(i, s + 2))
                    for unit in units(kind, s, (0,)):
                        unit_of(i, kind, unit)
                    if s > 0:
                        transposes(i, s - 1)
                    elif kind != "first":
                        transposes(i - 1, NH - 1)
                    for unit in units(kind, s, (1,)):
                        unit_of(i, kind, unit)
                    if s >= 3 and s % 2:
                        values(i, (s - 3) // 2)
                    elif s == 1 and kind != "first":
                        values(i - 1, H2 - 1)
                    for unit in units(kind, s, (2,)):
                        unit_of(i, kind, unit)

            iterations(pe, body)
            transposes(B - 1, NH - 1)
            values(B - 1, H2 - 1)
            for unit in ORDER["end"]:
                unit_of(B, "end", unit)


def experts(nc, w1, w2, xn_dram, table_dram, out):
    FB = F // 128
    NT = CAP // 128
    HC = CAP // 2
    NW = E * FB
    PAIRS = E // 2
    NSLOT = 4
    w2_v = w2.rearrange("(g b p) c -> g p b c", b=2, p=128)
    tab_v = table_dram.rearrange("(e t p) w -> e p t w", e=E, p=128)
    with ExitStack() as ctx:
        sb = lambda n, s, d=F32: ctx.enter_context(nc.sbuf_tensor("f_" + n, s, d))
        sem = lambda n: ctx.enter_context(nc.semaphore("f_" + n))
        ident = sb("ident", [128, 128])
        raw1 = sb("raw1", [128, 2, 2, C])
        raw2 = sb("raw2", [128, 2, 2, C])
        w1s = [sb(f"w1{k}", [128, NSLOT, KC, 128], F32R) for k in "hl"]
        w2s = [sb(f"w2{k}", [128, NSLOT, C], F32R) for k in "hl"]
        meta = sb("meta", [128, 2, NT, 2])
        xg = sb("xg", [128, NT, C])
        xT = [[sb(f"xT{k}{p}", [128, KC, CAP], F32R) for k in "hl"] for p in range(2)]
        hf = sb("hf", [128, 2, HC])
        hs = [sb(f"h{k}", [128, 2, CAP], F32R) for k in "hl"]
        ys = sb("ys", [128, NT, C])
        Y = [ctx.enter_context(nc.psum_tensor(f"f_y{k}", [128, 512], F32)) for k in range(NT)]
        H = ctx.enter_context(nc.psum_tensor("f_h", [128, 512], F32))

        const_set, const_ready = sem("const_set"), sem("const_ready")
        loaded = [sem("loaded0"), sem("loaded1")]
        w_hi, w_lo = sem("w_hi"), sem("w_lo")
        meta_loaded, gathered, scattered = sem("meta_loaded"), sem("gathered"), sem("scattered")
        full, free = sem("full"), sem("free")
        x_hi = sem("x_hi")
        h_hi, h_lo = sem("h_hi"), sem("h_lo")
        y_done, yt_done, ys_made = sem("y_done"), sem("yt_done"), sem("ys_made")

        FIRST_T = 5
        order = []
        for j in range(FB):
            order.append(("h", 2 * j))
            if FIRST_T <= j < FIRST_T + NT:
                order.append(("t", j - FIRST_T))
            order.append(("h", 2 * j + 1))
        use = {key: n for n, key in enumerate(order)}
        USES = len(order)
        GATHER_J = 3
        BL = 2 * FB

        block = ctx.enter_context(nc.Block())

        @block.sync
        def _(sp):
            sp.dma_start(meta[:, 0], tab_v[0]).then_inc(meta_loaded, 16)

            def load(g, a, b):
                sp.dma_start(raw1[:, g % 2].rearrange("p b c -> p (b c)"), a).then_inc(loaded[g % 2], 16)
                sp.dma_start(raw2[:, g % 2], b).then_inc(loaded[g % 2], 16)

            for g in range(2):
                load(g, w1[g], w2_v[g])
            with sp.Fori(0, PAIRS) as it:
                for g in range(FB):
                    if g % (FB // 2) == 1:
                        p = g // (FB // 2)
                        nxt = sp.snap((it * 2 + p + 1) % E)
                        sp.wait_ge(const_ready, 1)
                        sp.wait_ge(scattered, (it * 2 + p) * (16 * NT))
                        sp.dma_start(meta[:, (p + 1) % 2], tab_v[bass.ds(nxt, 1)].rearrange("a p t w -> (a p) t w")).then_inc(meta_loaded, 16)
                    src = sp.snap((it * FB + g + 2) % (NW // 2))
                    sp.wait_ge(const_ready, 1)
                    sp.wait_ge(w_lo, it * (4 * FB) + 4 * g + 4)
                    load(g + 2, w1[bass.ds(src, 1)].rearrange("a p n -> (a p) n"), w2_v[bass.ds(src, 1)].rearrange("a p b c -> (a p) b c"))
            sp.wait_ge(scattered, E * 16 * NT)
            for g in range(2):
                sp.wait_ge(loaded[g], 32 * (NW // 4 + 1))
            sp.wait_ge(meta_loaded, 16 * (E + 1))
            sp.wait_ge(gathered, 16 * NT * (E + 1))

        @block.gpsimd
        def _(pool):
            pool.memset(ident[:], 1.0).then_inc(const_set, 1)
            pool.wait_ge(const_set, 1)
            pool.affine_select(out=ident[:], in_=ident[:], pattern=[[1, 128]], compare_op=ALU.is_equal, fill=0.0,
                               base=0, channel_multiplier=-1).then_inc(const_ready, 1)

            def gather(p):
                for t in range(NT):
                    pool.indirect_dma_start(out=xg[:, t, :], out_offset=None, in_=xn_dram,
                                            in_offset=bass.IndirectOffsetOnAxis(ap=meta[:, p, t, 0:1].bitcast(U32), axis=0)).then_inc(gathered, 16)

            def scatter(p):
                for t in range(NT):
                    pool.indirect_dma_start(out=out, out_offset=bass.IndirectOffsetOnAxis(ap=meta[:, p, t, 0:1].bitcast(U32), axis=0),
                                            in_=ys[:, t, :], in_offset=None, compute_op=ALU.add).then_inc(scattered, 16)

            def split(n, w, base):
                g = n // 2
                pool.wait_ge(w_hi, base + 2 * n + 1)
                pool.tensor_tensor(w1s[1][:, n % NSLOT].rearrange("p k c -> p (k c)"), raw1[:, g % 2, n % 2, :],
                                   w1s[0][:, n % NSLOT].rearrange("p k c -> p (k c)").bitcast(F32), ALU.subtract).then_inc(w_lo, 1)
                for s, val in w:
                    pool.wait_ge(s, val)
                pool.wait_ge(w_hi, base + 2 * n + 2)
                pool.tensor_tensor(w2s[1][:, n % NSLOT], raw2[:, g % 2, n % 2, :], w2s[0][:, n % NSLOT].bitcast(F32),
                                   ALU.subtract).then_inc(w_lo, 1)

            pool.wait_ge(meta_loaded, 16)
            gather(0)
            for n in range(2):
                split(n, (), 0)

            with pool.Fori(0, PAIRS) as it:
                for l in range(BL):
                    p, j = divmod(l, FB)
                    w = ()
                    if j == GATHER_J:
                        w = ((meta_loaded, it * 32 + 16 * p + 32), (free, it * (2 * USES) + p * USES + NT))
                    if j == FB - 1:
                        w = ((ys_made, it * (2 * NT) + NT * (p + 1)), (scattered, (it * 2 + p) * (16 * NT)))
                    split(l + 2, w, it * (2 * BL))
                    if j == GATHER_J:
                        gather((p + 1) % 2)
                    if j == FB - 1:
                        scatter(p)

        @block.vector
        def _(dve):
            def split(n, it):
                g = n // 2
                dve.wait_ge(loaded[g % 2], it * (16 * FB) + 32 * (g // 2) + 32)
                dve.tensor_copy(w1s[0][:, n % NSLOT].rearrange("p k c -> p (k c)"), raw1[:, g % 2, n % 2, :]).then_inc(w_hi, 1)
                dve.tensor_copy(w2s[0][:, n % NSLOT], raw2[:, g % 2, n % 2, :]).then_inc(w_hi, 1)

            def rows_lo(p, t, count):
                dve.wait_ge(x_hi, count)
                dve.tensor_tensor(xT[p][1][:, :, 128 * t:128 * t + 128], H[:].rearrange("p (k s) -> p k s", k=KC),
                                  xT[p][0][:, :, 128 * t:128 * t + 128].bitcast(F32), ALU.subtract).then_inc(free, 1)

            for n in range(2):
                split(n, 0)
            for t in range(NT):
                rows_lo(0, t, t + 1)
            with dve.Fori(0, PAIRS) as it:
                for l in range(BL):
                    p, j = divmod(l, FB)
                    for c in range(2):
                        dve.wait_ge(free, it * (2 * USES) + p * USES + NT + use["h", 2 * j + c] + 1)
                        dve.wait_ge(y_done, it * BL + max(l - 1, 0))
                        dve.tensor_copy(hs[0][:, l % 2, c * HC:c * HC + HC], hf[:, c, :]).then_inc(h_hi, 1)
                        dve.wait_ge(h_hi, it * (2 * BL) + 2 * l + c + 1)
                        dve.tensor_tensor(hs[1][:, l % 2, c * HC:c * HC + HC], hf[:, c, :],
                                          hs[0][:, l % 2, c * HC:c * HC + HC].bitcast(F32), ALU.subtract).then_inc(h_lo, 1)
                        t = j - FIRST_T
                        if c == 0 and 0 <= t < NT:
                            rows_lo((p + 1) % 2, t, it * (2 * NT) + p * NT + NT + t + 1)
                    split(l + 2, it)

        @block.scalar
        def _(act):
            def rows_hi(p, t, count):
                act.wait_ge(full, count)
                act.copy(xT[p][0][:, :, 128 * t:128 * t + 128], H[:].rearrange("p (k s) -> p k s", k=KC)).then_inc(x_hi, 1)

            for t in range(NT):
                rows_hi(0, t, t + 1)
            with act.Fori(0, PAIRS) as it:
                for l in range(BL):
                    p, j = divmod(l, FB)
                    for c in range(2):
                        base = it * (2 * USES) + p * USES + NT
                        act.wait_ge(full, base + use["h", 2 * j + c] + 1)
                        act.wait_ge(h_lo, it * (2 * BL) + max(2 * l + c - 1, 0))
                        act.activation(hf[:, c, :], H[:, 0:HC], ACT.Gelu_apprx_tanh).then_inc(free, 1)
                        t = j - FIRST_T
                        if c == 0 and 0 <= t < NT:
                            rows_hi((p + 1) % 2, t, base + use["t", t] + 1)
                    if j == FB - 1:
                        act.wait_ge(scattered, (it * 2 + p) * (16 * NT))
                        for t in range(NT):
                            act.wait_ge(yt_done, it * (2 * NT) + p * NT + t + 1)
                            act.activation(ys[:, t, :], Y[t][:], ACT.Copy, scale=meta[:, p, t, 1:2]).then_inc(ys_made, 1)

        @block.tensor
        def _(pe):
            THREE = ((0, 0), (0, 1), (1, 0))

            def rows(t):
                for k in range(KC):
                    mm = pe.transpose(H[:, 128 * k:128 * k + 128], xg[:, t, 128 * k:128 * k + 128], ident[:])
                mm.then_inc(full, 1)

            pe.wait_ge(const_ready, 1)
            pe.wait_ge(gathered, 16 * NT)
            for t in range(NT):
                if t:
                    pe.wait_ge(free, t)
                rows(t)
            with pe.Fori(0, PAIRS) as it:
                for l in range(BL):
                    p, j = divmod(l, FB)
                    base = it * (2 * USES) + p * USES + NT

                    def hidden(c):
                        pe.wait_ge(free, base + use["h", 2 * j + c])
                        if c == 0:
                            pe.wait_ge(w_lo, it * (2 * BL) + 2 * l + 1)
                        for q, (a, b) in enumerate(THREE):
                            for k in range(KC):
                                mm = pe.matmul(H[:, 0:HC], w1s[a][:, l % NSLOT, k, :], xT[p][b][:, k, c * HC:c * HC + HC],
                                               start=q + k == 0, stop=(q, k) == (2, KC - 1))
                        mm.then_inc(full, 1)

                    def outputs(l, tiles):
                        p, j = divmod(l, FB)
                        for t in tiles:
                            if t == 0:
                                pe.wait_ge(w_lo, it * (2 * BL) + 2 * l + 2)
                                pe.wait_ge(h_lo, it * (2 * BL) + 2 * l + (2 if j < FB - 1 else 1))
                                if j == 0:
                                    pe.wait_ge(ys_made, it * (2 * NT) + p * NT)
                            if j == FB - 1 and t == 3:
                                pe.wait_ge(h_lo, it * (2 * BL) + 2 * l + 2)
                            for q, (a, b) in enumerate(THREE):
                                mm = pe.matmul(Y[t][:], hs[a][:, l % 2, 128 * t:128 * t + 128], w2s[b][:, l % NSLOT, :],
                                               start=j == 0 and q == 0, stop=j == FB - 1 and q == 2)
                            if j == FB - 1:
                                mm.then_inc(yt_done, 1)
                        if NT - 1 in tiles:
                            if j == FB - 1:
                                pe.wait_ge(yt_done, it * (2 * NT) + p * NT + NT)
                                pe.sem_inc(y_done, 1)
                            else:
                                mm.then_inc(y_done, 1)

                    hidden(0)
                    if j > 0:
                        outputs(l - 1, (0, 1))
                    t = j - FIRST_T
                    if 0 <= t < NT:
                        if t == 0:
                            pe.wait_ge(gathered, it * (2 * 16 * NT) + (p + 2) * (16 * NT))
                        pe.wait_ge(free, base + use["t", t])
                        rows(t)
                    if j > 0:
                        outputs(l - 1, (2, 3))
                    hidden(1)
                    if j > 0:
                        outputs(l - 1, (4, 5, 6))
                    if j == FB - 1:
                        outputs(l, range(NT))


def decoder_block(nc, x, w_qkvT, w_outT, slopes, w_qT, w_k, w_v, w_o, b_o, ctxT, mask, w_r, w1, w2, bias, out):
    scratch = lambda name, shape: nc.dram_tensor(name, shape, F32, kind="Internal").ap()
    x1_dram = scratch("x1_dram", [B * T, C])
    q2_dram = scratch("q2_dram", [B, 128, KC, T])
    xn_dram = scratch("xn_dram", [B * T + CAP, C])
    table_dram = scratch("table_dram", [E * CAP, 2])
    self_attention(nc, x, w_qkvT, w_outT, w_qT, slopes, x1_dram, q2_dram)
    cross_attention(nc, ctxT, mask, q2_dram, x1_dram, w_k, w_v, w_o, b_o, w_r, bias, out, xn_dram, table_dram)
    experts(nc, w1, w2, xn_dram, table_dram, out)


def kernel(**inputs):
    import numpy as _np
    import concourse.bacc as _bacc
    from concourse import mybir as _mybir
    from concourse.bass_utils import run_bass_kernel_spmd as _run

    def rows_on_partitions(w):
        return w.reshape(-1, 128, w.shape[1]).transpose(1, 0, 2)

    g = {name: _np.asarray(a) for name, a in inputs.items()}
    laid = {
        "x": g["x"].reshape(B * T, C),
        "w_qkvT": rows_on_partitions(g["L0_attn_w_qkv"].T),
        "w_outT": rows_on_partitions(g["L0_attn_w_out"].T),
        "slopes": g["L0_attn_alibi_slopes"],
        "w_qT": rows_on_partitions(g["L0_xattn_W_q"]),
        "w_k": rows_on_partitions(g["L0_xattn_W_k"]),
        "w_v": rows_on_partitions(g["L0_xattn_W_v"]),
        "w_o": rows_on_partitions(g["L0_xattn_W_o"]),
        "b_o": g["L0_xattn_b_o"],
        "ctxT": g["ctx_768"].transpose(0, 2, 1).reshape(B, CC, 128, J).transpose(0, 2, 1, 3),
        "mask": g["mask_BxS2_bk0"].reshape(-1).view(_np.int32),
        "w_r": rows_on_partitions(g["L0_ffn_w_router"]),
        "w1": g["L0_ffn_w1"].reshape(E, KC, 128, F // 256, 2, 128).transpose(0, 3, 2, 4, 1, 5).reshape(E * F // 256, 128, 2 * C),
        "w2": g["L0_ffn_w2"].reshape(E * F, C),
        "bias": g["L0_ffn_bias"].reshape(C),
    }
    nc = _bacc.Bacc("TRN2", target_bir_lowering=False, num_devices=1)
    arrays, args = {}, []
    for name, a in laid.items():
        a = _np.ascontiguousarray(a)
        arrays[f"in_{name}"] = a
        args.append(nc.dram_tensor(f"in_{name}", a.shape, _mybir.dt.from_np(a.dtype), kind="ExternalInput").ap())
    args.append(nc.dram_tensor("out_x", (B * T + CAP, C), F32, kind="ExternalOutput").ap())
    decoder_block(nc, *args)
    r = _run(nc, [arrays], core_ids=[0])
    return r.results[0]["out_x"][:B * T].reshape(B, T, C)
```
